# Optimizing a Trainium2 kernel written in Bass

```python
import numpy as np
import jax
import jax.numpy as jnp

def _softmax(x, axis=-1):
    return jax.nn.softmax(x, axis=axis)

def _gelu(x):
    return jax.nn.gelu(x, approximate=True)

def _silu(x):
    return jax.nn.silu(x)

def _sigmoid(x):
    return jax.nn.sigmoid(x)

def _layernorm(x, axis=-1, eps=1e-05):
    m = jnp.mean(x, axis=axis, keepdims=True)
    v = jnp.var(x, axis=axis, keepdims=True)
    return (x - m) / jnp.sqrt(v + eps)

def _scatter_add(tgt, idx, src, axis=0):
    return tgt.at[idx].add(src)

def _segment_sum(src, seg, n):
    return jax.ops.segment_sum(src, seg, n)
kernel_name = 'mk_gps_d1_gnn_r8_19e832'

def setup_inputs(seed: int=0):
    np.random.seed(seed)
    _w = jnp.asarray

    def _rec_inputs():
        import jax
        import jax.numpy as jnp
        _gk = jax.random.key(seed)
        x = -0.0003713 + 1 * jax.random.normal(jax.random.fold_in(_gk, 1), (6250, 256), jnp.float32)
        src = jax.random.randint(jax.random.fold_in(_gk, 2), (100000,), 0, 6250, jnp.int32)
        dst = jnp.minimum((6250 * jax.random.uniform(jax.random.fold_in(_gk, 3), (100000,)) ** 2.0).astype(jnp.int32), 49999)
        _o = jnp.argsort(dst, stable=True)
        src = src[_o]
        dst = dst[_o]
        edge_attr_3 = -1.09012e-05 + 0.99985 * jax.random.normal(jax.random.fold_in(_gk, 11), (100000, 3), jnp.float32)
        return (x, src, dst, edge_attr_3)
    x, src, dst, edge_attr_3 = _rec_inputs()

    def _L0_gnn_setup():
        import jax, jax.numpy as jnp
        import numpy as np
        N = 6250
        E = 50000
        IN = 256
        H = 8
        D = 32
        EF = 3
        key = jax.random.key(seed)
        ks = jax.random.split(key, 8)
        x = jax.random.normal(ks[0], (N, IN), dtype=jnp.float32)
        edge_index = jax.random.randint(ks[1], (2, E), 0, N, dtype=jnp.int64)
        edge_attr = jax.random.normal(ks[2], (E, EF), dtype=jnp.float32)
        W = jax.random.normal(ks[3], (H * D, IN), dtype=jnp.float32) * np.float32(np.sqrt(2.0 / (IN + H * D)))
        a_src = jax.random.normal(ks[4], (H, D), dtype=jnp.float32) * np.float32(np.sqrt(2.0 / (H + D)))
        a_dst = jax.random.normal(ks[5], (H, D), dtype=jnp.float32) * np.float32(np.sqrt(2.0 / (H + D)))
        edge_W = jax.random.normal(ks[6], (H * D, EF), dtype=jnp.float32) * np.float32(np.sqrt(2.0 / (EF + H * D)))
        edge_b = jnp.zeros((H * D,), dtype=jnp.float32)
        bias = jnp.zeros((H * D,), dtype=jnp.float32)
        return {'x': x, 'W': W, 'a_src': a_src, 'a_dst': a_dst, 'edge_W': edge_W, 'edge_b': edge_b, 'bias': bias, 'edge_attr': edge_attr, 'edge_index': edge_index}
    _L0_gnn_all = _L0_gnn_setup()
    _L0_gnn_in = {k: v for k, v in _L0_gnn_all.items() if k in ('W', 'a_src', 'a_dst', 'edge_W', 'edge_b', 'bias')}
    del _L0_gnn_all

    def _L0_mix_setup():
        import jax, jax.numpy as jnp
        import numpy as np
        DIM = 256
        HEADS = 4
        DIM_HEAD = 32
        NUM_MEM = 4
        HIDDEN = HEADS * DIM_HEAD
        SCALE = DIM_HEAD ** (-0.5)

        def rmsnorm(x, g):
            n = jnp.linalg.norm(x, axis=-1, keepdims=True)
            return x / jnp.maximum(n, 1e-12) * g * x.shape[-1] ** 0.5
        key = jax.random.key(seed)
        ks = jax.random.split(key, 8)
        B, N = (4, 2048)
        return {'x': jax.random.normal(ks[0], (B, N, DIM), jnp.float32), 't': jax.random.normal(ks[1], (B,), jnp.float32), 'w_qkv': jax.random.normal(ks[2], (DIM, 3 * HIDDEN), jnp.float32) * 0.02, 'mem_kv': jax.random.normal(ks[3], (2, HEADS, DIM_HEAD, NUM_MEM), jnp.float32), 'w_out': jax.random.normal(ks[4], (HIDDEN, DIM), jnp.float32) * 0.02, 'b_out': jnp.zeros((DIM,), jnp.float32), 'g_out': jnp.ones((DIM,), jnp.float32), 'g_pre': jnp.ones((DIM,), jnp.float32)}
    _L0_mix_all = _L0_mix_setup()
    _L0_mix_in = {k: v for k, v in _L0_mix_all.items() if k in ('t', 'w_qkv', 'mem_kv', 'w_out', 'b_out', 'g_out', 'g_pre')}
    del _L0_mix_all

    def _L0_ffn_setup():
        import jax, jax.numpy as jnp
        import numpy as np
        B, S, D, H, E, K = (8, 1024, 256, 1024, 8, 2)
        key = jax.random.key(seed)
        ks = jax.random.split(key, 7)
        s_in = 1.0 / np.sqrt(D)
        s_hid = 1.0 / np.sqrt(H)
        return {'x': jax.random.normal(ks[0], (B, S, D), dtype=jnp.float32), 'Wg': jax.random.uniform(ks[1], (E, D), jnp.float32, -s_in, s_in), 'bg': jax.random.uniform(ks[2], (E,), jnp.float32, -s_in, s_in), 'W1': jax.random.uniform(ks[3], (E, H, D), jnp.float32, -s_in, s_in), 'b1': jax.random.uniform(ks[4], (E, H), jnp.float32, -s_in, s_in), 'W2': jax.random.uniform(ks[5], (E, D, H), jnp.float32, -s_hid, s_hid), 'b2': jax.random.uniform(ks[6], (E, D), jnp.float32, -s_hid, s_hid)}
    _L0_ffn_all = _L0_ffn_setup()
    _L0_ffn_in = {k: v for k, v in _L0_ffn_all.items() if k in ('Wg', 'bg', 'W1', 'b1', 'W2', 'b2')}
    del _L0_ffn_all
    return {'x': x, 'src': src, 'dst': dst, 'edge_attr_3': edge_attr_3, 'L0_gnn_W': _L0_gnn_in['W'], 'L0_gnn_a_src': _L0_gnn_in['a_src'], 'L0_gnn_a_dst': _L0_gnn_in['a_dst'], 'L0_gnn_edge_W': _L0_gnn_in['edge_W'], 'L0_gnn_edge_b': _L0_gnn_in['edge_b'], 'L0_gnn_bias': _L0_gnn_in['bias'], 'L0_mix_t': _L0_mix_in['t'], 'L0_mix_w_qkv': _L0_mix_in['w_qkv'], 'L0_mix_mem_kv': _L0_mix_in['mem_kv'], 'L0_mix_w_out': _L0_mix_in['w_out'], 'L0_mix_b_out': _L0_mix_in['b_out'], 'L0_mix_g_out': _L0_mix_in['g_out'], 'L0_mix_g_pre': _L0_mix_in['g_pre'], 'L0_ffn_Wg': _L0_ffn_in['Wg'], 'L0_ffn_bg': _L0_ffn_in['bg'], 'L0_ffn_W1': _L0_ffn_in['W1'], 'L0_ffn_b1': _L0_ffn_in['b1'], 'L0_ffn_W2': _L0_ffn_in['W2'], 'L0_ffn_b2': _L0_ffn_in['b2']}

def reference(x, src, dst, edge_attr_3, L0_gnn_W, L0_gnn_a_src, L0_gnn_a_dst, L0_gnn_edge_W, L0_gnn_edge_b, L0_gnn_bias, L0_mix_t, L0_mix_w_qkv, L0_mix_mem_kv, L0_mix_w_out, L0_mix_b_out, L0_mix_g_out, L0_mix_g_pre, L0_ffn_Wg, L0_ffn_bg, L0_ffn_W1, L0_ffn_b1, L0_ffn_W2, L0_ffn_b2):
    import jax
    import jax.numpy as jnp

    def _L0_gnn_ref(x, W, a_src, a_dst, edge_W, edge_b, bias, edge_attr, edge_index):
        import jax, jax.numpy as jnp
        import numpy as np
        N = 6250
        E = 50000
        IN = 256
        H = 8
        D = 32
        EF = 3
        n = x.shape[0]
        h = (x @ W.T).reshape(n, H, D)
        src, dst = (edge_index[0], edge_index[1])
        h_src = h[src]
        h_dst = h[dst]
        alpha = jnp.einsum('ehd,hd->eh', h_src, a_src) + jnp.einsum('ehd,hd->eh', h_dst, a_dst)
        enc = jax.nn.relu(edge_attr @ edge_W.T + edge_b).reshape(-1, H, D)
        alpha = alpha + jnp.sum(enc * h_dst, axis=-1)
        alpha = jnp.where(alpha >= 0, alpha, 0.2 * alpha)
        amax = jax.ops.segment_max(alpha, dst, num_segments=n)
        ex = jnp.exp(alpha - amax[dst])
        denom = jax.ops.segment_sum(ex, dst, num_segments=n)
        attn = ex / jnp.maximum(denom[dst], 1e-10)
        out = jax.ops.segment_sum(h_src * attn[..., None], dst, num_segments=n)
        return out.reshape(n, H * D) + bias

    def _L0_mix_ref(x, t, w_qkv, mem_kv, w_out, b_out, g_out, g_pre):
        import jax, jax.numpy as jnp
        import numpy as np
        DIM = 256
        HEADS = 4
        DIM_HEAD = 32
        NUM_MEM = 4
        HIDDEN = HEADS * DIM_HEAD
        SCALE = DIM_HEAD ** (-0.5)

        def rmsnorm(x, g):
            n = jnp.linalg.norm(x, axis=-1, keepdims=True)
            return x / jnp.maximum(n, 1e-12) * g * x.shape[-1] ** 0.5
        b, n, c = x.shape
        xn = rmsnorm(x, g_pre)
        qkv = xn @ w_qkv
        q, k, v = jnp.split(qkv, 3, axis=-1)

        def to_heads(z):
            return z.reshape(b, n, HEADS, DIM_HEAD).transpose(0, 2, 3, 1)
        q, k, v = map(to_heads, (q, k, v))
        mk = jnp.broadcast_to(mem_kv[0], (b, HEADS, DIM_HEAD, NUM_MEM))
        mv = jnp.broadcast_to(mem_kv[1], (b, HEADS, DIM_HEAD, NUM_MEM))
        k = jnp.concatenate([mk, k], axis=-1)
        v = jnp.concatenate([mv, v], axis=-1)
        q = jax.nn.softmax(q, axis=-2) * SCALE
        k = jax.nn.softmax(k, axis=-1)
        context = jnp.einsum('bhdn,bhen->bhde', k, v)
        out = jnp.einsum('bhde,bhdn->bhen', context, q)
        out = out.transpose(0, 3, 1, 2).reshape(b, n, HIDDEN)
        out = rmsnorm(out @ w_out + b_out, g_out)
        return out + x

    def _L0_ffn_ref(x, Wg, bg, W1, b1, W2, b2):
        import jax, jax.numpy as jnp
        import numpy as np
        B, S, D, H, E, K = (8, 1024, 256, 1024, 8, 2)
        gate_scores = jnp.einsum('bsd,ed->bse', x, Wg) + bg
        topk_scores, topk_idx = jax.lax.top_k(gate_scores, K)
        topk_probs = jax.nn.softmax(topk_scores, axis=-1)
        combine = jnp.sum(topk_probs[..., None] * jax.nn.one_hot(topk_idx, E, dtype=x.dtype), axis=-2)
        out = jnp.zeros_like(x)
        for e in range(E):
            h = jax.nn.relu(jnp.einsum('bsd,hd->bsh', x, W1[e]) + b1[e])
            y = jnp.einsum('bsh,dh->bsd', h, W2[e]) + b2[e]
            out = out + combine[..., e:e + 1] * y
        return out
    edge_index = jnp.stack([src, dst])
    xn = _layernorm(x, axis=-1)
    x = x + _L0_gnn_ref(xn, L0_gnn_W, L0_gnn_a_src, L0_gnn_a_dst, L0_gnn_edge_W, L0_gnn_edge_b, L0_gnn_bias, edge_attr_3, edge_index) + _L0_mix_ref(xn[None], L0_mix_t, L0_mix_w_qkv, L0_mix_mem_kv, L0_mix_w_out, L0_mix_b_out, L0_mix_g_out, L0_mix_g_pre)[0]
    x = x + _L0_ffn_ref(_layernorm(x, axis=-1)[None], L0_ffn_Wg, L0_ffn_bg, L0_ffn_W1, L0_ffn_b1, L0_ffn_W2, L0_ffn_b2)[0]
    return x

_drawn_inputs = setup_inputs


def setup_inputs(seed=0):
    import zlib

    import numpy as np

    out = dict(_drawn_inputs(seed))
    spreads = {'L0_gnn_edge_b': (0.0, 0.1),
     'L0_gnn_bias': (0.0, 0.1),
     'L0_mix_b_out': (0.0, 0.1),
     'L0_mix_g_out': (1.0, 0.2),
     'L0_mix_g_pre': (1.0, 0.6)}
    factors = {'L0_mix_w_qkv': 8.0,
     'L0_mix_mem_kv': 8.0,
     'L0_mix_w_out': 8.0,
     'L0_ffn_bg': 3.627,
     'L0_ffn_b1': 8.0,
     'L0_ffn_b2': 8.0}
    for name, (base, spread) in spreads.items():
        noise = np.random.default_rng([zlib.crc32(name.encode()), seed]).standard_normal(out[name].shape)
        drawn = base * np.exp(spread * noise) if base else spread * noise
        out[name] = jnp.asarray(drawn.astype(out[name].dtype))
    for name, factor in factors.items():
        out[name] = (out[name] * factor).astype(out[name].dtype)
    return out
```

```python
from contextlib import ExitStack

import concourse.bass as bass
from concourse import mybir

F32 = mybir.dt.float32
BF16 = mybir.dt.bfloat16
I32 = mybir.dt.int32
U32 = mybir.dt.uint32
ALU = mybir.AluOpType
ACT = mybir.ActivationFunctionType
AX = mybir.AxisListType

P = 128
N, C = 6250, 256
E = 100000
H, D = 8, 32
HW = D + 1
ROW = H * HW
NT = -(-N // P)
NPAD = NT * P
NLAST = N - (NT - 1) * P
ETILES = -(-E // P)
ER = 7
EP = 112
EROWS = EP * ER
EFULL = E // (ER * P)
EREST = E - EFULL * ER * P
CH = 16
CT = -(-(ETILES + NT - 1) // CH)
V = CH * CT
VC = -(-V // P)
VPAD = VC * P
NOWHERE = 7000
BIG = 1e30
EPS = 1e-5
MH, MD, MEM = 4, 32, 4
MHID = MH * MD
QW = 3 * MHID
NE = 8
HID = 1024
BROWS = NE * (HID + C) // P
NB = (2 * NPAD + NE * (P - 1)) // P + 1
NW = C + 2 * H
BS = 8
NBLK = V // BS
G = 7
assert NT % G == 0 and V % BS == 0 and ETILES + NT - 1 <= V and ETILES < EROWS


class Ctx:
    pass


def allocators(nc, ctx):
    def sb(name, shape, dt=F32):
        return ctx.enter_context(nc.sbuf_tensor(name, shape, dt))

    def ps(name, shape, dt=F32):
        return ctx.enter_context(nc.psum_tensor(name, shape, dt))

    used = []

    def sem(name):
        used.append(nc.alloc_semaphore(name))
        return used[-1]

    def give_back():
        if used:
            nc.clear_and_free_semaphores(used)
            nc.all_engine_barrier()

    ctx.callback(give_back)
    return sb, ps, sem


def chain(eng, sem):
    count = [0]

    def link(ins):
        count[0] += 1
        ins.then_inc(sem, 1)
        eng.wait_ge(sem, count[0])

    return link


def node_tiles(eng, k, j):
    words = [eng.value_load(k.nt_words[0:1, bass.ds(j * (BS // 4) + w, 1)]) for w in range(BS // 4)]
    return [((words[b // 4] >> (6 * (b % 4))) & 63).with_bounds(min_val=0, max_val=NT - 1) for b in range(BS)]


def heads(ap, width=D):
    return ap.rearrange("p (h d) -> p h d", d=width)


def moments(nc, link, stats, mv, ready):
    even, odd = stats[:, :, 1], stats[:, :, 4]
    link(nc.vector.tensor_tensor(mv[:, :, 0], even, odd, ALU.subtract))
    link(nc.vector.tensor_scalar(mv[:, :, 0], mv[:, :, 0], 0.5, None, ALU.mult))
    link(nc.vector.tensor_tensor(mv[:, :, 1], mv[:, :, 0], mv[:, :, 0], ALU.mult))
    link(nc.vector.tensor_tensor(mv[:, :, 0], stats[:, :, 2], stats[:, :, 5], ALU.add))
    link(nc.vector.scalar_tensor_tensor(mv[:, :, 1], mv[:, :, 0], 1.0 / C, mv[:, :, 1], ALU.mult, ALU.add))
    link(nc.vector.tensor_tensor(mv[:, :, 0], even, odd, ALU.add))
    nc.vector.tensor_scalar(mv[:, :, 0], mv[:, :, 0], 0.5, None, ALU.mult).then_inc(ready, 1)


def edge_tables(nc, k):
    with ExitStack() as ctx:
        sb, ps, sem = allocators(nc, ctx)
        dst_in = sb("dst_in", [EP, ER * P], I32)
        src_in = sb("src_in", [EP, ER * P], I32)
        ea_in = sb("ea_in", [EP, ER * P * 3])
        iota_i = sb("iota_i", [P, VPAD], I32)
        nt_row = sb("nt_row", [1, VPAD], I32)
        words_f = sb("words_f", [1, VPAD // 4])
        iota_v = sb("iota_v", [P, VPAD])
        iota_e = sb("iota_e", [P, ER])
        iota_s = sb("iota_s", [P, VC])
        last_tile = sb("last_tile", [EP, ER], I32)
        ends_at = sb("ends_at", [EP, ER])
        passed = sb("passed", [EP, VPAD])
        passed_b = sb("passed_b", [EP, VPAD], BF16)
        ones_b = sb("ones_b", [P, 1], BF16)
        et_raw = sb("et_raw", [P, VC])
        et_f = sb("et_f", [P, VC])
        et_u = sb("et_u", [P, VC], U32)
        nt_f = sb("nt_f", [P, VC])
        nt_i = sb("nt_i", [P, VC], I32)
        nt_base = sb("nt_base", [P, VC])
        dst_g = sb("dst_g", [P, VC, P], I32)
        src_g = sb("src_g", [P, VC, P], I32)
        ea_g = sb("ea_g", [P, VC, P * 3])
        local = sb("local", [P, VC, P])
        local_c = sb("local_c", [P, VC, P])
        local_b = sb("local_b", [P, VC, P], BF16)
        key = sb("key", [P, VC, P])
        src_f = sb("src_f", [P, VC, P])
        ea_rest = sb("ea_rest", [P, VC, 3, P])
        ea_parts = sb("ea_parts", [P, VC, 3, 3, P], BF16)
        ew_t = sb("ew_t", [3, C])
        ew_33 = sb("ew_33", [3, ROW])
        ew_rest = sb("ew_rest", [3, ROW])
        ew_parts = sb("ew_parts", [3, 3, ROW], BF16)
        eb_in = sb("eb_in", [1, C])
        eb_33 = sb("eb_33", [1, ROW])
        eb_rest = sb("eb_rest", [1, ROW])
        eb_parts = sb("eb_parts", [1, 3, ROW], BF16)
        ps_et = ps("ps_et", [P, 512])
        ps_local = ps("ps_local", [P, 2, 512])
        ps_src = ps("ps_src", [P, 2, 512])

        padded, edges_in, edge_w_in = sem("padded"), sem("edges_in"), sem("edge_w_in")
        tables_out, iotas = sem("tables_out"), sem("iotas")
        passed_ready, et_counted, et_ready = sem("passed_ready"), sem("et_counted"), sem("et_ready")
        gathered = [sem(f"gathered{i}") for i in range(3)]
        dve_step, pool_step = sem("et_dve_step"), sem("et_pool_step")
        nt_out, row_in, locals_ready, parts_ready = sem("nt_out"), sem("row_in"), sem("locals_ready"), sem("parts_ready")
        turned, cols_ready, vt_out, w_split, w_out, w_rows = (
            sem("turned"), sem("cols_ready"), sem("vt_out"), sem("w_split"), sem("w_out"), sem("w_rows"))
        block = ctx.enter_context(nc.Block())

        @block.sync
        def _(sp):
            with nc.allow_non_contiguous_dma("a small weight and a short list are read across"):
                sp.dma_start(ew_t[:, :], k.edge_W.rearrange("c f -> f c")).then_inc(edge_w_in, 16)
                sp.dma_start(eb_in[:, :], k.edge_b.rearrange("(a c) -> a c", a=1)).then_inc(edge_w_in, 16)
                sp.wait_ge(padded, 3)
                full = EFULL * ER * P
                for buf, src, w in ((dst_in, k.dst, 1), (src_in, k.src, 1),
                                    (ea_in, k.edge_attr.rearrange("e f -> (e f)"), 3)):
                    sp.dma_start(buf[0:EFULL, :], src[0:full * w].rearrange("(p n) -> p n", p=EFULL)).then_inc(edges_in, 16)
                    sp.dma_start(buf[EFULL:EFULL + 1, 0:EREST * w],
                                 src[full * w:E * w].rearrange("(a n) -> a n", a=1)).then_inc(edges_in, 16)
                sp.wait_ge(edges_in, 96)
                for buf, out in ((dst_in, k.dst_rows), (src_in, k.src_rows), (ea_in, k.ea_rows)):
                    sp.dma_start(out.rearrange("(p r) e -> p (r e)", r=ER), buf[:, :]).then_inc(tables_out, 16)
                sp.wait_ge(w_split, 2)
                sp.dma_start(k.ew_rows.rearrange("j f c -> f j c"), ew_parts[:, :, :]).then_inc(w_out, 16)
                sp.dma_start(k.eb_rows.rearrange("(a j) c -> a j c", a=1), eb_parts[:, :, :]).then_inc(w_out, 16)
                sp.wait_ge(w_out, 32)
                for j in range(3):
                    for f in range(3):
                        r = 9 * j + 3 * f
                        sp.dma_start(k.enc_w[r:r + 3, :], k.ew_rows[j, f:f + 1, :].to_broadcast([3, ROW])).then_inc(w_rows, 16)
                sp.dma_start(k.enc_w[27:30, :], k.eb_rows[:, :]).then_inc(w_rows, 16)
                sp.wait_ge(et_ready, 1)
                sp.dma_start(k.nt_list.rearrange("(c p) -> p c", p=P), nt_i[:, :]).then_inc(nt_out, 16)
                sp.wait_ge(nt_out, 16)
                sp.dma_start(nt_row[:, :], k.nt_list.rearrange("(a v) -> a v", a=1)).then_inc(row_in, 16)
                sp.wait_ge(locals_ready, 1)
                sp.dma_start(k.local_rows.rearrange("(c p) e -> p c e", p=P), local_b[:, :, :]).then_inc(vt_out, 16)
                sp.dma_start(k.key_rows.rearrange("(c p) e -> p c e", p=P), key[:, :, :]).then_inc(vt_out, 16)
                sp.wait_ge(parts_ready, 1)
                for c in range(VC):
                    sp.dma_start(k.ea_parts[:, c * P:(c + 1) * P, :].rearrange("r v e -> v r e"),
                                 ea_parts[:, c].rearrange("p f i e -> p (f i) e")).then_inc(vt_out, 16)
                sp.wait_ge(w_rows, 160)
                sp.wait_ge(row_in, 16)
                sp.wait_ge(vt_out, 16 * (2 + VC))

        @block.gpsimd
        def _(pool):
            link = chain(pool, pool_step)
            nc.gpsimd.memset(dst_in[:, :], NOWHERE).then_inc(padded, 1)
            nc.gpsimd.memset(src_in[:, :], 0).then_inc(padded, 1)
            nc.gpsimd.memset(ea_in[:, :], 0.0).then_inc(padded, 1)
            nc.gpsimd.memset(ones_b[:, :], 1.0).then_inc(iotas, 1)
            link(nc.gpsimd.iota(iota_i[:, :], [[1, VPAD]], 0, 0))
            nc.gpsimd.tensor_copy(iota_v[:, :], iota_i[:, :]).then_inc(iotas, 1)
            nc.gpsimd.tensor_copy(k.iota_row[:, :], iota_i[:, 0:P]).then_inc(iotas, 1)
            pool.wait_ge(iotas, 3)
            link(nc.gpsimd.iota(iota_i[:, 0:ER], [[1, ER]], 0, ER))
            nc.gpsimd.tensor_copy(iota_e[:, :], iota_i[:, 0:ER]).then_inc(iotas, 1)
            link(nc.gpsimd.iota(iota_i[:, P:P + VC], [[P, VC]], 0, 1))
            nc.gpsimd.tensor_copy(iota_s[:, :], iota_i[:, P:P + VC]).then_inc(iotas, 1)
            nc.gpsimd.tensor_copy(k.iota_col[:, :], iota_i[:, P:P + 1]).then_inc(iotas, 1)
            pool.wait_ge(et_ready, 1)
            pool.wait_ge(tables_out, 48)
            for n, (out, rows) in enumerate(((dst_g, k.dst_rows), (src_g, k.src_rows), (ea_g, k.ea_rows))):
                for c in range(VC):
                    pool.indirect_dma_start(out[:, c, :], None, rows[:, :],
                                            bass.IndirectOffsetOnAxis(ap=et_u[:, c:c + 1], axis=0)).then_inc(gathered[n], 16)

        @block.vector
        def _(dve):
            link = chain(dve, dve_step)
            link(nc.vector.memset(ew_33[:, :], 0.0))
            link(nc.vector.memset(eb_33[:, :], 1.0))
            dve.wait_ge(edge_w_in, 32)
            link(nc.vector.tensor_copy(heads(ew_33[:, :], HW)[:, :, 0:D], heads(ew_t[:, :])))
            link(nc.vector.tensor_copy(heads(eb_33[:, :], HW)[:, :, 0:D], heads(eb_in[:, :])))
            for full, rest, parts in ((ew_33, ew_rest, ew_parts), (eb_33, eb_rest, eb_parts)):
                link(nc.vector.tensor_copy(parts[:, 0, :], full[:, :]))
                link(nc.vector.tensor_tensor(rest[:, :], full[:, :], parts[:, 0, :], ALU.subtract))
                link(nc.vector.tensor_copy(parts[:, 1, :], rest[:, :]))
                nc.vector.tensor_tensor(parts[:, 2, :], rest[:, :], parts[:, 1, :], ALU.subtract).then_inc(w_split, 1)
            dve.wait_ge(edges_in, 96)
            dve.wait_ge(iotas, 6)
            link(nc.vector.tensor_scalar(last_tile[:, :], dst_in[:, :].rearrange("p (r e) -> p r e", r=ER)[:, :, P - 1],
                                         7, None, ALU.arith_shift_right))
            link(nc.vector.tensor_scalar(ends_at[:, :], last_tile[:, :], float(NT - 1), None, ALU.min))
            link(nc.vector.tensor_tensor(ends_at[:, :], ends_at[:, :], iota_e[0:EP, :], ALU.add))
            link(nc.vector.tensor_scalar(passed[:, :], iota_v[0:EP, :], ends_at[:, 0:1], None, ALU.is_gt))
            for r in range(1, ER):
                out = passed if r < ER - 1 else passed_b
                ins = nc.vector.scalar_tensor_tensor(out[:, :], iota_v[0:EP, :], ends_at[:, r:r + 1], passed[:, :],
                                                     ALU.is_gt, ALU.add)
                if r < ER - 1:
                    link(ins)
            ins.then_inc(passed_ready, 1)
            dve.wait_ge(et_counted, 1)
            link(nc.vector.tensor_copy(et_raw[:, :], ps_et[:, 0:VC]))
            link(nc.vector.tensor_scalar(et_f[:, :], et_raw[:, :], float(EROWS - 1), 0.0, ALU.min, ALU.max))
            link(nc.vector.tensor_copy(et_u[:, :], et_f[:, :]))
            link(nc.vector.tensor_tensor(nt_f[:, :], iota_s[:, :], et_raw[:, :], ALU.subtract))
            link(nc.vector.tensor_scalar(nt_f[:, :], nt_f[:, :], float(NT - 1), 0.0, ALU.min, ALU.max))
            link(nc.vector.tensor_scalar(nt_base[:, :], nt_f[:, :], float(P), None, ALU.mult))
            nc.vector.tensor_copy(nt_i[:, :], nt_f[:, :]).then_inc(et_ready, 1)
            dve.wait_ge(gathered[0], 16 * VC)
            for c in range(VC):
                link(nc.vector.tensor_scalar(local[:, c, :], dst_g[:, c, :], nt_base[:, c:c + 1], None, ALU.subtract))
            link(nc.vector.tensor_scalar(local_c[:, :, :], local[:, :, :], -1.0, float(P), ALU.max, ALU.min))
            link(nc.vector.tensor_copy(local_b[:, :, :], local_c[:, :, :]))
            link(nc.vector.tensor_scalar(local[:, :, :], local[:, :, :], 0.0, float(P - 1), ALU.max, ALU.min))
            dve.wait_ge(gathered[1], 16 * VC)
            link(nc.vector.tensor_copy(src_f[:, :, :], src_g[:, :, :]))
            for c in range(VC):
                link(nc.vector.tensor_scalar(key[:, c, :], local[:, c, :], nt_base[:, c:c + 1], None, ALU.add))
            nc.vector.memset(k.zero[:, :], 0.0).then_inc(locals_ready, 1)
            dve.wait_ge(gathered[2], 16 * VC)
            ea_v = ea_g[:, :, :].rearrange("p c (e f) -> p c f e", f=3)
            link(nc.vector.tensor_copy(ea_parts[:, :, :, 0, :], ea_v))
            link(nc.vector.tensor_tensor(ea_rest[:, :, :, :], ea_v, ea_parts[:, :, :, 0, :], ALU.subtract))
            link(nc.vector.tensor_copy(ea_parts[:, :, :, 1, :], ea_rest[:, :, :, :]))
            nc.vector.tensor_tensor(ea_parts[:, :, :, 2, :], ea_rest[:, :, :, :], ea_parts[:, :, :, 1, :],
                                    ALU.subtract).then_inc(parts_ready, 1)
            dve.wait_ge(row_in, 16)
            by_four = nt_row[:, :].rearrange("a (w i) -> a w i", i=4)
            link(nc.vector.tensor_copy(words_f[:, :], by_four[:, :, 3]))
            for i in (2, 1, 0):
                out = words_f if i else k.nt_words
                link(nc.vector.scalar_tensor_tensor(out[:, :], words_f[:, :], 64.0, by_four[:, :, i], ALU.mult, ALU.add))
            dve.wait_ge(turned, 1)
            for a in range(2):
                n = 4 * P if a == 0 else (VC - 4) * P
                nc.vector.tensor_copy(k.local_col[:, 4 * P * a:4 * P * a + n], ps_local[:, a, 0:n])
                nc.vector.tensor_copy(k.src_col[:, 4 * P * a:4 * P * a + n], ps_src[:, a, 0:n]).then_inc(cols_ready, 1)
            dve.wait_ge(cols_ready, 2)

        @block.tensor
        def _(pe):
            pe.wait_ge(passed_ready, 1)
            pe.wait_ge(iotas, 6)
            for c in range(VC):
                last = nc.tensor.matmul(ps_et[:, c:c + 1], passed_b[:, c * P:(c + 1) * P], ones_b[0:EP, :],
                                        start=True, stop=True)
            last.then_inc(et_counted, 1)
            pe.wait_ge(locals_ready, 1)
            for c in range(VC):
                nc.tensor.transpose(ps_local[:, c // 4, (c % 4) * P:(c % 4 + 1) * P], local_c[:, c, :], k.ident[:, :])
                last = nc.tensor.transpose(ps_src[:, c // 4, (c % 4) * P:(c % 4 + 1) * P], src_f[:, c, :], k.ident[:, :])
            last.then_inc(turned, 1)


def constants(nc, k):
    with ExitStack() as ctx:
        sb, ps, sem = allocators(nc, ctx)
        zeroed = sem("zeroed")
        made = sem("consts_made")
        block = ctx.enter_context(nc.Block())

        @block.gpsimd
        def _(pool):
            nc.gpsimd.memset(k.ident[:, :], 0.0).then_inc(zeroed, 1)
            nc.gpsimd.memset(k.eps[:, :], EPS)
            pool.wait_ge(zeroed, 1)
            nc.gpsimd.affine_select(out=k.ident[:, :], in_=k.ident[:, :], compare_op=ALU.not_equal, fill=1.0, base=0,
                                    pattern=[[-1, P]], channel_multiplier=1).then_inc(made, 1)
            pool.wait_ge(made, 1)


def node_rows(nc, k):
    with ExitStack() as ctx:
        sb, ps, sem = allocators(nc, ctx)
        w_nat = sb("w_nat", [P, 2, C])
        a_cols = sb("a_cols", [P, 2, 2])
        a_mask = sb("a_mask", [P, 2, H])
        a_blocks = sb("a_blocks", [P, 2, 2 * H])
        w_node = sb("w_node", [P, 2, NW])
        w_qkv = sb("w_qkv", [P, 2, QW])
        g_pre = sb("g_pre", [P, 2])
        stats = sb("stats", [P, NT, 6])
        mv = sb("mv", [P, NT, 2])
        std = sb("std", [P, NT])
        xn = sb("xn", [P, G, C])
        xn_t = sb("xn_t", [P, 2, 2, P])
        h_row = sb("h_row", [P, G, ROW])
        h_out = sb("h_out", [P, 2, NW])
        h_dst = sb("h_dst", [P, 2, ROW])
        h_rest = sb("h_rest", [P, 2, ROW])
        h_parts = sb("h_parts", [P, G, 3, ROW], BF16)
        s_src = sb("s_src", [P, NT, H])
        ps_w = ps("ps_w", [P, 512])
        ps_t = [ps(f"ps_t{i}", [P, 512]) for i in range(2)]
        ps_h = [ps(f"ps_h{i}", [P, 512]) for i in range(2)]
        ps_q = [ps(f"ps_q{i}", [P, 512]) for i in range(2)]

        w_in, x_in, x_pad = sem("w_in"), sem("x_in"), sem("x_pad")
        pool_step, dve_step, act_step = sem("n_pool_step"), sem("n_dve_step"), sem("n_act_step")
        mask_ready, blocks_ready, qkv_w_ready = sem("mask_ready"), sem("blocks_ready"), sem("qkv_w_ready")
        w_turned, w_node_ready, a_folded = sem("w_turned"), sem("w_node_ready"), sem("a_folded")
        stats_ready, std_ready, rstd_ready, squared, norm_ready = (
            sem("stats_ready"), sem("std_ready"), sem("rstd_ready"), sem("squared"), sem("norm_ready"))
        xn_ready, x_turned, xt_ready, h_done, q_done = (
            sem("xn_ready"), sem("x_turned"), sem("xt_ready"), sem("h_done"), sem("q_done"))
        ps_h_free, h_taken, ps_q_free, dve_split = sem("ps_h_free"), sem("h_taken"), sem("ps_q_free"), sem("dve_split")
        src_done, pool_seen = sem("src_done"), sem("pool_seen")
        rows_ready, parts_ready = sem("rows_ready"), sem("h_parts_ready")
        rows_out = [sem(f"rows_out{g}") for g in range(G)]
        parts_out = [sem(f"parts_out{g}") for g in range(G)]
        ones_set, src_out, stat_steps, squares = sem("ones_set"), sem("src_out"), sem("stat_steps"), sem("squares")
        block = ctx.enter_context(nc.Block())

        @block.sync
        def _(sp):
            with nc.allow_non_contiguous_dma("vectors laid down the partitions"):
                sp.wait_ge(x_pad, 1)
                for t in range(0, NT - 1, 8):
                    sp.dma_start(k.x_res[:, t:t + 8, :], k.x[t * P:(t + 8) * P, :].rearrange("(t p) c -> p t c", p=P)).then_inc(x_in, 16)
                sp.dma_start(k.x_res[0:NLAST, NT - 1, :], k.x[(NT - 1) * P:N, :]).then_inc(x_in, 16)
                sp.dma_start(w_nat[:, :, :], k.W.rearrange("(a p) c -> p a c", p=P)).then_inc(w_in, 16)
                sp.dma_start(a_cols[:, :, 0], k.a_src.rearrange("h d -> (h d)").rearrange("(a p) -> p a", p=P)).then_inc(w_in, 16)
                sp.dma_start(a_cols[:, :, 1], k.a_dst.rearrange("h d -> (h d)").rearrange("(a p) -> p a", p=P)).then_inc(w_in, 16)
                sp.dma_start(w_qkv[:, :, :], k.w_qkv.rearrange("(a p) c -> p a c", p=P)).then_inc(w_in, 16)
                sp.dma_start(g_pre[:, :], k.g_pre.rearrange("(a p) -> p a", p=P)).then_inc(w_in, 16)
            with sp.Fori(0, NT // G) as it:
                for g in range(G):
                    sp.wait_ge(rows_ready, it * G + (g + 3))
                    sp.dma_start(k.h_rows[bass.ds((it * G + g) * P, P), :], h_row[:, g, :]).then_inc(rows_out[g], 16)
                    sp.wait_ge(parts_ready, it * G + (g + 1))
                    sp.dma_start(k.hd_parts[bass.ds((it * G + g) * P, P), :],
                                 h_parts[:, g].rearrange("p i c -> p (i c)")).then_inc(parts_out[g], 16)
            sp.wait_ge(rows_ready, NT + 2)
            sp.dma_start(k.src_logits.rearrange("(t p) h -> p t h", p=P), s_src[:, :, :]).then_inc(src_out, 16)
            for g in range(G):
                sp.wait_ge(rows_out[g], 16 * (NT // G + 1))
                sp.wait_ge(parts_out[g], 16 * (NT // G + 1))
            sp.wait_ge(src_out, 16)

        @block.gpsimd
        def _(pool):
            link = chain(pool, pool_step)
            nc.gpsimd.memset(k.x_res[:, NT - 1, :], 0.0).then_inc(x_pad, 1)
            nc.gpsimd.memset(h_row[:, :, :], 1.0).then_inc(ones_set, 1)
            link(nc.gpsimd.memset(a_mask[:, :, :], 1.0))
            link(nc.gpsimd.affine_select(out=a_mask[:, :, :], in_=a_mask[:, :, :], compare_op=ALU.is_ge, fill=0.0, base=0,
                                         pattern=[[P, 2], [-D, H]], channel_multiplier=1))
            nc.gpsimd.affine_select(out=a_mask[:, :, :], in_=a_mask[:, :, :], compare_op=ALU.is_ge, fill=0.0, base=D - 1,
                                    pattern=[[-P, 2], [D, H]], channel_multiplier=-1).then_inc(mask_ready, 1)
            pool.wait_ge(ones_set, 1)
            with pool.Fori(0, NT // G) as it:
                for g in range(G):
                    t = it * G + g
                    pool.wait_ge(ps_h_free, t + 3)
                    pool.wait_ge(rows_out[g], it * 16 + 16)
                    pool.sem_inc(pool_seen, 1)
                    nc.gpsimd.tensor_copy(heads(h_row[:, g, :], HW)[:, :, 0:D], heads(h_out[:, g % 2, 0:C]))
                    nc.gpsimd.tensor_copy(s_src[:, bass.ds(t, 1), :], h_out[:, g % 2, C:C + H]).then_inc(rows_ready, 1)

        @block.vector
        def _(dve):
            link = chain(dve, dve_step)
            dve.wait_ge(w_in, 80)
            dve.wait_ge(mask_ready, 1)
            for a in range(2):
                nc.vector.tensor_scalar(a_blocks[:, a, 0:H], a_mask[:, a, :], a_cols[:, a, 0:1], None, ALU.mult)
                last = nc.vector.tensor_scalar(a_blocks[:, a, H:2 * H], a_mask[:, a, :], a_cols[:, a, 1:2], None, ALU.mult)
            last.then_inc(blocks_ready, 1)
            for a in range(2):
                link(nc.vector.tensor_scalar(w_qkv[:, a, :], w_qkv[:, a, :], g_pre[:, a:a + 1], None, ALU.mult))
            for a in range(2):
                dve.wait_ge(w_turned, a + 1)
                last = nc.vector.tensor_copy(w_node[:, a, 0:C], ps_w[:, 0:C])
                last.then_inc(w_node_ready, 1)
            dve.wait_ge(a_folded, 1)
            for a in range(2):
                nc.vector.tensor_copy(w_node[:, a, C:NW], ps_w[:, C + 2 * H * a:C + 2 * H * (a + 1)]).then_inc(w_node_ready, 1)
            dve.wait_ge(x_in, 16 * 7)
            with dve.Fori(0, NT) as t:
                nc.vector.bn_stats(stats[:, bass.ds(t, 1), :], k.x_res[:, bass.ds(t, 1), :]).then_inc(stat_steps, 1)
            dve.wait_ge(stat_steps, NT)
            moments(nc, link, stats, mv, stats_ready)
            dve.wait_ge(stats_ready, 1)
            dve.wait_ge(std_ready, 1)
            link(nc.vector.reciprocal(k.rstd[:, :], std[:, :]))
            nc.vector.scalar_tensor_tensor(k.shift[:, :], mv[:, :, 0], -1.0, k.rstd[:, :], ALU.mult, ALU.mult).then_inc(rstd_ready, 1)
            dve.wait_ge(squared, 1)
            link(nc.vector.tensor_scalar(k.norm[:, :], k.norm[:, :], 1e-12, 1.0 / 16.0, ALU.max, ALU.mult))
            nc.vector.reciprocal(k.norm[:, :], k.norm[:, :]).then_inc(norm_ready, 1)
            with dve.Fori(0, NT // G) as it:
                for g in range(G):
                    s = g % 2
                    dve.wait_ge(ps_h_free, it * G + (g + 3))
                    nc.vector.tensor_copy(heads(h_dst[:, s, :], HW)[:, :, D], h_out[:, s, C + H:NW])
                    nc.vector.tensor_copy(heads(h_dst[:, s, :], HW)[:, :, 0:D], heads(h_out[:, s, 0:C])).then_inc(h_taken, 1)
                    dve.wait_ge(h_taken, it * G + (g + 3))
                    dve.wait_ge(parts_out[g], it * 16 + 16)
                    nc.vector.tensor_copy(h_parts[:, g, 0, :], h_dst[:, s, :]).then_inc(dve_split, 1)
                    dve.wait_ge(dve_split, (it * G + g) * 3 + 1)
                    nc.vector.tensor_tensor(h_rest[:, s, :], h_dst[:, s, :], h_parts[:, g, 0, :], ALU.subtract).then_inc(dve_split, 1)
                    dve.wait_ge(dve_split, (it * G + g) * 3 + 2)
                    nc.vector.tensor_copy(h_parts[:, g, 1, :], h_rest[:, s, :]).then_inc(dve_split, 1)
                    dve.wait_ge(dve_split, (it * G + g) * 3 + 3)
                    nc.vector.tensor_tensor(h_parts[:, g, 2, :], h_rest[:, s, :], h_parts[:, g, 1, :], ALU.subtract).then_inc(parts_ready, 1)

        @block.scalar
        def _(act):
            link = chain(act, act_step)
            for g in range(G):
                act.sem_inc(parts_out[g], 16)
                act.sem_inc(rows_out[g], 16)
            act.sem_inc(ps_h_free, 2)
            act.sem_inc(h_taken, 2)
            act.sem_inc(rows_ready, 2)
            act.sem_inc(ps_q_free, 2)
            act.wait_ge(stats_ready, 1)
            nc.scalar.activation(std[:, :], mv[:, :, 1], ACT.Sqrt, bias=k.eps[:, 0:1]).then_inc(std_ready, 1)
            act.wait_ge(rstd_ready, 1)
            act.sem_inc(squares, G)
            with act.Fori(0, NT // G) as it:
                for g in range(G):
                    t = it * G + g
                    act.wait_ge(squares, t + 1)
                    nc.scalar.activation(xn[:, g, :], k.x_res[:, bass.ds(t, 1), :], ACT.Square, scale=k.rstd[:, bass.ds(t, 1)],
                                         bias=k.shift[:, bass.ds(t, 1)], accum_out=k.norm[:, bass.ds(t, 1)]).then_inc(squares, 1)
            act.wait_ge(squares, NT + G)
            nc.scalar.activation(k.norm[:, :], k.norm[:, :], ACT.Sqrt).then_inc(squared, 1)
            act.wait_ge(norm_ready, 1)
            act.wait_ge(ones_set, 1)
            with act.Fori(0, NT // G) as it:
                for g in range(G + 1):
                    if g < G:
                        s = g % 2
                        nc.scalar.activation(xn[:, g, :], k.x_res[:, bass.ds(it * G + g, 1), :], ACT.Identity,
                                             scale=k.rstd[:, bass.ds(it * G + g, 1)],
                                             bias=k.shift[:, bass.ds(it * G + g, 1)]).then_inc(xn_ready, 1)
                        act.wait_ge(x_turned, it * G + (g + 1))
                        nc.scalar.copy(xn_t[:, s].rearrange("p a n -> p (a n)"), ps_t[s][:, 0:C]).then_inc(xt_ready, 1)
                    if g >= 1:
                        b = g - 1
                        s = b % 2
                        act.wait_ge(h_done, it * G + (b + 1))
                        back = 2 if b else 1
                        act.wait_ge(rows_ready, it * G + (b + 3 - back))
                        act.wait_ge(h_taken, it * G + (b + 3 - back))
                        nc.scalar.copy(h_out[:, s, :], ps_h[s][:, 0:NW]).then_inc(ps_h_free, 1)
                        act.wait_ge(q_done, it * G + (b + 1))
                        nc.scalar.activation(k.qkv[:, bass.ds(it * G + b, 1), 0:QW], ps_q[s][:, 0:QW], ACT.Copy,
                                             scale=k.norm[:, bass.ds(it * G + b, 1)]).then_inc(ps_q_free, 1)

        @block.tensor
        def _(pe):
            pe.wait_ge(w_in, 80)
            for a in range(2):
                if a:
                    pe.wait_ge(w_node_ready, 1)
                for b in range(2):
                    last = nc.tensor.transpose(ps_w[:, b * P:(b + 1) * P], w_nat[:, b, a * P:(a + 1) * P], k.ident[:, :])
                last.then_inc(w_turned, 1)
            pe.wait_ge(blocks_ready, 1)
            pe.wait_ge(w_node_ready, 2)
            for a in range(2):
                for b in range(2):
                    last = nc.tensor.matmul(ps_w[:, C + 2 * H * a:C + 2 * H * (a + 1)], w_nat[:, b, a * P:(a + 1) * P],
                                            a_blocks[:, b, :], start=b == 0, stop=b == 1)
            last.then_inc(a_folded, 1)
            pe.wait_ge(w_node_ready, 4)
            pe.wait_ge(dve_step, 2)
            with pe.Fori(0, NT // G) as it:
                for g in range(G + 1):
                    if g < G:
                        s = g % 2
                        pe.wait_ge(xn_ready, it * G + (g + 1))
                        if g >= 2:
                            pe.wait_ge(xt_ready, it * G + (g - 1))
                        for a in range(2):
                            last = nc.tensor.transpose(ps_t[s][:, a * P:(a + 1) * P], xn[:, g, a * P:(a + 1) * P], k.ident[:, :])
                        last.then_inc(x_turned, 1)
                    if g >= 1:
                        b = g - 1
                        s = b % 2
                        pe.wait_ge(xt_ready, it * G + (b + 1))
                        back = 2 if b else 1
                        pe.wait_ge(ps_h_free, it * G + (b + 3 - back))
                        for a in range(2):
                            last = nc.tensor.matmul(ps_h[s][:, 0:NW], xn_t[:, s, a, :], w_node[:, a, :], start=a == 0, stop=a == 1)
                        last.then_inc(h_done, 1)
                        pe.wait_ge(ps_q_free, it * G + (b + 3 - back))
                        for a in range(2):
                            last = nc.tensor.matmul(ps_q[s][:, 0:QW], xn_t[:, s, a, :], w_qkv[:, a, :], start=a == 0, stop=a == 1)
                        last.then_inc(q_done, 1)


def edge_logits(nc, k):
    with ExitStack() as ctx:
        sb, ps, sem = allocators(nc, ctx)
        hd_tab = sb("hd_tab", [P, NT, 3 * ROW], BF16)
        ea_t = [sb(f"ea_t{s}", [30, BS * P], BF16) for s in range(2)]
        loc_row = [sb(f"loc_row{s}", [P, BS * P], BF16) for s in range(2)]
        onehot = [sb(f"onehot{s}", [P, BS * P], BF16) for s in range(2)]
        src_idx = [sb(f"src_idx{s}", [P, BS], U32) for s in range(2)]
        src_ring = [sb(f"src_ring{s}", [P, BS, H]) for s in range(2)]
        enc = sb("enc", [P, 4, ROW])
        prod = sb("prod", [P, 4, ROW])
        src_all = sb("src_all", [P, V, H])
        outside = sb("outside", [P, V])
        outside2 = sb("outside2", [P, V])
        ps_enc = [ps(f"ps_enc{i}", [P, 512]) for i in range(4)]
        ps_hd = [ps(f"ps_hd{i}", [P, 512]) for i in range(4)]
        tab_in, set_up = sem("tab_in"), sem("set_up")
        ea_in = [sem(f"ea_in{s}") for s in range(2)]
        loc_in = [sem(f"loc_in{s}") for s in range(2)]
        src_in = [sem(f"src_in{s}") for s in range(2)]
        enc_done, relu_done, hd_done = sem("enc_done"), sem("relu_done"), sem("hd_done")
        prod_done, reduced, onehot_ready, block_done = sem("prod_done"), sem("reduced"), sem("onehot_ready"), sem("block_done")
        src_taken, idx_ready, idx_seen, out_step = sem("src_taken"), sem("idx_ready"), sem("idx_seen"), sem("b_out_step")
        block = ctx.enter_context(nc.Block())

        @block.sync
        def _(sp):
            for t in range(0, NT, G):
                sp.dma_start(hd_tab[:, t:t + G, :], k.hd_parts[t * P:(t + G) * P, :].rearrange("(t p) c -> p t c", p=P)).then_inc(tab_in, 16)
            sp.wait_ge(set_up, 2)
            with sp.Fori(0, NBLK // 2) as it:
                for s in range(2):
                    v0 = (it * 2 + s) * BS
                    sp.wait_ge(block_done, it * 2 + (s + 1))
                    sp.wait_ge(onehot_ready, it * 2 + (s + 1))
                    for j in range(3):
                        sp.dma_start(ea_t[s][9 * j:9 * j + 9, :],
                                     k.ea_parts[:, bass.ds(v0, BS), :].rearrange("r v e -> r (v e)")).then_inc(ea_in[s], 16)
                    sp.dma_start(loc_row[s][:, :], k.local_rows[bass.ds(v0, BS), :].rearrange("(a v) e -> a (v e)", a=1)
                                 .to_broadcast([P, BS * P])).then_inc(loc_in[s], 16)

        @block.gpsimd
        def _(pool):
            for s in range(2):
                nc.gpsimd.memset(ea_t[s][:, :], 1.0).then_inc(set_up, 1)
            with pool.Fori(0, NBLK // 2) as it:
                for s in range(2):
                    j = it * 2 + s
                    pool.wait_ge(src_taken, j + 1)
                    pool.sem_inc(idx_seen, 1)
                    nc.gpsimd.tensor_copy(src_idx[s][:, :], k.src_col[:, bass.ds(j * BS, BS)]).then_inc(idx_ready, 1)
                    pool.wait_ge(idx_ready, j + 1)
                    pool.sem_inc(idx_seen, 1)
                    for b in range(BS):
                        pool.indirect_dma_start(src_ring[s][:, b, :], None, k.src_logits[:, :],
                                                bass.IndirectOffsetOnAxis(ap=src_idx[s][:, b:b + 1], axis=0)).then_inc(src_in[s], 16)

        @block.scalar
        def _(act):
            act.sem_inc(block_done, 2)
            act.sem_inc(onehot_ready, 2)
            act.sem_inc(src_taken, 2)
            act.sem_inc(relu_done, 4)
            act.sem_inc(prod_done, 4)
            act.sem_inc(reduced, 4)
            with act.Fori(0, NBLK // 2) as it:
                for s in range(2):
                    j = it * 2 + s
                    for b in range(BS):
                        v = j * BS + b
                        act.wait_ge(enc_done, v + 1)
                        act.wait_ge(prod_done, v + 1)
                        nc.scalar.activation(enc[:, b % 4, :], ps_enc[b % 4][:, 0:ROW], ACT.Relu).then_inc(relu_done, 1)
                    act.wait_ge(src_in[s], (it + 1) * (16 * BS))
                    nc.scalar.copy(src_all[:, bass.ds(j * BS, BS), :], src_ring[s][:, :, :]).then_inc(src_taken, 1)

        @block.tensor
        def _(pe):
            pe.wait_ge(tab_in, 16 * (NT // G))
            with pe.Fori(0, NBLK // 2) as it:
                for s in range(2):
                    j = it * 2 + s
                    nts = node_tiles(pe, k, j)
                    pe.wait_ge(ea_in[s], (it + 1) * 48)
                    for b in range(BS):
                        v = j * BS + b
                        e = slice(b * P, (b + 1) * P)
                        pe.wait_ge(relu_done, v + 1)
                        nc.tensor.matmul(ps_enc[b % 4][:, 0:ROW], ea_t[s][:, e], k.enc_w[:, :], start=True, stop=True).then_inc(enc_done, 1)
                        if b == 0:
                            pe.wait_ge(onehot_ready, j + 3)
                        pe.wait_ge(prod_done, v + 1)
                        for i in range(3):
                            last = nc.tensor.matmul(ps_hd[b % 4][:, 0:ROW], onehot[s][:, e],
                                                    hd_tab[:, bass.ds(nts[b], 1), i * ROW:(i + 1) * ROW], start=i == 0, stop=i == 2)
                        last.then_inc(hd_done, 1)
                    pe.wait_ge(hd_done, (j + 1) * BS)
                    pe.sem_inc(block_done, 1)

        @block.vector
        def _(dve):
            link = chain(dve, out_step)
            with dve.Fori(0, NBLK // 2) as it:
                for s in range(2):
                    j = it * 2 + s
                    dve.wait_ge(loc_in[s], (it + 1) * 16)
                    dve.wait_ge(block_done, j + 1)
                    nc.vector.tensor_scalar(onehot[s][:, :], loc_row[s][:, :], k.iota_col[:, 0:1], None, ALU.is_equal).then_inc(onehot_ready, 1)
                    for b in range(BS + 1):
                        v = j * BS + b
                        if b < BS:
                            dve.wait_ge(hd_done, v + 1)
                            dve.wait_ge(relu_done, v + 5)
                            dve.wait_ge(reduced, v + 1)
                            nc.vector.tensor_tensor(prod[:, b % 4, :], enc[:, b % 4, :], ps_hd[b % 4][:, 0:ROW], ALU.mult).then_inc(prod_done, 1)
                        if b >= 1:
                            dve.wait_ge(prod_done, v + 4)
                            nc.vector.tensor_reduce(k.alpha[:, bass.ds(v - 1, 1), :], heads(prod[:, (b - 1) % 4, :], HW), AX.X, ALU.add).then_inc(reduced, 1)
            dve.wait_ge(src_taken, NBLK + 2)
            dve.wait_ge(reduced, V + 4)
            link(nc.vector.tensor_tensor(k.alpha[:, :, :], k.alpha[:, :, :], src_all[:, :, :], ALU.add))
            link(nc.vector.tensor_scalar(src_all[:, :, :], k.alpha[:, :, :], 0.2, None, ALU.mult))
            link(nc.vector.tensor_tensor(k.alpha[:, :, :], k.alpha[:, :, :], src_all[:, :, :], ALU.max))
            link(nc.vector.tensor_scalar(outside[:, :], k.local_col[:, 0:V], 0.0, -BIG, ALU.is_lt, ALU.mult))
            link(nc.vector.tensor_scalar(outside2[:, :], k.local_col[:, 0:V], float(P), -BIG, ALU.is_ge, ALU.mult))
            link(nc.vector.tensor_tensor(outside[:, :], outside[:, :], outside2[:, :], ALU.add))
            link(nc.vector.tensor_tensor(k.alpha[:, :, :], k.alpha[:, :, :], outside[:, :].unsqueeze(2).to_broadcast([P, V, H]), ALU.add))


def segment_softmax(nc, k):
    with ExitStack() as ctx:
        sb, ps, sem = allocators(nc, ctx)
        L = CT * P
        gathered_cols = [sb(f"turn_in{s}", [P, 2, P]) for s in range(2)]
        alpha_t = sb("alpha_t", [P, L])
        key_t = sb("key_t", [P, L])
        reset = sb("reset", [P, L + 1])
        fwd = sb("fwd", [P, L])
        best = sb("best", [P, L])
        edge_stat = sb("edge_stat", [P, 4])
        stat_all = sb("stat_all", [P, CH, 4])
        other = sb("other", [P, 2, 2, CH])
        across = sb("across", [P, 2])
        zeros = sb("zero_rows", [P, 2, C])
        zeroed, cleared = sem("zero_rows_set"), sem("cleared")
        ps_in = [ps(f"ps_in{s}", [P, 512]) for s in range(2)]
        ps_out = [ps(f"ps_out{s}", [P, 512]) for s in range(2)]
        keys_in, stat_ready, stat_out, stat_in = sem("keys_in"), sem("stat_ready"), sem("stat_out"), sem("stat_in")
        cols_ready, cols_turned, cols_copied = sem("s_cols_ready"), sem("s_cols_turned"), sem("s_cols_copied")
        shifted, exp_ready, exp_turned, exp_copied = sem("shifted"), sem("exp_ready"), sem("exp_turned"), sem("exp_copied")
        dve_step = sem("s_dve_step")
        block = ctx.enter_context(nc.Block())
        by_chunk = k.alpha[:, :, :].rearrange("p (j g) h -> p g j h", g=CT)

        @block.sync
        def _(sp):
            for j in range(CH):
                sp.dma_start(key_t[H * j:H * (j + 1), :], k.key_rows[j * CT:(j + 1) * CT, :].rearrange("(a v) e -> a (v e)", a=1)
                             .to_broadcast([H, L])).then_inc(keys_in, 16)
            sp.wait_ge(stat_ready, 4)
            sp.dma_start(k.chunk_stats[:, :], edge_stat[:, :]).then_inc(stat_out, 16)
            sp.wait_ge(stat_out, 16)
            for j in range(CH):
                sp.dma_start(stat_all[H * j:H * (j + 1), :, :], k.chunk_stats.rearrange("(i h) c -> h i c", h=H)).then_inc(stat_in, 16)
            sp.wait_ge(zeroed, 1)
            for b in range(0, NB, 2):
                sp.dma_start(k.list_rows[b * P:(b + 2) * P, :].rearrange("(t p) c -> p t c", p=P), zeros[:, :, :]).then_inc(cleared, 16)
            sp.wait_ge(cleared, 8 * NB)

        @block.gpsimd
        def _(pool):
            nc.gpsimd.memset(zeros[:, :, :], 0.0).then_inc(zeroed, 1)

        @block.scalar
        def _(act):
            act.sem_inc(cols_turned, 2)
            act.sem_inc(cols_copied, 2)
            with act.Fori(0, CT // 4) as it:
                for s in range(2):
                    act.wait_ge(cols_turned, it * 2 + (s + 1))
                    nc.scalar.copy(gathered_cols[s][:, :, :].rearrange("p g (j h) -> p g j h", h=H),
                                   by_chunk[:, bass.ds(it * 4 + 2 * s, 2), :, :]).then_inc(cols_ready, 1)
            act.wait_ge(shifted, 1)
            with act.Fori(0, CT // 4) as it:
                for s in range(2):
                    act.wait_ge(exp_turned, it * 2 + (s + 1))
                    nc.scalar.activation(gathered_cols[s][:, :, :].rearrange("p g e -> p (g e)"),
                                         alpha_t[:, bass.ds((it * 4 + 2 * s) * P, 2 * P)], ACT.Exp).then_inc(exp_ready, 1)

        @block.tensor
        def _(pe):
            with pe.Fori(0, CT // 4) as it:
                for s in range(2):
                    pe.wait_ge(cols_ready, it * 2 + (s + 1))
                    pe.wait_ge(cols_copied, it * 2 + (s + 1))
                    for g in range(2):
                        last = nc.tensor.transpose(ps_in[s][:, g * P:(g + 1) * P], gathered_cols[s][:, g, :], k.ident[:, :])
                    last.then_inc(cols_turned, 1)
            with pe.Fori(0, CT // 4) as it:
                for s in range(2):
                    pe.wait_ge(exp_ready, it * 2 + (s + 1))
                    pe.wait_ge(exp_copied, it * 2 + (s + 1))
                    for g in range(2):
                        last = nc.tensor.transpose(ps_out[s][:, g * P:(g + 1) * P], gathered_cols[s][:, g, :], k.ident[:, :])
                    last.then_inc(exp_turned, 1)

        @block.vector
        def _(dve):
            link = chain(dve, dve_step)
            dve.sem_inc(exp_turned, 2)
            dve.sem_inc(exp_copied, 2)
            with dve.Fori(0, CT // 4) as it:
                for s in range(2):
                    dve.wait_ge(cols_turned, it * 2 + (s + 3))
                    nc.vector.tensor_copy(alpha_t[:, bass.ds((it * 4 + 2 * s) * P, 2 * P)], ps_in[s][:, 0:2 * P]).then_inc(cols_copied, 1)
            dve.wait_ge(keys_in, 16 * CH)
            nc.vector.memset(reset[:, 0:1], 0.0)
            nc.vector.memset(reset[:, L:L + 1], 0.0)
            link(nc.vector.tensor_tensor(reset[:, 1:L], key_t[:, 1:L], key_t[:, 0:L - 1], ALU.not_equal))
            link(nc.vector.tensor_scalar(reset[:, 1:L], reset[:, 1:L], -BIG * 1e6, None, ALU.mult))
            dve.wait_ge(cols_copied, CT // 2 + 2)
            link(nc.vector.tensor_tensor_scan(fwd[:, :], reset[:, 0:L], alpha_t[:, :], -BIG * 1e6, ALU.add, ALU.max))
            link(nc.vector.tensor_tensor_scan(best[:, ::-1], reset[:, 1:L + 1][:, ::-1], fwd[:, ::-1], -BIG * 1e6, ALU.add, ALU.max))
            for c, col in enumerate((best[:, 0:1], best[:, L - 1:L], key_t[:, 0:1], key_t[:, L - 1:L])):
                nc.vector.tensor_copy(edge_stat[:, c:c + 1], col).then_inc(stat_ready, 1)
            dve.wait_ge(stat_in, 16 * CH)
            dve.wait_ge(stat_ready, 4)
            for mine in range(2):
                for theirs in range(2):
                    link(nc.vector.tensor_scalar(other[:, mine, theirs, :], stat_all[:, :, 2 + theirs], edge_stat[:, 2 + mine:3 + mine],
                                                 -BIG * 1e6, ALU.not_equal, ALU.mult))
                    link(nc.vector.tensor_tensor(other[:, mine, theirs, :], other[:, mine, theirs, :], stat_all[:, :, theirs], ALU.add))
            link(nc.vector.tensor_reduce(across[:, :], other[:, :, :, :], AX.XY, ALU.max))
            for mine in range(2):
                link(nc.vector.tensor_scalar(reset[:, 0:L], key_t[:, :], edge_stat[:, 2 + mine:3 + mine], -BIG * 1e6,
                                             ALU.not_equal, ALU.mult))
                link(nc.vector.scalar_tensor_tensor(best[:, :], reset[:, 0:L], across[:, mine:mine + 1], best[:, :], ALU.add, ALU.max))
            nc.vector.tensor_tensor(alpha_t[:, :], alpha_t[:, :], best[:, :], ALU.subtract).then_inc(shifted, 1)
            with dve.Fori(0, CT // 4) as it:
                for s in range(2):
                    dve.wait_ge(exp_turned, it * 2 + (s + 3))
                    nc.vector.tensor_copy(by_chunk[:, bass.ds(it * 4 + 2 * s, 2), :, :],
                                          ps_out[s][:, 0:2 * P].rearrange("p (g j h) -> p g j h", g=2, h=H)).then_inc(exp_copied, 1)


def aggregate(nc, k):
    with ExitStack() as ctx:
        sb, ps, sem = allocators(nc, ctx)
        src_idx = [sb(f"row_idx{s}", [P, BS], U32) for s in range(2)]
        rows = [sb(f"rows{s}", [P, BS, ROW]) for s in range(2)]
        weighted = sb("weighted", [P, 4, ROW])
        away = sb("away", [P, 4, P])
        onehot = sb("onehot_f", [P, 4, P])
        ps_sum = [ps(f"ps_sum{i}", [P, 512]) for i in range(4)]
        rows_in = [sem(f"rows_in{s}") for s in range(2)]
        idx_ready, idx_seen, weighted_ready, onehot_ready = sem("d_idx_ready"), sem("d_idx_seen"), sem("weighted_ready"), sem("d_onehot_ready")
        summed, added, away_ready = sem("summed"), sem("added"), sem("away_ready")
        block = ctx.enter_context(nc.Block())

        @block.gpsimd
        def _(pool):
            with pool.Fori(0, NBLK // 2) as it:
                for s in range(2):
                    j = it * 2 + s
                    pool.wait_ge(weighted_ready, (j + 1) * BS)
                    pool.sem_inc(idx_seen, 1)
                    nc.gpsimd.tensor_copy(src_idx[s][:, :], k.src_col[:, bass.ds(j * BS, BS)]).then_inc(idx_ready, 1)
                    pool.wait_ge(idx_ready, j + 1)
                    pool.sem_inc(idx_seen, 1)
                    for b in range(BS):
                        pool.indirect_dma_start(rows[s][:, b, :], None, k.h_rows[:, :],
                                                bass.IndirectOffsetOnAxis(ap=src_idx[s][:, b:b + 1], axis=0)).then_inc(rows_in[s], 16)

        @block.scalar
        def _(act):
            with act.Fori(0, NBLK // 2) as it:
                for s in range(2):
                    for b in range(BS):
                        v = (it * 2 + s) * BS + b
                        act.wait_ge(summed, v + 1)
                        nc.scalar.activation(away[:, b % 4, :], k.iota_row[:, :], ACT.Abs, scale=-1.0,
                                             bias=k.local_col[:, bass.ds(v, 1)]).then_inc(away_ready, 1)
                        act.wait_ge(away_ready, v + 1)
                        nc.scalar.activation(onehot[:, b % 4, :], away[:, b % 4, :], ACT.Relu, scale=-1.0, bias=1.0).then_inc(onehot_ready, 1)

        @block.tensor
        def _(pe):
            with pe.Fori(0, NBLK // 2) as it:
                for s in range(2):
                    for b in range(BS):
                        v = (it * 2 + s) * BS + b
                        pe.wait_ge(weighted_ready, v + 2 * BS + 1)
                        pe.wait_ge(onehot_ready, v + 1)
                        pe.wait_ge(added, v + 1)
                        nc.tensor.matmul(ps_sum[b % 4][:, 0:ROW], onehot[:, b % 4, :], weighted[:, b % 4, :],
                                         start=True, stop=True).then_inc(summed, 1)

        @block.vector
        def _(dve):
            nc.vector.memset(k.acc[:, :, :], 0.0).then_inc(added, 4)
            dve.sem_inc(weighted_ready, 2 * BS)
            dve.sem_inc(summed, 4)
            with dve.Fori(0, NBLK // 2) as it:
                for s in range(2):
                    nts = node_tiles(dve, k, it * 2 + s)
                    dve.wait_ge(rows_in[s], (it + 1) * (16 * BS))
                    for b in range(BS + 2):
                        v = (it * 2 + s) * BS + b
                        if b < BS:
                            dve.wait_ge(summed, v + 1)
                            nc.vector.tensor_tensor(heads(weighted[:, b % 4, :], HW), heads(rows[s][:, b, :], HW),
                                                    k.alpha[:, bass.ds(v, 1), :].rearrange("p a h -> p h a").to_broadcast([P, H, HW]),
                                                    ALU.mult).then_inc(weighted_ready, 1)
                        if b >= 2:
                            tile = bass.ds(nts[b - 2], 1)
                            dve.wait_ge(summed, v + 3)
                            dve.wait_ge(added, v + 2)
                            nc.vector.tensor_tensor(k.acc[:, tile, :], k.acc[:, tile, :],
                                                    ps_sum[(b - 2) % 4][:, 0:ROW], ALU.add).then_inc(added, 1)


def linear_attention(nc, k):
    with ExitStack() as ctx:
        sb, ps, sem = allocators(nc, ctx)
        q_max = sb("q_max", [P, NT * MH])
        q_sum = sb("q_sum", [P, NT * MH])
        beyond = sb("beyond", [P, 1])
        k_max = sb("k_max", [P, MHID])
        k_top = sb("k_top", [P, 4])
        k_top_b = sb("k_top_b", [P, P])
        k_top_row = sb("k_top_row", [P, P])
        mem_k = sb("mem_k", [P, MEM])
        mem_v = sb("mem_v", [P, MEM])
        mem_kt = sb("mem_kt", [MEM, P])
        mem_vt = sb("mem_vt", [MEM, P + 1])
        same_head = sb("same_head", [P, P])
        w_out = sb("w_out_sb", [P, C])
        b_out = sb("b_out_sb", [1, C])
        ones_row = sb("ones_row", [1, P])
        g_out = sb("g_out_sb", [P, C])
        bias = sb("bias_sb", [P, C])
        exp_k = sb("exp_k", [P, 4, P])
        context = sb("context", [P, P])
        context_t = sb("context_t", [P, P])
        mixer = sb("mixer", [P, C])
        k_total = sb("k_total", [P, 1])
        q_norm = sb("q_norm", [P, G, P])
        q_t = sb("q_t", [P, 2, P])
        squares = sb("squares_dump", [P, 2, C])
        out_norm = sb("out_norm", [P, NT])
        xn = sb("xn_again", [P, G, C])
        x_bias = sb("x_bias", [P, G, C])
        base = sb("base_ring", [P, G, C])
        ps_a = ps("m_ps_a", [P, 512])
        ps_b = ps("m_ps_b", [P, 512])
        ps_c = ps("m_ps_c", [P, 512])
        ps_qt = [ps(f"ps_qt{i}", [P, 512]) for i in range(2)]
        ps_o = [ps(f"ps_o{i}", [P, 512]) for i in range(2)]
        small_in, masks_ready, q_shifted, q_exp, q_ready = sem("small_in"), sem("masks_ready"), sem("q_shifted"), sem("q_exp"), sem("q_ready")
        kmax_ready, kmax_turned, top_ready, top_spread, k_shifted = (
            sem("kmax_ready"), sem("kmax_turned"), sem("top_ready"), sem("top_spread"), sem("k_shifted"))
        mem_exp, mem_turned, mem_ready = sem("mem_exp"), sem("mem_turned"), sem("mem_ready")
        exp_ready, exp_used, context_done = sem("m_exp_ready"), sem("m_exp_used"), sem("context_done")
        ctx_ready, ctx_turned, ctx_t_ready, mixed, mixer_ready = (
            sem("ctx_ready"), sem("ctx_turned"), sem("ctx_t_ready"), sem("mixed"), sem("mixer_ready"))
        qn_ready, qn_turned, qt_ready, out_done, out_copied, squared = (
            sem("qn_ready"), sem("qn_turned"), sem("qt_ready"), sem("m_out_done"), sem("out_copied"), sem("m_squared"))
        roots, norms_ready, xn_ready, xb_ready, base_step, base_ready = (
            sem("roots"), sem("norms_ready"), sem("m_xn_ready"), sem("xb_ready"), sem("base_step"), sem("base_ready"))
        base_out = [sem(f"base_out{g}") for g in range(G)]
        dve_step, pool_step, pool_seen = sem("m_dve_step"), sem("m_pool_step"), sem("m_pool_seen")
        block = ctx.enter_context(nc.Block())
        q_heads = k.qkv[:, :, 0:MHID].rearrange("p t (h d) -> p t h d", d=MD)
        keys = k.qkv[:, :, MHID:2 * MHID]
        out_raw = k.qkv[:, :, 0:C]

        @block.sync
        def _(sp):
            sp.dma_start(mem_k[:, :], k.mem_kv[0].rearrange("h d m -> (h d) m")).then_inc(small_in, 16)
            sp.dma_start(mem_v[:, :], k.mem_kv[1].rearrange("h d m -> (h d) m")).then_inc(small_in, 16)
            sp.dma_start(w_out[:, :], k.w_out[:, :]).then_inc(small_in, 16)
            sp.dma_start(b_out[:, :], k.b_out.rearrange("(a c) -> a c", a=1)).then_inc(small_in, 16)
            sp.dma_start(g_out[:, :], k.g_out.rearrange("(a c) -> a c", a=1).to_broadcast([P, C])).then_inc(small_in, 16)
            sp.dma_start(bias[:, :], k.bias.rearrange("(a c) -> a c", a=1).to_broadcast([P, C])).then_inc(small_in, 16)
            with sp.Fori(0, NT // G) as it:
                for g in range(G):
                    sp.wait_ge(base_ready, it * G + (g + 1 + G))
                    sp.dma_start(k.base_rows[bass.ds((it * G + g) * P, P), :], base[:, g, :]).then_inc(base_out[g], 16)
            for g in range(G):
                sp.wait_ge(base_out[g], 16 * (NT // G + 1))

        @block.gpsimd
        def _(pool):
            link = chain(pool, pool_step)
            nc.gpsimd.memset(ones_row[:, :], 1.0).then_inc(masks_ready, 1)
            nc.gpsimd.memset(mem_vt[:, :], 1.0).then_inc(masks_ready, 1)
            nc.gpsimd.memset(k.qkv[:, :, QW:QW + 1], 1.0).then_inc(masks_ready, 1)
            link(nc.gpsimd.memset(same_head[:, :], 1.0))
            link(nc.gpsimd.affine_select(out=heads(same_head[:, :], MD), in_=heads(same_head[:, :], MD), compare_op=ALU.is_ge,
                                         fill=0.0, base=0, pattern=[[-MD, MH], [0, MD]], channel_multiplier=1))
            nc.gpsimd.affine_select(out=heads(same_head[:, :], MD), in_=heads(same_head[:, :], MD), compare_op=ALU.is_ge,
                                    fill=0.0, base=MD - 1, pattern=[[MD, MH], [0, MD]], channel_multiplier=-1).then_inc(masks_ready, 1)
            pool.wait_ge(small_in, 96)
            with pool.Fori(0, NT // G) as it:
                for g in range(G):
                    t = it * G + g
                    pool.wait_ge(base_ready, t + 1)
                    pool.sem_inc(pool_seen, 1)
                    nc.gpsimd.tensor_tensor(x_bias[:, g, :], k.x_res[:, bass.ds(t, 1), :], bias[:, :], ALU.add).then_inc(xb_ready, 1)

        @block.vector
        def _(dve):
            link = chain(dve, dve_step)
            link(nc.vector.tensor_reduce(q_max[:, :], q_heads, AX.X, ALU.max))
            nc.vector.tensor_tensor(q_heads, q_heads, q_max[:, :].rearrange("p (t h) -> p t h", h=MH).unsqueeze(3)
                                    .to_broadcast([P, NT, MH, MD]), ALU.subtract).then_inc(q_shifted, 1)
            link(nc.vector.tensor_scalar(beyond[:, :], k.iota_col[:, :], float(NLAST), -BIG, ALU.is_ge, ALU.mult))
            link(nc.vector.tensor_scalar(keys[:, NT - 1, :], keys[:, NT - 1, :], beyond[:, 0:1], None, ALU.add))
            nc.vector.tensor_reduce(k_max[:, :], keys.rearrange("p t c -> p c t"), AX.X, ALU.max).then_inc(kmax_ready, 1)
            dve.wait_ge(small_in, 96)
            link(nc.vector.tensor_reduce(k_top[:, 0:1], mem_k[:, :], AX.X, ALU.max))
            dve.wait_ge(kmax_turned, 1)
            link(nc.vector.tensor_reduce(k_top[:, 1:2], ps_a[:, 0:P], AX.X, ALU.max))
            link(nc.vector.tensor_tensor(k_top[:, 2:3], k_top[:, 0:1], k_top[:, 1:2], ALU.max))
            link(nc.vector.memset(k_top_b[:, :], 0.0))
            link(nc.vector.tensor_scalar(k_top_b[:, :], k_top_b[:, :], k_top[:, 2:3], None, ALU.add))
            nc.vector.tensor_scalar(k_top[:, 3:4], k_top[:, 2:3], -1.0, None, ALU.mult).then_inc(top_ready, 1)
            dve.wait_ge(top_spread, 1)
            link(nc.vector.tensor_copy(k_top_row[:, :], ps_b[:, 0:P]))
            nc.vector.tensor_tensor(keys, keys, k_top_row[:, :].unsqueeze(1).to_broadcast([P, NT, P]), ALU.subtract).then_inc(k_shifted, 1)
            dve.wait_ge(q_exp, 1)
            link(nc.vector.tensor_reduce(q_sum[:, :], q_heads, AX.X, ALU.add))
            link(nc.vector.reciprocal(q_sum[:, :], q_sum[:, :]))
            dve.wait_ge(mem_turned, 1)
            dve.wait_ge(masks_ready, 4)
            nc.vector.tensor_copy(mem_kt[:, :], ps_a[0:MEM, P:2 * P])
            nc.vector.tensor_copy(mem_vt[:, 0:P], ps_a[0:MEM, 2 * P:3 * P]).then_inc(mem_ready, 1)
            dve.wait_ge(context_done, 1)
            link(nc.vector.reciprocal(k_total[:, :], ps_c[:, P:P + 1]))
            link(nc.vector.tensor_scalar(k_total[:, :], k_total[:, :], float(MD) ** -0.5, None, ALU.mult))
            nc.vector.scalar_tensor_tensor(context[:, :], ps_c[:, 0:P], k_total[:, 0:1], same_head[:, :], ALU.mult, ALU.mult).then_inc(ctx_ready, 1)
            dve.wait_ge(ctx_turned, 1)
            nc.vector.tensor_copy(context_t[:, :], ps_b[:, P:2 * P]).then_inc(ctx_t_ready, 1)
            dve.wait_ge(mixed, 1)
            nc.vector.tensor_copy(mixer[:, :], ps_a[:, 0:C]).then_inc(mixer_ready, 1)
            dve.sem_inc(qn_turned, G)
            with dve.Fori(0, NT // G) as it:
                for g in range(G):
                    t = it * G + g
                    dve.wait_ge(qn_turned, t + 1)
                    nc.vector.tensor_tensor(q_norm[:, g, :].rearrange("p (a h d) -> p a h d", a=1, d=MD), q_heads[:, bass.ds(t, 1)],
                                            q_sum[:, bass.ds(t * MH, MH)].rearrange("p (a h) -> p a h", a=1).unsqueeze(3)
                                            .to_broadcast([P, 1, MH, MD]), ALU.mult).then_inc(qn_ready, 1)
            dve.wait_ge(roots, 1)
            link(nc.vector.tensor_scalar(out_norm[:, :], out_norm[:, :], 1e-12, 1.0 / 16.0, ALU.max, ALU.mult))
            link(nc.vector.reciprocal(out_norm[:, :], out_norm[:, :]))
            dve.sem_inc(base_ready, G)
            for g in range(G):
                dve.sem_inc(base_out[g], 16)
            with dve.Fori(0, NT // G) as it:
                for g in range(G):
                    t = it * G + g
                    dve.wait_ge(base_out[g], it * 16 + 16)
                    nc.vector.scalar_tensor_tensor(base[:, g, :], out_raw[:, bass.ds(t, 1), :], out_norm[:, bass.ds(t, 1)],
                                                   g_out[:, :], ALU.mult, ALU.mult).then_inc(base_step, 1)
                    dve.wait_ge(xn_ready, t + 1)
                    dve.wait_ge(base_step, t * 2 + 1)
                    nc.vector.tensor_tensor(base[:, g, :], base[:, g, :], xn[:, g, :], ALU.add).then_inc(base_step, 1)
                    dve.wait_ge(xb_ready, t + 1)
                    dve.wait_ge(base_step, t * 2 + 2)
                    nc.vector.tensor_tensor(base[:, g, :], base[:, g, :], x_bias[:, g, :], ALU.add).then_inc(base_ready, 1)

        @block.scalar
        def _(act):
            act.sem_inc(exp_used, 4)
            act.sem_inc(out_copied, 2)
            act.sem_inc(squared, 2)
            act.wait_ge(q_shifted, 1)
            nc.scalar.activation(k.qkv[:, :, 0:MHID], k.qkv[:, :, 0:MHID], ACT.Exp).then_inc(q_exp, 1)
            act.wait_ge(top_ready, 1)
            nc.scalar.activation(mem_k[:, :], mem_k[:, :], ACT.Exp, bias=k_top[:, 3:4]).then_inc(mem_exp, 1)
            act.wait_ge(k_shifted, 1)
            nc.scalar.activation(exp_k[:, 0, :], keys[:, 0, :], ACT.Exp).then_inc(exp_ready, 1)
            with act.Fori(0, (NT - 1) // 4) as it:
                for g in range(4):
                    act.wait_ge(exp_used, it * 4 + (g + 2))
                    nc.scalar.activation(exp_k[:, (g + 1) % 4, :], keys[:, bass.ds(it * 4 + (g + 1), 1), :], ACT.Exp).then_inc(exp_ready, 1)
            with act.Fori(0, NT // G) as it:
                for g in range(G + 1):
                    if g < G:
                        act.wait_ge(qn_turned, it * G + (g + 1 + G))
                        nc.scalar.copy(q_t[:, g % 2, :], ps_qt[g % 2][:, 0:P]).then_inc(qt_ready, 1)
                    if g >= 1:
                        b = g - 1
                        t = it * G + b
                        act.wait_ge(out_done, t + 1)
                        nc.scalar.copy(out_raw[:, bass.ds(t, 1), :], ps_o[b % 2][:, 0:C]).then_inc(out_copied, 1)
                        act.wait_ge(squared, t + (2 if b else 2))
                        nc.scalar.activation(squares[:, b % 2, :], ps_o[b % 2][:, 0:C], ACT.Square,
                                             accum_out=out_norm[:, bass.ds(t, 1)]).then_inc(squared, 1)
            act.wait_ge(squared, NT + 2)
            nc.scalar.activation(out_norm[:, :], out_norm[:, :], ACT.Sqrt).then_inc(roots, 1)
            with act.Fori(0, NT // G) as it:
                for g in range(G):
                    t = it * G + g
                    act.wait_ge(base_ready, t + 1)
                    nc.scalar.activation(xn[:, g, :], k.x_res[:, bass.ds(t, 1), :], ACT.Identity, scale=k.rstd[:, bass.ds(t, 1)],
                                         bias=k.shift[:, bass.ds(t, 1)]).then_inc(xn_ready, 1)

        @block.tensor
        def _(pe):
            pe.wait_ge(kmax_ready, 1)
            nc.tensor.transpose(ps_a[:, 0:P], k_max[:, :], k.ident[:, :]).then_inc(kmax_turned, 1)
            pe.wait_ge(top_ready, 1)
            nc.tensor.matmul(ps_b[:, 0:P], k_top_b[:, :], k.ident[:, :], start=True, stop=True).then_inc(top_spread, 1)
            pe.wait_ge(mem_exp, 1)
            nc.tensor.transpose(ps_a[0:MEM, P:2 * P], mem_k[:, :], k.ident[:, :])
            nc.tensor.transpose(ps_a[0:MEM, 2 * P:3 * P], mem_v[:, :], k.ident[:, :]).then_inc(mem_turned, 1)
            pe.wait_ge(masks_ready, 4)
            pe.wait_ge(exp_ready, 1)
            nc.tensor.matmul(ps_c[:, 0:P + 1], exp_k[:, 0, :], k.qkv[:, 0, 2 * MHID:QW + 1], start=True, stop=False).then_inc(exp_used, 1)
            with pe.Fori(0, (NT - 1) // 4) as it:
                for g in range(4):
                    pe.wait_ge(exp_ready, it * 4 + (g + 2))
                    nc.tensor.matmul(ps_c[:, 0:P + 1], exp_k[:, (g + 1) % 4, :], k.qkv[:, bass.ds(it * 4 + (g + 1), 1), 2 * MHID:QW + 1],
                                     start=False, stop=False).then_inc(exp_used, 1)
            pe.wait_ge(mem_ready, 1)
            nc.tensor.matmul(ps_c[:, 0:P + 1], mem_kt[:, :], mem_vt[:, :], start=False, stop=True).then_inc(context_done, 1)
            pe.wait_ge(ctx_ready, 1)
            nc.tensor.transpose(ps_b[:, P:2 * P], context[:, :], k.ident[:, :]).then_inc(ctx_turned, 1)
            pe.wait_ge(ctx_t_ready, 1)
            nc.tensor.matmul(ps_a[:, 0:C], context_t[:, :], w_out[:, :], start=True, stop=True).then_inc(mixed, 1)
            pe.wait_ge(mixer_ready, 1)
            with pe.Fori(0, NT // G) as it:
                for g in range(G + 1):
                    if g < G:
                        pe.wait_ge(qn_ready, it * G + (g + 1))
                        if g >= 2:
                            pe.wait_ge(qt_ready, it * G + (g - 1))
                        nc.tensor.transpose(ps_qt[g % 2][:, 0:P], q_norm[:, g, :], k.ident[:, :]).then_inc(qn_turned, 1)
                    if g >= 1:
                        b = g - 1
                        t = it * G + b
                        back = 2 if b else 1
                        pe.wait_ge(qt_ready, t + 1)
                        pe.wait_ge(squared, t + (3 - back))
                        pe.wait_ge(out_copied, t + (3 - back))
                        nc.tensor.matmul(ps_o[b % 2][:, 0:C], q_t[:, b % 2, :], mixer[:, :], start=True, stop=False)
                        nc.tensor.matmul(ps_o[b % 2][:, 0:C], ones_row[:, :], b_out[:, :], start=False, stop=True).then_inc(out_done, 1)


def gate_and_dispatch(nc, k):
    with ExitStack() as ctx:
        sb, ps, sem = allocators(nc, ctx)
        x1 = sb("x1", [P, NT, C])
        den = sb("den", [P, NT * H])
        stats = sb("stats2", [P, NT, 6])
        mv = sb("mv2", [P, NT, 2])
        std = sb("std2", [P, NT])
        rstd = sb("rstd2", [P, NT])
        shift = sb("shift2", [P, NT])
        wg_in = sb("wg_in", [NE, C])
        wg_t = sb("wg_t", [P, 2, NE])
        bg_in = sb("bg_in", [1, NE])
        ones = sb("ones_sq", [P, P])
        before = sb("before", [P, P])
        y = sb("y", [P, G, C])
        y_t = sb("y_t", [P, 2, 2, P])
        score = sb("score", [P, NT, NE])
        score2 = sb("score2", [P, NT, NE])
        expert_i = sb("expert_i", [P, NT, NE], I32)
        expert_no = sb("expert_no", [P, NT, NE])
        cand = sb("cand", [P, NT, NE])
        first = sb("first", [P, NT, NE])
        second = sb("second", [P, NT, NE])
        both = sb("both", [P, NT, NE])
        top = sb("top", [P, 2, NT])
        which = sb("which", [P, NT])
        gap = sb("gap", [P, NT])
        totals = sb("totals", [P, NT, NE])
        upto = sb("upto", [P, NT, NE])
        place = sb("place", [P, NT, NE])
        count_i = sb("count_i", [P, NE], I32)
        padded = sb("padded_count", [P, NE])
        ends = sb("ends", [P, NE])
        starts = sb("starts", [P, NE])
        block_i = sb("block_i", [P, NB, NE], I32)
        block_no = sb("block_no", [P, NB, NE])
        expert_f = sb("expert_f", [P, NB])
        place_f = sb("place_f", [P, 2, NT])
        place_idx = [sb(f"place_idx{g}", [P, 2], U32) for g in range(G)]
        ps_w = ps("g_ps_w", [P, 512])
        ps_t = [ps(f"g_ps_t{i}", [P, 512]) for i in range(2)]
        ps_s = [ps(f"g_ps_s{i}", [P, 512]) for i in range(2)]
        ps_before = ps("ps_before", [P, 512])
        ps_total = ps("ps_total", [P, 512])
        base_in, w_in, consts_ready, dve_step, pool_step = sem("base_in"), sem("g_w_in"), sem("g_consts"), sem("g_dve_step"), sem("g_pool_step")
        x1_ready, x1_out, stat_steps, moments_ready, std_ready, rstd_ready = (
            sem("x1_ready"), sem("x1_out"), sem("g_stat_steps"), sem("g_moments"), sem("g_std"), sem("g_rstd"))
        wg_turned, wg_ready, y_ready, y_turned, yt_ready, scored, score_copied = (
            sem("wg_turned"), sem("wg_ready"), sem("y_ready"), sem("y_turned"), sem("yt_ready"), sem("scored"), sem("score_copied"))
        gap_ready, gap_exp, picked, counted, places_ready, row_ready = (
            sem("gap_ready"), sem("gap_exp"), sem("picked"), sem("counted"), sem("places_ready"), sem("row_ready"))
        y2_ready, idx_ready, pool_seen = sem("y2_ready"), sem("g_idx_ready"), sem("g_pool_seen")
        sent = [sem(f"sent{g}") for g in range(G)]
        block = ctx.enter_context(nc.Block())
        sums = k.acc[:, :, :].rearrange("p t (h w) -> p (t h) w", w=HW)

        @block.sync
        def _(sp):
            for t in range(0, NT, G):
                sp.dma_start(x1[:, t:t + G, :], k.base_rows[t * P:(t + G) * P, :].rearrange("(t p) c -> p t c", p=P)).then_inc(base_in, 16)
            sp.dma_start(wg_in[:, :], k.Wg[:, :]).then_inc(w_in, 16)
            sp.dma_start(bg_in[:, :], k.bg.rearrange("(a e) -> a e", a=1)).then_inc(w_in, 16)
            sp.wait_ge(x1_ready, 1)
            for t in range(0, NT, G):
                sp.dma_start(k.x1_rows[t * P:(t + G) * P, :].rearrange("(t p) c -> p t c", p=P), x1[:, t:t + G, :]).then_inc(x1_out, 16)
            sp.wait_ge(x1_out, 16 * (NT // G))

        @block.gpsimd
        def _(pool):
            link = chain(pool, pool_step)
            nc.gpsimd.memset(ones[:, :], 1.0).then_inc(consts_ready, 1)
            link(nc.gpsimd.memset(before[:, :], 1.0))
            nc.gpsimd.affine_select(out=before[:, :], in_=before[:, :], compare_op=ALU.is_gt, fill=0.0, base=0,
                                    pattern=[[1, P]], channel_multiplier=-1).then_inc(consts_ready, 1)
            link(nc.gpsimd.iota(expert_i[:, :, :], [[0, NT], [1, NE]], 0, 0))
            nc.gpsimd.tensor_copy(expert_no[:, :, :], expert_i[:, :, :]).then_inc(consts_ready, 1)
            link(nc.gpsimd.iota(block_i[:, :, :], [[1, NB], [0, NE]], 0, 0))
            nc.gpsimd.tensor_copy(block_no[:, :, :], block_i[:, :, :]).then_inc(consts_ready, 1)
            pool.wait_ge(places_ready, 1)

            def dispatch(it, g):
                t = it * G + g
                nc.gpsimd.tensor_copy(place_idx[g][:, :], k.places[:, :, bass.ds(t, 1)].rearrange("p a t -> p (a t)")).then_inc(idx_ready, 1)
                pool.wait_ge(idx_ready, t + 1)
                pool.wait_ge(y2_ready, t + 1)
                pool.sem_inc(pool_seen, 1)
                for a in range(2):
                    pool.indirect_dma_start(k.list_rows[:, :], bass.IndirectOffsetOnAxis(ap=place_idx[g][:, a:a + 1], axis=0),
                                            y[:, g, :], None).then_inc(sent[g], 16)

            for g in range(G):
                dispatch(0, g)
            with pool.Fori(1, NT // G) as it:
                for g in range(G):
                    pool.wait_ge(sent[g], it * 32)
                    pool.sem_inc(pool_seen, 1)
                    dispatch(it, g)
            for g in range(G):
                pool.wait_ge(sent[g], 32 * (NT // G))

        @block.vector
        def _(dve):
            link = chain(dve, dve_step)
            link(nc.vector.tensor_scalar(den[:, :], sums[:, :, D], 1e-10, None, ALU.max))
            link(nc.vector.reciprocal(den[:, :], den[:, :]))
            link(nc.vector.tensor_tensor(sums[:, :, 0:D], sums[:, :, 0:D], den[:, :].unsqueeze(2).to_broadcast([P, NT * H, D]), ALU.mult))
            dve.wait_ge(base_in, 16 * (NT // G))
            x1_heads = x1[:, :, :].rearrange("p t (h d) -> p (t h) d", d=D)
            link(nc.vector.tensor_tensor(x1_heads, x1_heads, sums[:, :, 0:D], ALU.add))
            dve.sem_inc(x1_ready, 1)
            with dve.Fori(0, NT) as t:
                nc.vector.bn_stats(stats[:, bass.ds(t, 1), :], x1[:, bass.ds(t, 1), :]).then_inc(stat_steps, 1)
            dve.wait_ge(stat_steps, NT)
            moments(nc, link, stats, mv, moments_ready)
            dve.wait_ge(moments_ready, 1)
            dve.wait_ge(std_ready, 1)
            link(nc.vector.reciprocal(rstd[:, :], std[:, :]))
            nc.vector.scalar_tensor_tensor(shift[:, :], mv[:, :, 0], -1.0, rstd[:, :], ALU.mult, ALU.mult).then_inc(rstd_ready, 1)
            dve.wait_ge(wg_turned, 1)
            nc.vector.tensor_copy(wg_t[:, :, :], ps_w[:, 0:2 * NE].rearrange("p (a e) -> p a e", a=2)).then_inc(wg_ready, 1)
            dve.sem_inc(score_copied, 2)
            with dve.Fori(0, NT // G) as it:
                for g in range(G):
                    t = it * G + g
                    dve.wait_ge(scored, t + 1)
                    nc.vector.tensor_copy(score[:, bass.ds(t, 1), :], ps_s[g % 2][:, 0:NE]).then_inc(score_copied, 1)
            dve.wait_ge(score_copied, NT + 2)
            dve.wait_ge(consts_ready, 4)

            def across(ap):
                return ap.unsqueeze(2).to_broadcast([P, NT, NE])

            for n, (s, hot) in enumerate(((score, first), (score2, second))):
                link(nc.vector.tensor_reduce(top[:, n, :], s[:, :, :], AX.X, ALU.max))
                link(nc.vector.tensor_tensor(cand[:, :, :], s[:, :, :], across(top[:, n, :]), ALU.is_equal))
                link(nc.vector.tensor_scalar(cand[:, :, :], cand[:, :, :], -100.0, None, ALU.mult))
                link(nc.vector.tensor_tensor(cand[:, :, :], cand[:, :, :], expert_no[:, :, :], ALU.add))
                link(nc.vector.tensor_reduce(which[:, :], cand[:, :, :], AX.X, ALU.min))
                link(nc.vector.tensor_scalar(which[:, :], which[:, :], 100.0, None, ALU.add))
                link(nc.vector.tensor_tensor(hot[:, :, :], expert_no[:, :, :], across(which[:, :]), ALU.is_equal))
                if n == 0:
                    link(nc.vector.tensor_scalar(cand[:, :, :], hot[:, :, :], -BIG, None, ALU.mult))
                    link(nc.vector.tensor_tensor(score2[:, :, :], score[:, :, :], cand[:, :, :], ALU.add))
            nc.vector.tensor_tensor(gap[:, :], top[:, 1, :], top[:, 0, :], ALU.subtract).then_inc(gap_ready, 1)
            nc.vector.tensor_tensor(both[:, :, :], first[:, :, :], second[:, :, :], ALU.add).then_inc(picked, 1)
            dve.wait_ge(gap_exp, 1)
            link(nc.vector.tensor_scalar(k.weights[:, 0, :], gap[:, :], 1.0, None, ALU.add))
            link(nc.vector.reciprocal(k.weights[:, 0, :], k.weights[:, 0, :]))
            link(nc.vector.tensor_tensor(k.weights[:, 1, :], k.weights[:, 0, :], gap[:, :], ALU.mult))
            dve.wait_ge(counted, 1)
            link(nc.vector.tensor_copy(totals[:, :, :], ps_total[:, 0:NT * NE].rearrange("p (t e) -> p t e", e=NE)))
            for e in range(NE):
                link(nc.vector.tensor_tensor_scan(upto[:, :, e], ones[:, 0:NT], totals[:, :, e], 0.0, ALU.mult, ALU.add))
            link(nc.vector.tensor_scalar(count_i[:, :], upto[:, NT - 1, :], float(P - 1), None, ALU.add))
            link(nc.vector.tensor_scalar(count_i[:, :], count_i[:, :], 7, None, ALU.arith_shift_right))
            link(nc.vector.tensor_copy(padded[:, :], count_i[:, :]))
            link(nc.vector.tensor_tensor_scan(ends[:, :], ones[:, 0:NE], padded[:, :], 0.0, ALU.mult, ALU.add))
            link(nc.vector.tensor_tensor(starts[:, :], ends[:, :], padded[:, :], ALU.subtract))
            link(nc.vector.tensor_scalar(starts[:, :], starts[:, :], float(P), None, ALU.mult))
            link(nc.vector.tensor_tensor(upto[:, :, :], upto[:, :, :], totals[:, :, :], ALU.subtract))
            link(nc.vector.tensor_tensor(upto[:, :, :], upto[:, :, :], starts[:, :].unsqueeze(1).to_broadcast([P, NT, NE]), ALU.add))
            link(nc.vector.tensor_tensor(upto[:, :, :], upto[:, :, :], ps_before[:, 0:NT * NE].rearrange("p (t e) -> p t e", e=NE), ALU.add))
            for n, hot in enumerate((first, second)):
                link(nc.vector.tensor_tensor(place[:, :, :], upto[:, :, :], hot[:, :, :], ALU.mult))
                link(nc.vector.tensor_reduce(place_f[:, n, :], place[:, :, :], AX.X, ALU.add))
            nc.vector.tensor_copy(k.places[:, :, :], place_f[:, :, :]).then_inc(places_ready, 1)
            link(nc.vector.tensor_tensor(block_no[:, :, :], block_no[:, :, :], ends[:, :].unsqueeze(1).to_broadcast([P, NB, NE]), ALU.is_ge))
            link(nc.vector.tensor_reduce(expert_f[:, :], block_no[:, :, :], AX.X, ALU.add))
            link(nc.vector.tensor_scalar(expert_f[:, :], expert_f[:, :], float(NE - 1), None, ALU.min))
            link(nc.vector.tensor_copy(k.expert_row[:, :], expert_f[0:1, :]))

        @block.scalar
        def _(act):
            act.wait_ge(moments_ready, 1)
            nc.scalar.activation(std[:, :], mv[:, :, 1], ACT.Sqrt, bias=k.eps[:, 0:1]).then_inc(std_ready, 1)
            act.wait_ge(rstd_ready, 1)
            act.sem_inc(y_turned, G)
            with act.Fori(0, NT // G) as it:
                for g in range(G):
                    t = it * G + g
                    act.wait_ge(y_turned, t + 1)
                    nc.scalar.activation(y[:, g, :], x1[:, bass.ds(t, 1), :], ACT.Identity, scale=rstd[:, bass.ds(t, 1)],
                                         bias=shift[:, bass.ds(t, 1)]).then_inc(y_ready, 1)
                    act.wait_ge(y_turned, t + (1 + G))
                    nc.scalar.copy(y_t[:, g % 2].rearrange("p a n -> p (a n)"), ps_t[g % 2][:, 0:C]).then_inc(yt_ready, 1)
            act.wait_ge(gap_ready, 1)
            nc.scalar.activation(gap[:, :], gap[:, :], ACT.Exp).then_inc(gap_exp, 1)
            act.wait_ge(y_turned, NT + G)

            def normed(it, g):
                t = it * G + g
                nc.scalar.activation(y[:, g, :], x1[:, bass.ds(t, 1), :], ACT.Identity, scale=rstd[:, bass.ds(t, 1)],
                                     bias=shift[:, bass.ds(t, 1)]).then_inc(y2_ready, 1)

            for g in range(G):
                normed(0, g)
            with act.Fori(1, NT // G) as it:
                for g in range(G):
                    act.wait_ge(sent[g], it * 32)
                    normed(it, g)

        @block.tensor
        def _(pe):
            pe.wait_ge(w_in, 32)
            for a in range(2):
                last = nc.tensor.transpose(ps_w[:, NE * a:NE * (a + 1)], wg_in[:, a * P:(a + 1) * P], k.ident[0:NE, 0:NE])
            last.then_inc(wg_turned, 1)
            pe.wait_ge(wg_ready, 1)
            pe.wait_ge(consts_ready, 2)
            with pe.Fori(0, NT // G) as it:
                for g in range(G + 1):
                    if g < G:
                        pe.wait_ge(y_ready, it * G + (g + 1))
                        if g >= 2:
                            pe.wait_ge(yt_ready, it * G + (g - 1))
                        for a in range(2):
                            last = nc.tensor.transpose(ps_t[g % 2][:, a * P:(a + 1) * P], y[:, g, a * P:(a + 1) * P], k.ident[:, :])
                        last.then_inc(y_turned, 1)
                    if g >= 1:
                        b = g - 1
                        t = it * G + b
                        pe.wait_ge(yt_ready, t + 1)
                        pe.wait_ge(score_copied, t + (1 if b else 2))
                        for a in range(2):
                            nc.tensor.matmul(ps_s[b % 2][:, 0:NE], y_t[:, b % 2, a, :], wg_t[:, a, :], start=a == 0, stop=False)
                        nc.tensor.matmul(ps_s[b % 2][:, 0:NE], ones[0:1, :], bg_in[:, :], start=False, stop=True).then_inc(scored, 1)
            pe.wait_ge(picked, 1)
            flat = both[:, :, :].rearrange("p t e -> p (t e)")
            nc.tensor.matmul(ps_before[:, 0:NT * NE], before[:, :], flat, start=True, stop=True)
            nc.tensor.matmul(ps_total[:, 0:NT * NE], ones[:, :], flat, start=True, stop=True).then_inc(counted, 1)


def expert_weights(nc, k):
    with ExitStack() as ctx:
        sb, ps, sem = allocators(nc, ctx)
        w1_in = [sb(f"w1_in{s}", [P, 8, C]) for s in range(2)]
        w2_in = [sb(f"w2_in{s}", [P, 2, HID]) for s in range(2)]
        b_in_sb = sb("b_in_sb", [BROWS, P])
        b_rest = sb("b_rest", [BROWS, P])
        b_parts = sb("b_parts", [BROWS, 3, P], BF16)
        ps_a = [ps(f"w_ps_a{i}", [P, 512]) for i in range(4)]
        ps_d = [ps(f"w_ps_d{i}", [P, 512]) for i in range(4)]
        w_in = [sem(f"ew_in{s}") for s in range(2)]
        turned_a, turned_d, copied_a, copied_d = sem("turned_a"), sem("turned_d"), sem("copied_a"), sem("copied_d")
        b_in, b_split, b_out, dve_step = sem("b_in"), sem("b_split"), sem("b_out"), sem("w_dve_step")
        block = ctx.enter_context(nc.Block())

        @block.sync
        def _(sp):
            sp.dma_start(b_in_sb[0:NE * HID // P, :], k.b1.rearrange("e (i p) -> (e i) p", p=P)).then_inc(b_in, 16)
            sp.dma_start(b_in_sb[NE * HID // P:BROWS, :], k.b2.rearrange("e (i p) -> (e i) p", p=P)).then_inc(b_in, 16)
            with sp.Fori(0, NE // 2) as it:
                for s in range(2):
                    e = it * 2 + s
                    sp.wait_ge(w_in[s], it * 32 + 1)
                    sp.wait_ge(turned_a, e * 4 + 4)
                    sp.wait_ge(turned_d, e * 4 + 4)
                    sp.dma_start(w1_in[s][:, :, :], k.W1[bass.ds(e, 1), :, :].rearrange("e (i p) c -> p (e i) c", p=P)).then_inc(w_in[s], 16)
                    sp.dma_start(w2_in[s][:, :, :], k.W2[bass.ds(e, 1), :, :].rearrange("e (i p) c -> p (e i) c", p=P)).then_inc(w_in[s], 16)
            sp.wait_ge(b_split, 1)
            sp.dma_start(k.bias_rows.rearrange("j (r p) -> r j p", p=P), b_parts[:, :, :]).then_inc(b_out, 16)
            sp.wait_ge(b_out, 16)
            sp.dma_start(k.biases[:, :], k.bias_rows[:, :]).then_inc(b_out, 16)
            sp.wait_ge(b_out, 32)

        @block.tensor
        def _(pe):
            with pe.Fori(0, NE // 2) as it:
                for s in range(2):
                    e = it * 2 + s
                    pe.wait_ge(w_in[s], it * 32 + 33)
                    for n in range(4):
                        pe.wait_ge(copied_a, e * 4 + (n + 1))
                        for i in range(4):
                            a, chunk = n // 2, (n % 2) * 4 + i
                            last = nc.tensor.transpose(ps_a[n][:, i * P:(i + 1) * P], w1_in[s][:, chunk, a * P:(a + 1) * P], k.ident[:, :])
                        last.then_inc(turned_a, 1)
                        pe.wait_ge(copied_d, e * 4 + (n + 1))
                        for i in range(4):
                            chunk, a = n * 2 + i // 2, i % 2
                            last = nc.tensor.transpose(ps_d[n][:, i * P:(i + 1) * P], w2_in[s][:, a, chunk * P:(chunk + 1) * P], k.ident[:, :])
                        last.then_inc(turned_d, 1)

        @block.scalar
        def _(act):
            act.sem_inc(w_in[0], 1)
            act.sem_inc(w_in[1], 1)
            act.sem_inc(turned_a, 8)
            act.sem_inc(copied_a, 4)
            with act.Fori(0, NE) as e:
                for n in range(4):
                    act.wait_ge(turned_a, e * 4 + (n + 9))
                    nc.scalar.copy(k.w1_t[:, bass.ds(e * 4 + n, 1), :], ps_a[n][:, :]).then_inc(copied_a, 1)

        @block.vector
        def _(dve):
            link = chain(dve, dve_step)
            dve.wait_ge(b_in, 32)
            link(nc.vector.tensor_copy(b_parts[:, 0, :], b_in_sb[:, :]))
            link(nc.vector.tensor_tensor(b_rest[:, :], b_in_sb[:, :], b_parts[:, 0, :], ALU.subtract))
            link(nc.vector.tensor_copy(b_parts[:, 1, :], b_rest[:, :]))
            nc.vector.tensor_tensor(b_parts[:, 2, :], b_rest[:, :], b_parts[:, 1, :], ALU.subtract).then_inc(b_split, 1)
            dve.sem_inc(turned_d, 8)
            dve.sem_inc(copied_d, 4)
            with dve.Fori(0, NE) as e:
                for n in range(4):
                    dve.wait_ge(turned_d, e * 4 + (n + 9))
                    nc.vector.tensor_copy(k.w2_t[:, bass.ds(e * 4 + n, 1), :], ps_d[n][:, :]).then_inc(copied_d, 1)


def experts(nc, k):
    with ExitStack() as ctx:
        sb, ps, sem = allocators(nc, ctx)
        rows = [sb(f"e_rows{s}", [P, C]) for s in range(2)]
        rows_t = [sb(f"e_rows_t{s}", [P, C]) for s in range(2)]
        hidden = sb("hidden", [P, HID])
        hidden_t = sb("hidden_t", [P, 8, P])
        out = [sb(f"e_out{s}", [P, C]) for s in range(2)]
        ones = sb("e_ones", [3, P], BF16)
        ps_x = ps("e_ps_x", [P, 512])
        ps_h = [ps(f"e_ps_h{i}", [P, 512]) for i in range(2)]
        ps_ht = [ps(f"e_ps_ht{i}", [P, 512]) for i in range(2)]
        ps_y = ps("e_ps_y", [P, 512])
        rows_in = [sem(f"e_rows_in{s}") for s in range(2)]
        out_sent = [sem(f"e_out_sent{s}") for s in range(2)]
        turned, xt_ready, h_done = sem("e_turned"), sem("e_xt_ready"), sem("e_h_done")
        relu_a, relu_d, ht_done, ht_a, ht_d, y_done, y_copied, set_up = (
            sem("relu_a"), sem("relu_d"), sem("ht_done"), sem("ht_a"), sem("ht_d"), sem("y_done"), sem("y_copied"), sem("e_set_up"))
        pool_seen = sem("e_pool_seen")
        block = ctx.enter_context(nc.Block())
        pairs = (NB - 2) // 2

        @block.sync
        def _(sp):
            for i in range(2):
                sp.dma_start(rows[i][:, :], k.list_rows[i * P:(i + 1) * P, :]).then_inc(rows_in[i], 16)
            with sp.Fori(0, pairs) as it:
                for s in range(2):
                    i = it * 2 + (2 + s)
                    sp.wait_ge(turned, i - 1)
                    sp.dma_start(rows[s][:, :], k.list_rows[bass.ds(i * P, P), :]).then_inc(rows_in[s], 16)

        @block.gpsimd
        def _(pool):
            with pool.Fori(0, pairs) as it:
                for s in range(2):
                    i = it * 2 + s
                    pool.wait_ge(y_copied, i + 2)
                    pool.sem_inc(pool_seen, 1)
                    pool.dma_start(k.expert_out[bass.ds(i * P, P), :], out[s][:, :]).then_inc(out_sent[s], 16)
            last = NB - 2
            pool.wait_ge(y_copied, last + 2)
            pool.dma_start(k.expert_out[last * P:(last + 1) * P, :], out[0][:, :]).then_inc(out_sent[0], 16)
            pool.wait_ge(out_sent[0], 16 * (pairs + 1))
            pool.wait_ge(out_sent[1], 16 * pairs)

        def turn(pe, s, i, n):
            pe.wait_ge(rows_in[s], n * 16)
            pe.wait_ge(xt_ready, i + 1)
            for a in range(2):
                last = nc.tensor.transpose(ps_x[:, a * P:(a + 1) * P], rows[s][:, a * P:(a + 1) * P], k.ident[:, :])
            last.then_inc(turned, 1)

        def up(pe, s, i, e):
            pe.wait_ge(xt_ready, i + 2)
            pe.wait_ge(relu_a, i + 1)
            pe.wait_ge(relu_d, i + 1)
            for n in range(2):
                nc.tensor.matmul(ps_h[n][:, :], ones[:, :], k.biases[:, bass.ds(e * HID + n * 512, 512)], start=True, stop=False)
                for a in range(2):
                    last = nc.tensor.matmul(ps_h[n][:, :], rows_t[s][:, a * P:(a + 1) * P],
                                            k.w1_t[:, bass.ds(e * 4 + (2 * a + n), 1), :], start=False, stop=a == 1)
                last.then_inc(h_done, 1)

        def turn_hidden(pe, i):
            for n in range(2):
                pe.wait_ge((relu_a, relu_d)[n], i + 2)
                pe.wait_ge((ht_a, ht_d)[n], i + 1)
                for m in range(4):
                    last = nc.tensor.transpose(ps_ht[n][:, m * P:(m + 1) * P], hidden[:, (4 * n + m) * P:(4 * n + m + 1) * P], k.ident[:, :])
                last.then_inc(ht_done, 1)

        def down(pe, i, e):
            pe.wait_ge(y_copied, i + 1)
            nc.tensor.matmul(ps_y[:, 0:C], ones[:, :], k.biases[:, bass.ds(e * C + NE * HID, C)], start=True, stop=False)
            for m in range(8):
                if m % 4 == 0:
                    pe.wait_ge((ht_a, ht_d)[m // 4], i + 2)
                last = nc.tensor.matmul(ps_y[:, 0:C], hidden_t[:, m, :],
                                        k.w2_t[:, bass.ds(e * 4 + m // 2, 1), (m % 2) * C:(m % 2 + 1) * C], start=False, stop=m == 7)
            last.then_inc(y_done, 1)

        @block.tensor
        def _(pe):
            pe.wait_ge(set_up, 1)
            turn(pe, 0, 0, 1)
            turn(pe, 1, 1, 1)
            e = pe.value_load(k.expert_row[0:1, 0:1], min_val=0, max_val=NE - 1)
            up(pe, 0, 0, e)
            turn_hidden(pe, 0)
            with pe.Fori(0, pairs) as it:
                for s in range(2):
                    i = it * 2 + (1 + s)
                    e = pe.value_load(k.expert_row[0:1, bass.ds(i, 1)], min_val=0, max_val=NE - 1)
                    before = pe.value_load(k.expert_row[0:1, bass.ds(i - 1, 1)], min_val=0, max_val=NE - 1)
                    turn(pe, s, i + 1, it + 2)
                    up(pe, (1 + s) % 2, i, e)
                    down(pe, i - 1, before)
                    turn_hidden(pe, i)
            e = pe.value_load(k.expert_row[0:1, NB - 2:NB - 1], min_val=0, max_val=NE - 1)
            down(pe, NB - 2, e)

        def rows_copy(act, s, i):
            act.wait_ge(turned, i + 1)
            act.wait_ge(h_done, 2 * i + 1)
            nc.scalar.copy(rows_t[s][:, :], ps_x[:, 0:C]).then_inc(xt_ready, 1)

        def out_copy(act, s, i, n):
            act.wait_ge(y_done, i + 1)
            if n is not None:
                act.wait_ge(out_sent[s], n * 16)
            nc.scalar.copy(out[s][:, :], ps_y[:, 0:C]).then_inc(y_copied, 1)

        def relu_first(act, i):
            act.wait_ge(h_done, 2 * i + 4)
            nc.scalar.activation(hidden[:, 0:512], ps_h[0][:, :], ACT.Relu).then_inc(relu_a, 1)

        def hidden_copy(act, i):
            act.wait_ge(ht_done, 2 * i + 1)
            nc.scalar.copy(hidden_t[:, 0:4, :].rearrange("p m n -> p (m n)"), ps_ht[0][:, :]).then_inc(ht_a, 1)

        @block.scalar
        def _(act):
            act.sem_inc(xt_ready, 1)
            act.sem_inc(relu_a, 1)
            act.sem_inc(relu_d, 1)
            act.sem_inc(ht_a, 1)
            act.sem_inc(ht_d, 1)
            act.sem_inc(y_copied, 1)
            act.sem_inc(h_done, 3)
            rows_copy(act, 0, 0)
            rows_copy(act, 1, 1)
            relu_first(act, 0)
            hidden_copy(act, 0)

            def turn_of_two(it, n):
                for s in range(2):
                    i = it * 2 + (1 + s)
                    rows_copy(act, s, i + 1)
                    relu_first(act, i)
                    out_copy(act, s, i - 1, n)
                    hidden_copy(act, i)

            turn_of_two(0, None)
            with act.Fori(1, pairs) as it:
                turn_of_two(it, it)
            out_copy(act, 0, NB - 2, pairs)

        @block.vector
        def _(dve):
            nc.vector.memset(ones[:, :], 1.0).then_inc(set_up, 1)

            def relu_second(i):
                dve.wait_ge(h_done, 2 * i + 5)
                nc.vector.tensor_scalar(hidden[:, 512:HID], ps_h[1][:, :], 0.0, None, ALU.max).then_inc(relu_d, 1)

            def hidden_copy_second(i):
                dve.wait_ge(ht_done, 2 * i + 2)
                nc.vector.tensor_copy(hidden_t[:, 4:8, :].rearrange("p m n -> p (m n)"), ps_ht[1][:, :]).then_inc(ht_d, 1)

            relu_second(0)
            hidden_copy_second(0)
            with dve.Fori(0, pairs) as it:
                for s in range(2):
                    i = it * 2 + (1 + s)
                    relu_second(i)
                    hidden_copy_second(i)


def combine(nc, k):
    with ExitStack() as ctx:
        sb, ps, sem = allocators(nc, ctx)
        x1 = sb("x1_again", [P, G, C])
        picked = sb("picked_rows", [P, G, 2, C])
        out = sb("out_ring", [P, G, C])
        place_idx = [sb(f"c_place_idx{g}", [P, 2], U32) for g in range(G)]
        x1_in = [sem(f"x1_in{g}") for g in range(G)]
        rows_in = [sem(f"c_rows_in{g}") for g in range(G)]
        out_sent = [sem(f"c_out_sent{g}") for g in range(G)]
        idx_ready, pool_seen, half, added = sem("c_idx_ready"), sem("c_pool_seen"), sem("c_half"), sem("c_added")
        block = ctx.enter_context(nc.Block())
        turns = NT // G - 1

        @block.sync
        def _(sp):
            def store(t, it, g, n):
                sp.wait_ge(added, t + (1 + G))
                rows = k.out[bass.ds(t * P, P), :] if n == P else k.out[t * P:t * P + n, :]
                sp.dma_start(rows, out[0:n, g, :]).then_inc(out_sent[g], 16)

            with sp.Fori(0, turns) as it:
                for g in range(G):
                    t = it * G + g
                    sp.wait_ge(added, t + 1)
                    sp.dma_start(x1[:, g, :], k.x1_rows[bass.ds(t * P, P), :]).then_inc(x1_in[g], 16)
                for g in range(G):
                    store(it * G + g, it, g, P)
            for g in range(G):
                t = turns * G + g
                sp.wait_ge(added, t + 1)
                sp.dma_start(x1[:, g, :], k.x1_rows[t * P:(t + 1) * P, :]).then_inc(x1_in[g], 16)
            for g in range(G):
                t = turns * G + g
                store(t, turns, g, P if t < NT - 1 else NLAST)
            for g in range(G):
                sp.wait_ge(out_sent[g], 16 * (NT // G + 1))

        @block.gpsimd
        def _(pool):
            with pool.Fori(0, NT // G) as it:
                for g in range(G):
                    t = it * G + g
                    pool.wait_ge(added, t + 1)
                    pool.sem_inc(pool_seen, 1)
                    nc.gpsimd.tensor_copy(place_idx[g][:, :], k.places[:, :, bass.ds(t, 1)].rearrange("p a t -> p (a t)")).then_inc(idx_ready, 1)
                    pool.wait_ge(idx_ready, t + 1)
                    pool.sem_inc(pool_seen, 1)
                    for a in range(2):
                        pool.indirect_dma_start(picked[:, g, a, :], None, k.expert_out[:, :],
                                                bass.IndirectOffsetOnAxis(ap=place_idx[g][:, a:a + 1], axis=0)).then_inc(rows_in[g], 16)

        @block.vector
        def _(dve):
            dve.sem_inc(added, G)
            for g in range(G):
                dve.sem_inc(out_sent[g], 16)
            with dve.Fori(0, NT // G) as it:
                for g in range(G):
                    t = it * G + g
                    dve.wait_ge(x1_in[g], it * 16 + 16)
                    dve.wait_ge(rows_in[g], it * 32 + 32)
                    dve.wait_ge(out_sent[g], it * 16 + 16)
                    nc.vector.scalar_tensor_tensor(x1[:, g, :], picked[:, g, 0, :], k.weights[:, 0, bass.ds(t, 1)], x1[:, g, :],
                                                   ALU.mult, ALU.add).then_inc(half, 1)
                    dve.wait_ge(half, t + 1)
                    nc.vector.scalar_tensor_tensor(out[:, g, :], picked[:, g, 1, :], k.weights[:, 1, bass.ds(t, 1)], x1[:, g, :],
                                                   ALU.mult, ALU.add).then_inc(added, 1)


def program(nc, k):
    with ExitStack() as ctx:
        sb, ps, sem = allocators(nc, ctx)
        dram = lambda name, shape, dt=F32: nc.dram_tensor(name, shape, dt, kind="Internal").ap()
        k.dst_rows = dram("dst_rows", [EROWS, P], I32)
        k.src_rows = dram("src_rows", [EROWS, P], I32)
        k.ea_rows = dram("ea_rows", [EROWS, 3 * P])
        k.nt_list = dram("nt_list", [VPAD], I32)
        k.local_rows = dram("local_rows", [VPAD, P], BF16)
        k.key_rows = dram("key_rows", [VPAD, P])
        k.ea_parts = dram("ea_part_rows", [9, VPAD, P], BF16)
        k.ew_rows = dram("ew_rows", [3, 3, ROW], BF16)
        k.eb_rows = dram("eb_rows", [3, ROW], BF16)
        k.h_rows = dram("h_rows", [NPAD, ROW])
        k.hd_parts = dram("hd_part_rows", [NPAD, 3 * ROW], BF16)
        k.chunk_stats = dram("chunk_stats", [P, 4])
        k.src_logits = dram("src_logits", [NPAD, H])
        k.base_rows = dram("base_rows", [NPAD, C])
        k.x1_rows = dram("x1_rows", [NPAD, C])
        k.bias_rows = dram("bias_rows", [3, BROWS * P], BF16)
        k.list_rows = dram("list_rows", [NB * P, C])
        k.expert_out = dram("expert_out", [(NB - 1) * P, C])

        k.ident = sb("ident", [P, P])
        k.zero = sb("zero", [P, 1])
        k.eps = sb("eps", [P, 1])
        k.iota_row = sb("iota_row", [P, P])
        k.iota_col = sb("iota_col", [P, 1])
        k.enc_w = sb("enc_w", [30, ROW], BF16)
        k.nt_words = sb("nt_words", [1, VPAD // 4], I32)
        k.places = sb("places", [P, 2, NT], U32)
        k.weights = sb("weights", [P, 2, NT])
        k.expert_row = sb("expert_row", [1, NB], I32)
        constants(nc, k)
        with ExitStack() as edges:
            k.local_col = edges.enter_context(nc.sbuf_tensor("local_col", [P, VPAD], F32))
            k.src_col = edges.enter_context(nc.sbuf_tensor("src_col", [P, VPAD], U32))
            edge_tables(nc, k)
            with ExitStack() as nodes:
                k.rstd = nodes.enter_context(nc.sbuf_tensor("rstd", [P, NT], F32))
                k.shift = nodes.enter_context(nc.sbuf_tensor("shift", [P, NT], F32))
                k.norm = nodes.enter_context(nc.sbuf_tensor("norm", [P, NT], F32))
                k.x_res = nodes.enter_context(nc.sbuf_tensor("x_res", [P, NT, C], F32))
                k.qkv = nodes.enter_context(nc.sbuf_tensor("qkv", [P, NT, QW + 1], F32))
                node_rows(nc, k)
                linear_attention(nc, k)
            k.alpha = edges.enter_context(nc.sbuf_tensor("alpha", [P, V, H], F32))
            edge_logits(nc, k)
            segment_softmax(nc, k)
            k.acc = edges.enter_context(nc.sbuf_tensor("acc", [P, NT, ROW], F32))
            aggregate(nc, k)
            gate_and_dispatch(nc, k)
        k.w1_t = sb("w1_t", [P, NE * 4, 512])
        k.w2_t = sb("w2_t", [P, NE * 4, 512])
        k.biases = sb("biases", [3, BROWS * P], BF16)
        expert_weights(nc, k)
        experts(nc, k)
        combine(nc, k)


_NAMES = {"x": "x", "src": "src", "dst": "dst", "edge_attr_3": "edge_attr", "L0_gnn_W": "W", "L0_gnn_a_src": "a_src",
          "L0_gnn_a_dst": "a_dst", "L0_gnn_edge_W": "edge_W", "L0_gnn_edge_b": "edge_b", "L0_gnn_bias": "bias",
          "L0_mix_w_qkv": "w_qkv", "L0_mix_mem_kv": "mem_kv", "L0_mix_w_out": "w_out", "L0_mix_b_out": "b_out",
          "L0_mix_g_out": "g_out", "L0_mix_g_pre": "g_pre", "L0_ffn_Wg": "Wg", "L0_ffn_bg": "bg", "L0_ffn_W1": "W1",
          "L0_ffn_b1": "b1", "L0_ffn_W2": "W2", "L0_ffn_b2": "b2"}


def kernel(**inputs):
    import numpy as np
    import concourse.bacc as bacc
    from concourse.bass_utils import run_bass_kernel_spmd as run

    nc = bacc.Bacc("TRN2", target_bir_lowering=False, num_devices=1)
    arrays, k = {}, Ctx()
    for name, short in _NAMES.items():
        a = np.ascontiguousarray(inputs[name])
        arrays["in_" + short] = a
        k.__dict__[short] = nc.dram_tensor("in_" + short, a.shape, mybir.dt.from_np(a.dtype), kind="ExternalInput").ap()
    k.out = nc.dram_tensor("out", (N, C), F32, kind="ExternalOutput").ap()
    program(nc, k)
    r = run(nc, [arrays], core_ids=[0])
    return r.results[0]["out"]
```

```python
from contextlib import ExitStack

import concourse.bass as bass
from concourse import mybir

F32 = mybir.dt.float32
BF16 = mybir.dt.bfloat16
I32 = mybir.dt.int32
U32 = mybir.dt.uint32
ALU = mybir.AluOpType
ACT = mybir.ActivationFunctionType
AX = mybir.AxisListType

P = 128
N, C = 6250, 256
E = 100000
H, D = 8, 32
HW = D + 1
ROW = H * HW
NT = -(-N // P)
NPAD = NT * P
NLAST = N - (NT - 1) * P
ETILES = -(-E // P)
ER = 7
EP = 112
EROWS = EP * ER
EFULL = E // (ER * P)
EREST = E - EFULL * ER * P
CH = 16
CT = -(-(ETILES + NT - 1) // CH)
V = CH * CT
VC = -(-V // P)
VPAD = VC * P
NOWHERE = 7000
BIG = 1e30
EPS = 1e-5
MH, MD, MEM = 4, 32, 4
MHID = MH * MD
QW = 3 * MHID
NE = 8
HID = 1024
BROWS = NE * (HID + C) // P
NB = (2 * NPAD + NE * (P - 1)) // P + 1
NW = C + 2 * H
BS = 8
NBLK = V // BS
SLOTS = 4
EARLY = 24
G = 7
R = 8
assert NBLK % SLOTS == 0 and EARLY % SLOTS == 0 and (NBLK + SLOTS) * BS <= VPAD
assert NT % G == 0 and NT % R == 1 and V % BS == 0 and ETILES + NT - 1 <= V and ETILES < EROWS


class Ctx:
    pass


def allocators(nc, ctx):
    def sb(name, shape, dt=F32):
        return ctx.enter_context(nc.sbuf_tensor(name, shape, dt))

    def ps(name, shape, dt=F32):
        return ctx.enter_context(nc.psum_tensor(name, shape, dt))

    used = []

    def sem(name):
        used.append(nc.alloc_semaphore(name))
        return used[-1]

    def give_back():
        if used:
            nc.clear_and_free_semaphores(used)
            nc.all_engine_barrier()

    ctx.callback(give_back)
    return sb, ps, sem


def chain(eng, sem):
    count = [0]

    def link(ins):
        count[0] += 1
        ins.then_inc(sem, 1)
        eng.wait_ge(sem, count[0])

    return link


def node_tiles(eng, k, j):
    words = [eng.value_load(k.nt_words[0:1, bass.ds(j * (BS // 4) + w, 1)]) for w in range(BS // 4)]
    return [((words[b // 4] >> (6 * (b % 4))) & 63).with_bounds(min_val=0, max_val=NT - 1) for b in range(BS)]


def heads(ap, width=D):
    return ap.rearrange("p (h d) -> p h d", d=width)


def moments(nc, link, stats, mv, ready):
    even, odd = stats[:, :, 1], stats[:, :, 4]
    link(nc.vector.tensor_tensor(mv[:, :, 0], even, odd, ALU.subtract))
    link(nc.vector.tensor_scalar(mv[:, :, 0], mv[:, :, 0], 0.5, None, ALU.mult))
    link(nc.vector.tensor_tensor(mv[:, :, 1], mv[:, :, 0], mv[:, :, 0], ALU.mult))
    link(nc.vector.tensor_tensor(mv[:, :, 0], stats[:, :, 2], stats[:, :, 5], ALU.add))
    link(nc.vector.scalar_tensor_tensor(mv[:, :, 1], mv[:, :, 0], 1.0 / C, mv[:, :, 1], ALU.mult, ALU.add))
    link(nc.vector.tensor_tensor(mv[:, :, 0], even, odd, ALU.add))
    nc.vector.tensor_scalar(mv[:, :, 0], mv[:, :, 0], 0.5, None, ALU.mult).then_inc(ready, 1)


def edge_tables(nc, k):
    with ExitStack() as ctx:
        sb, ps, sem = allocators(nc, ctx)
        dst_in = sb("dst_in", [EP, ER * P], I32)
        src_in = sb("src_in", [EP, ER * P], I32)
        ea_in = sb("ea_in", [EP, ER * P * 3])
        iota_i = sb("iota_i", [P, VPAD], I32)
        nt_row = sb("nt_row", [1, VPAD], I32)
        words_f = sb("words_f", [1, VPAD // 4])
        iota_v = sb("iota_v", [P, VPAD])
        iota_e = sb("iota_e", [P, ER])
        iota_s = sb("iota_s", [P, VC])
        last_tile = sb("last_tile", [EP, ER], I32)
        ends_at = sb("ends_at", [EP, ER])
        passed = sb("passed", [EP, VPAD])
        passed_b = sb("passed_b", [EP, VPAD], BF16)
        ones_b = sb("ones_b", [P, 1], BF16)
        et_raw = sb("et_raw", [P, VC])
        et_f = sb("et_f", [P, VC])
        et_u = sb("et_u", [P, VC], U32)
        nt_f = sb("nt_f", [P, VC])
        nt_i = sb("nt_i", [P, VC], I32)
        nt_base = sb("nt_base", [P, VC])
        dst_g = sb("dst_g", [P, VC, P], I32)
        src_g = sb("src_g", [P, VC, P], I32)
        ea_g = sb("ea_g", [P, VC, P * 3])
        local = sb("local", [P, VC, P])
        local_c = sb("local_c", [P, VC, P])
        local_b = sb("local_b", [P, VC, P], BF16)
        key = sb("key", [P, VC, P])
        src_f = sb("src_f", [P, VC, P])
        ea_rest = sb("ea_rest", [P, VC, 3, P])
        ea_parts = sb("ea_parts", [P, VC, 3, 3, P], BF16)
        ew_t = sb("ew_t", [3, C])
        ew_33 = sb("ew_33", [3, ROW])
        ew_rest = sb("ew_rest", [3, ROW])
        ew_parts = sb("ew_parts", [3, 3, ROW], BF16)
        eb_in = sb("eb_in", [1, C])
        eb_33 = sb("eb_33", [1, ROW])
        eb_rest = sb("eb_rest", [1, ROW])
        eb_parts = sb("eb_parts", [1, 3, ROW], BF16)
        ps_et = ps("ps_et", [P, 512])
        ps_local = ps("ps_local", [P, 2, 512])
        ps_src = ps("ps_src", [P, 2, 512])

        padded, edges_in, edge_w_in = sem("padded"), sem("edges_in"), sem("edge_w_in")
        tables_out, iotas = sem("tables_out"), sem("iotas")
        passed_ready, et_counted, et_ready = sem("passed_ready"), sem("et_counted"), sem("et_ready")
        gathered = [sem(f"gathered{i}") for i in range(3)]
        dve_step, pool_step = sem("et_dve_step"), sem("et_pool_step")
        nt_out, row_in, locals_ready, parts_ready = sem("nt_out"), sem("row_in"), sem("locals_ready"), sem("parts_ready")
        turned, cols_ready, vt_out, w_split, w_out, w_rows = (
            sem("turned"), sem("cols_ready"), sem("vt_out"), sem("w_split"), sem("w_out"), sem("w_rows"))
        block = ctx.enter_context(nc.Block())

        @block.sync
        def _(sp):
            with nc.allow_non_contiguous_dma("a small weight and a short list are read across"):
                sp.dma_start(ew_t[:, :], k.edge_W.rearrange("c f -> f c")).then_inc(edge_w_in, 16)
                sp.dma_start(eb_in[:, :], k.edge_b.rearrange("(a c) -> a c", a=1)).then_inc(edge_w_in, 16)
                sp.wait_ge(padded, 3)
                full = EFULL * ER * P
                for buf, src, w in ((dst_in, k.dst, 1), (src_in, k.src, 1),
                                    (ea_in, k.edge_attr.rearrange("e f -> (e f)"), 3)):
                    sp.dma_start(buf[0:EFULL, :], src[0:full * w].rearrange("(p n) -> p n", p=EFULL)).then_inc(edges_in, 16)
                    sp.dma_start(buf[EFULL:EFULL + 1, 0:EREST * w],
                                 src[full * w:E * w].rearrange("(a n) -> a n", a=1)).then_inc(edges_in, 16)
                sp.wait_ge(edges_in, 96)
                for buf, out in ((dst_in, k.dst_rows), (src_in, k.src_rows), (ea_in, k.ea_rows)):
                    sp.dma_start(out.rearrange("(p r) e -> p (r e)", r=ER), buf[:, :]).then_inc(tables_out, 16)
                sp.wait_ge(w_split, 2)
                sp.dma_start(k.ew_rows.rearrange("j f c -> f j c"), ew_parts[:, :, :]).then_inc(w_out, 16)
                sp.dma_start(k.eb_rows.rearrange("(a j) c -> a j c", a=1), eb_parts[:, :, :]).then_inc(w_out, 16)
                sp.wait_ge(w_out, 32)
                for j in range(3):
                    for f in range(3):
                        r = 9 * j + 3 * f
                        sp.dma_start(k.enc_w[r:r + 3, :], k.ew_rows[j, f:f + 1, :].to_broadcast([3, ROW])).then_inc(w_rows, 16)
                sp.dma_start(k.enc_w[27:30, :], k.eb_rows[:, :]).then_inc(w_rows, 16)
                sp.wait_ge(et_ready, 1)
                sp.dma_start(k.nt_list.rearrange("(c p) -> p c", p=P), nt_i[:, :]).then_inc(nt_out, 16)
                sp.wait_ge(nt_out, 16)
                sp.dma_start(nt_row[:, :], k.nt_list.rearrange("(a v) -> a v", a=1)).then_inc(row_in, 16)
                sp.wait_ge(locals_ready, 1)
                sp.dma_start(k.local_rows.rearrange("(c p) e -> p c e", p=P), local_b[:, :, :]).then_inc(vt_out, 16)
                sp.dma_start(k.key_rows.rearrange("(c p) e -> p c e", p=P), key[:, :, :]).then_inc(vt_out, 16)
                sp.wait_ge(parts_ready, 1)
                for c in range(VC):
                    sp.dma_start(k.ea_parts[:, c * P:(c + 1) * P, :].rearrange("r v e -> v r e"),
                                 ea_parts[:, c].rearrange("p f i e -> p (f i) e")).then_inc(vt_out, 16)
                sp.wait_ge(w_rows, 160)
                sp.wait_ge(row_in, 16)
                sp.wait_ge(vt_out, 16 * (2 + VC))

        @block.gpsimd
        def _(pool):
            link = chain(pool, pool_step)
            nc.gpsimd.memset(dst_in[:, :], NOWHERE).then_inc(padded, 1)
            nc.gpsimd.memset(src_in[:, :], 0).then_inc(padded, 1)
            nc.gpsimd.memset(ea_in[:, :], 0.0).then_inc(padded, 1)
            nc.gpsimd.memset(ones_b[:, :], 1.0).then_inc(iotas, 1)
            link(nc.gpsimd.iota(iota_i[:, :], [[1, VPAD]], 0, 0))
            nc.gpsimd.tensor_copy(iota_v[:, :], iota_i[:, :]).then_inc(iotas, 1)
            nc.gpsimd.tensor_copy(k.iota_row[:, :], iota_i[:, 0:P]).then_inc(iotas, 1)
            pool.wait_ge(iotas, 3)
            link(nc.gpsimd.iota(iota_i[:, 0:ER], [[1, ER]], 0, ER))
            nc.gpsimd.tensor_copy(iota_e[:, :], iota_i[:, 0:ER]).then_inc(iotas, 1)
            link(nc.gpsimd.iota(iota_i[:, P:P + VC], [[P, VC]], 0, 1))
            nc.gpsimd.tensor_copy(iota_s[:, :], iota_i[:, P:P + VC]).then_inc(iotas, 1)
            nc.gpsimd.tensor_copy(k.iota_col[:, :], iota_i[:, P:P + 1]).then_inc(iotas, 1)
            pool.wait_ge(et_ready, 1)
            pool.wait_ge(tables_out, 48)
            for n, (out, rows) in enumerate(((dst_g, k.dst_rows), (src_g, k.src_rows), (ea_g, k.ea_rows))):
                for c in range(VC):
                    pool.indirect_dma_start(out[:, c, :], None, rows[:, :],
                                            bass.IndirectOffsetOnAxis(ap=et_u[:, c:c + 1], axis=0)).then_inc(gathered[n], 16)

        @block.vector
        def _(dve):
            link = chain(dve, dve_step)
            link(nc.vector.memset(ew_33[:, :], 0.0))
            link(nc.vector.memset(eb_33[:, :], 1.0))
            dve.wait_ge(edge_w_in, 32)
            link(nc.vector.tensor_copy(heads(ew_33[:, :], HW)[:, :, 0:D], heads(ew_t[:, :])))
            link(nc.vector.tensor_copy(heads(eb_33[:, :], HW)[:, :, 0:D], heads(eb_in[:, :])))
            for full, rest, parts in ((ew_33, ew_rest, ew_parts), (eb_33, eb_rest, eb_parts)):
                link(nc.vector.tensor_copy(parts[:, 0, :], full[:, :]))
                link(nc.vector.tensor_tensor(rest[:, :], full[:, :], parts[:, 0, :], ALU.subtract))
                link(nc.vector.tensor_copy(parts[:, 1, :], rest[:, :]))
                nc.vector.tensor_tensor(parts[:, 2, :], rest[:, :], parts[:, 1, :], ALU.subtract).then_inc(w_split, 1)
            dve.wait_ge(edges_in, 96)
            dve.wait_ge(iotas, 6)
            link(nc.vector.tensor_scalar(last_tile[:, :], dst_in[:, :].rearrange("p (r e) -> p r e", r=ER)[:, :, P - 1],
                                         7, None, ALU.arith_shift_right))
            link(nc.vector.tensor_scalar(ends_at[:, :], last_tile[:, :], float(NT - 1), None, ALU.min))
            link(nc.vector.tensor_tensor(ends_at[:, :], ends_at[:, :], iota_e[0:EP, :], ALU.add))
            link(nc.vector.tensor_scalar(passed[:, :], iota_v[0:EP, :], ends_at[:, 0:1], None, ALU.is_gt))
            for r in range(1, ER):
                out = passed if r < ER - 1 else passed_b
                ins = nc.vector.scalar_tensor_tensor(out[:, :], iota_v[0:EP, :], ends_at[:, r:r + 1], passed[:, :],
                                                     ALU.is_gt, ALU.add)
                if r < ER - 1:
                    link(ins)
            ins.then_inc(passed_ready, 1)
            dve.wait_ge(et_counted, 1)
            link(nc.vector.tensor_copy(et_raw[:, :], ps_et[:, 0:VC]))
            link(nc.vector.tensor_scalar(et_f[:, :], et_raw[:, :], float(EROWS - 1), 0.0, ALU.min, ALU.max))
            link(nc.vector.tensor_copy(et_u[:, :], et_f[:, :]))
            link(nc.vector.tensor_tensor(nt_f[:, :], iota_s[:, :], et_raw[:, :], ALU.subtract))
            link(nc.vector.tensor_scalar(nt_f[:, :], nt_f[:, :], float(NT - 1), 0.0, ALU.min, ALU.max))
            link(nc.vector.tensor_scalar(nt_base[:, :], nt_f[:, :], float(P), None, ALU.mult))
            nc.vector.tensor_copy(nt_i[:, :], nt_f[:, :]).then_inc(et_ready, 1)
            dve.wait_ge(gathered[0], 16 * VC)
            for c in range(VC):
                link(nc.vector.tensor_scalar(local[:, c, :], dst_g[:, c, :], nt_base[:, c:c + 1], None, ALU.subtract))
            link(nc.vector.tensor_scalar(local_c[:, :, :], local[:, :, :], -1.0, float(P), ALU.max, ALU.min))
            link(nc.vector.tensor_copy(local_b[:, :, :], local_c[:, :, :]))
            link(nc.vector.tensor_scalar(local[:, :, :], local[:, :, :], 0.0, float(P - 1), ALU.max, ALU.min))
            dve.wait_ge(gathered[1], 16 * VC)
            link(nc.vector.tensor_copy(src_f[:, :, :], src_g[:, :, :]))
            for c in range(VC):
                link(nc.vector.tensor_scalar(key[:, c, :], local[:, c, :], nt_base[:, c:c + 1], None, ALU.add))
            nc.vector.memset(k.zero[:, :], 0.0).then_inc(locals_ready, 1)
            dve.wait_ge(gathered[2], 16 * VC)
            ea_v = ea_g[:, :, :].rearrange("p c (e f) -> p c f e", f=3)
            link(nc.vector.tensor_copy(ea_parts[:, :, :, 0, :], ea_v))
            link(nc.vector.tensor_tensor(ea_rest[:, :, :, :], ea_v, ea_parts[:, :, :, 0, :], ALU.subtract))
            link(nc.vector.tensor_copy(ea_parts[:, :, :, 1, :], ea_rest[:, :, :, :]))
            nc.vector.tensor_tensor(ea_parts[:, :, :, 2, :], ea_rest[:, :, :, :], ea_parts[:, :, :, 1, :],
                                    ALU.subtract).then_inc(parts_ready, 1)
            dve.wait_ge(row_in, 16)
            by_four = nt_row[:, :].rearrange("a (w i) -> a w i", i=4)
            link(nc.vector.tensor_copy(words_f[:, :], by_four[:, :, 3]))
            for i in (2, 1, 0):
                out = words_f if i else k.nt_words
                link(nc.vector.scalar_tensor_tensor(out[:, :], words_f[:, :], 64.0, by_four[:, :, i], ALU.mult, ALU.add))
            dve.wait_ge(turned, 1)
            for a in range(2):
                n = 4 * P if a == 0 else (VC - 4) * P
                nc.vector.tensor_copy(k.local_col[:, 4 * P * a:4 * P * a + n], ps_local[:, a, 0:n])
                nc.vector.tensor_copy(k.src_col[:, 4 * P * a:4 * P * a + n], ps_src[:, a, 0:n]).then_inc(cols_ready, 1)
            dve.wait_ge(cols_ready, 2)

        @block.tensor
        def _(pe):
            pe.wait_ge(passed_ready, 1)
            pe.wait_ge(iotas, 6)
            for c in range(VC):
                last = nc.tensor.matmul(ps_et[:, c:c + 1], passed_b[:, c * P:(c + 1) * P], ones_b[0:EP, :],
                                        start=True, stop=True)
            last.then_inc(et_counted, 1)
            pe.wait_ge(locals_ready, 1)
            for c in range(VC):
                nc.tensor.transpose(ps_local[:, c // 4, (c % 4) * P:(c % 4 + 1) * P], local_c[:, c, :], k.ident[:, :])
                last = nc.tensor.transpose(ps_src[:, c // 4, (c % 4) * P:(c % 4 + 1) * P], src_f[:, c, :], k.ident[:, :])
            last.then_inc(turned, 1)


def constants(nc, k):
    with ExitStack() as ctx:
        sb, ps, sem = allocators(nc, ctx)
        zeroed = sem("zeroed")
        made = sem("consts_made")
        block = ctx.enter_context(nc.Block())

        @block.gpsimd
        def _(pool):
            nc.gpsimd.memset(k.ident[:, :], 0.0).then_inc(zeroed, 1)
            nc.gpsimd.memset(k.eps[:, :], EPS)
            pool.wait_ge(zeroed, 1)
            nc.gpsimd.affine_select(out=k.ident[:, :], in_=k.ident[:, :], compare_op=ALU.not_equal, fill=1.0, base=0,
                                    pattern=[[-1, P]], channel_multiplier=1).then_inc(made, 1)
            pool.wait_ge(made, 1)


def node_rows(nc, k):
    with ExitStack() as ctx:
        sb, ps, sem = allocators(nc, ctx)
        w_nat = sb("w_nat", [P, 2, C])
        a_cols = sb("a_cols", [P, 2, 2])
        a_mask = sb("a_mask", [P, 2, H])
        a_blocks = sb("a_blocks", [P, 2, 2 * H])
        w_node = sb("w_node", [P, 2, NW])
        w_qkv = sb("w_qkv", [P, 2, QW])
        g_pre = sb("g_pre", [P, 2])
        stats = sb("stats", [P, NT, 6])
        mv = sb("mv", [P, NT, 2])
        std = sb("std", [P, NT])
        xn = sb("xn", [P, R, C])
        xn_t = sb("xn_t", [P, 2, 2, P])
        h_row = sb("h_row", [P, R, ROW])
        h_out = sb("h_out", [P, 2, NW])
        h_dst = sb("h_dst", [P, 2, ROW])
        h_rest = sb("h_rest", [P, 2, ROW])
        h_parts = sb("h_parts", [P, R, 3, ROW], BF16)
        s_src = sb("s_src", [P, NT, H])
        ps_w = ps("ps_w", [P, 512])
        ps_t = [ps(f"ps_t{i}", [P, 512]) for i in range(2)]
        ps_h = [ps(f"ps_h{i}", [P, 512]) for i in range(2)]
        ps_q = [ps(f"ps_q{i}", [P, 512]) for i in range(2)]

        w_in, x_in, x_pad = sem("w_in"), sem("x_in"), sem("x_pad")
        pool_step, dve_step = sem("n_pool_step"), sem("n_dve_step")
        mask_ready, blocks_ready, qkv_w_ready = sem("mask_ready"), sem("blocks_ready"), sem("qkv_w_ready")
        w_turned, w_node_ready, a_folded = sem("w_turned"), sem("w_node_ready"), sem("a_folded")
        stats_ready, std_ready, rstd_ready, norm_ready = (
            sem("stats_ready"), sem("std_ready"), sem("rstd_ready"), sem("norm_ready"))
        xn_ready, x_turned, xt_ready, h_done, q_done = (
            sem("xn_ready"), sem("x_turned"), sem("xt_ready"), sem("h_done"), sem("q_done"))
        ps_h_free, h_taken, ps_q_free, dve_split = sem("ps_h_free"), sem("h_taken"), sem("ps_q_free"), sem("dve_split")
        src_done, pool_seen = sem("src_done"), sem("pool_seen")
        rows_ready, parts_ready = sem("rows_ready"), sem("h_parts_ready")
        rows_out = [sem(f"rows_out{g}") for g in range(R)]
        parts_out = [sem(f"parts_out{g}") for g in range(R)]
        ones_set, src_out, stat_steps, squared, rooted = sem("ones_set"), sem("src_out"), sem("stat_steps"), sem("squared"), sem("rooted")
        block = ctx.enter_context(nc.Block())

        @block.sync
        def _(sp):
            with nc.allow_non_contiguous_dma("vectors laid down the partitions"):
                sp.wait_ge(x_pad, 1)
                for t in range(0, NT - 1, 8):
                    sp.dma_start(k.x_res[:, t:t + 8, :], k.x[t * P:(t + 8) * P, :].rearrange("(t p) c -> p t c", p=P)).then_inc(x_in, 16)
                sp.dma_start(k.x_res[0:NLAST, NT - 1, :], k.x[(NT - 1) * P:N, :]).then_inc(x_in, 16)
                sp.dma_start(w_nat[:, :, :], k.W.rearrange("(a p) c -> p a c", p=P)).then_inc(w_in, 16)
                sp.dma_start(a_cols[:, :, 0], k.a_src.rearrange("h d -> (h d)").rearrange("(a p) -> p a", p=P)).then_inc(w_in, 16)
                sp.dma_start(a_cols[:, :, 1], k.a_dst.rearrange("h d -> (h d)").rearrange("(a p) -> p a", p=P)).then_inc(w_in, 16)
                sp.dma_start(w_qkv[:, :, :], k.w_qkv.rearrange("(a p) c -> p a c", p=P)).then_inc(w_in, 16)
                sp.dma_start(g_pre[:, :], k.g_pre.rearrange("(a p) -> p a", p=P)).then_inc(w_in, 16)

            def store(it, g):
                t = it * R + g
                sp.wait_ge(rows_ready, t + 3)
                sp.dma_start(k.h_rows[bass.ds(t * P, P), :], h_row[:, g, :]).then_inc(rows_out[g], 16)
                sp.wait_ge(parts_ready, t + 1)
                sp.dma_start(k.hd_parts[bass.ds(t * P, P), :], h_parts[:, g].rearrange("p i c -> p (i c)")).then_inc(parts_out[g], 16)

            with sp.Fori(0, NT // R) as it:
                for g in range(R):
                    store(it, g)
            store(NT // R, 0)
            sp.wait_ge(rows_ready, NT + 2)
            sp.dma_start(k.src_logits.rearrange("(t p) h -> p t h", p=P), s_src[:, :, :]).then_inc(src_out, 16)
            for g in range(R):
                n = NT // R + (2 if g == 0 else 1)
                sp.wait_ge(rows_out[g], 16 * n)
                sp.wait_ge(parts_out[g], 16 * n)
            sp.wait_ge(src_out, 16)

        @block.gpsimd
        def _(pool):
            link = chain(pool, pool_step)
            nc.gpsimd.memset(k.x_res[:, NT - 1, :], 0.0).then_inc(x_pad, 1)
            nc.gpsimd.memset(h_row[:, :, :], 1.0).then_inc(ones_set, 1)
            link(nc.gpsimd.memset(a_mask[:, :, :], 1.0))
            link(nc.gpsimd.affine_select(out=a_mask[:, :, :], in_=a_mask[:, :, :], compare_op=ALU.is_ge, fill=0.0, base=0,
                                         pattern=[[P, 2], [-D, H]], channel_multiplier=1))
            nc.gpsimd.affine_select(out=a_mask[:, :, :], in_=a_mask[:, :, :], compare_op=ALU.is_ge, fill=0.0, base=D - 1,
                                    pattern=[[-P, 2], [D, H]], channel_multiplier=-1).then_inc(mask_ready, 1)
            pool.wait_ge(ones_set, 1)

            def source_rows(it, g):
                t = it * R + g
                pool.wait_ge(ps_h_free, t + 3)
                pool.wait_ge(rows_out[g], it * 16 + 16)
                pool.sem_inc(pool_seen, 1)
                nc.gpsimd.tensor_copy(heads(h_row[:, g, :], HW)[:, :, 0:D], heads(h_out[:, g % 2, 0:C]))
                nc.gpsimd.tensor_copy(s_src[:, bass.ds(t, 1), :], h_out[:, g % 2, C:C + H]).then_inc(rows_ready, 1)

            with pool.Fori(0, NT // R) as it:
                for g in range(R):
                    source_rows(it, g)
            source_rows(NT // R, 0)

        @block.vector
        def _(dve):
            link = chain(dve, dve_step)
            dve.wait_ge(w_in, 80)
            dve.wait_ge(mask_ready, 1)
            for a in range(2):
                nc.vector.tensor_scalar(a_blocks[:, a, 0:H], a_mask[:, a, :], a_cols[:, a, 0:1], None, ALU.mult)
                last = nc.vector.tensor_scalar(a_blocks[:, a, H:2 * H], a_mask[:, a, :], a_cols[:, a, 1:2], None, ALU.mult)
            last.then_inc(blocks_ready, 1)
            for a in range(2):
                link(nc.vector.tensor_scalar(w_qkv[:, a, :], w_qkv[:, a, :], g_pre[:, a:a + 1], None, ALU.mult))
            for a in range(2):
                dve.wait_ge(w_turned, a + 1)
                last = nc.vector.tensor_copy(w_node[:, a, 0:C], ps_w[:, 0:C])
                last.then_inc(w_node_ready, 1)
            dve.wait_ge(a_folded, 1)
            for a in range(2):
                nc.vector.tensor_copy(w_node[:, a, C:NW], ps_w[:, C + 2 * H * a:C + 2 * H * (a + 1)]).then_inc(w_node_ready, 1)
            dve.wait_ge(x_in, 16 * 7)
            with dve.Fori(0, NT // G) as it:
                for g in range(G):
                    t = it * G + g
                    nc.vector.bn_stats(stats[:, bass.ds(t, 1), :], k.x_res[:, bass.ds(t, 1), :]).then_inc(stat_steps, 1)
            dve.wait_ge(stat_steps, NT)
            moments(nc, link, stats, mv, stats_ready)
            dve.wait_ge(stats_ready, 1)
            dve.wait_ge(std_ready, 1)
            link(nc.vector.reciprocal(k.rstd[:, :], std[:, :]))
            nc.vector.scalar_tensor_tensor(k.shift[:, :], mv[:, :, 0], -1.0, k.rstd[:, :], ALU.mult, ALU.mult).then_inc(rstd_ready, 1)
            link(nc.vector.tensor_tensor(k.norm[:, :], k.rstd[:, :], k.rstd[:, :], ALU.mult))
            nc.vector.tensor_tensor(k.norm[:, :], k.norm[:, :], mv[:, :, 1], ALU.mult).then_inc(squared, 1)
            dve.wait_ge(rooted, 1)
            link(nc.vector.tensor_scalar(k.norm[:, :], k.norm[:, :], 1e-12, float(C) ** -0.5, ALU.max, ALU.mult))
            nc.vector.reciprocal(k.norm[:, :], k.norm[:, :]).then_inc(norm_ready, 1)

            def destination_rows(it, g):
                t = it * R + g
                s = g % 2
                dve.wait_ge(ps_h_free, t + 3)
                nc.vector.tensor_copy(heads(h_dst[:, s, :], HW)[:, :, D], h_out[:, s, C + H:NW])
                nc.vector.tensor_copy(heads(h_dst[:, s, :], HW)[:, :, 0:D], heads(h_out[:, s, 0:C])).then_inc(h_taken, 1)
                dve.wait_ge(h_taken, t + 3)
                dve.wait_ge(parts_out[g], it * 16 + 16)
                nc.vector.tensor_copy(h_parts[:, g, 0, :], h_dst[:, s, :]).then_inc(dve_split, 1)
                dve.wait_ge(dve_split, t * 3 + 1)
                nc.vector.tensor_tensor(h_rest[:, s, :], h_dst[:, s, :], h_parts[:, g, 0, :], ALU.subtract).then_inc(dve_split, 1)
                dve.wait_ge(dve_split, t * 3 + 2)
                nc.vector.tensor_copy(h_parts[:, g, 1, :], h_rest[:, s, :]).then_inc(dve_split, 1)
                dve.wait_ge(dve_split, t * 3 + 3)
                nc.vector.tensor_tensor(h_parts[:, g, 2, :], h_rest[:, s, :], h_parts[:, g, 1, :], ALU.subtract).then_inc(parts_ready, 1)

            with dve.Fori(0, NT // R) as it:
                for g in range(R):
                    destination_rows(it, g)
            destination_rows(NT // R, 0)

        @block.scalar
        def _(act):
            for g in range(R):
                act.sem_inc(parts_out[g], 16)
                act.sem_inc(rows_out[g], 16)
            for free in (ps_h_free, h_taken, rows_ready, ps_q_free, xt_ready):
                act.sem_inc(free, 2)
            act.wait_ge(stats_ready, 1)
            nc.scalar.activation(std[:, :], mv[:, :, 1], ACT.Sqrt, bias=k.eps[:, 0:1]).then_inc(std_ready, 1)
            act.wait_ge(squared, 1)
            nc.scalar.activation(k.norm[:, :], k.norm[:, :], ACT.Sqrt, scale=float(C)).then_inc(rooted, 1)
            act.wait_ge(norm_ready, 1)
            act.wait_ge(ones_set, 1)

            def normed(t, g):
                nc.scalar.activation(xn[:, g % R, :], k.x_res[:, bass.ds(t, 1), :], ACT.Identity, scale=k.rstd[:, bass.ds(t, 1)],
                                     bias=k.shift[:, bass.ds(t, 1)]).then_inc(xn_ready, 1)

            def turned_copy(t, g):
                act.wait_ge(x_turned, t + 1)
                nc.scalar.copy(xn_t[:, g % 2].rearrange("p a n -> p (a n)"), ps_t[g % 2][:, 0:C]).then_inc(xt_ready, 1)

            def node_tile(it, g, ahead=2):
                t = it * R + g
                s = g % 2
                if ahead >= 1:
                    turned_copy(t + 1, g + 1)
                if ahead >= 2:
                    normed(t + 2, g + 2)
                act.wait_ge(h_done, t + 1)
                act.wait_ge(rows_ready, t + 1)
                act.wait_ge(h_taken, t + 1)
                nc.scalar.copy(h_out[:, s, :], ps_h[s][:, 0:NW]).then_inc(ps_h_free, 1)
                act.wait_ge(q_done, t + 1)
                nc.scalar.activation(k.qkv[:, bass.ds(t, 1), 0:QW], ps_q[s][:, 0:QW], ACT.Copy,
                                     scale=k.norm[:, bass.ds(t, 1)]).then_inc(ps_q_free, 1)

            normed(0, 0)
            normed(1, 1)
            turned_copy(0, 0)
            with act.Fori(0, NT // R - 1) as it:
                for g in range(R):
                    node_tile(it, g)
            for t in range(NT - 1 - R, NT):
                node_tile(t // R, t % R, min(2, NT - 1 - t))

        @block.tensor
        def _(pe):
            pe.wait_ge(w_in, 80)
            for a in range(2):
                if a:
                    pe.wait_ge(w_node_ready, 1)
                for b in range(2):
                    last = nc.tensor.transpose(ps_w[:, b * P:(b + 1) * P], w_nat[:, b, a * P:(a + 1) * P], k.ident[:, :])
                last.then_inc(w_turned, 1)
            pe.wait_ge(blocks_ready, 1)
            pe.wait_ge(w_node_ready, 2)
            for a in range(2):
                for b in range(2):
                    last = nc.tensor.matmul(ps_w[:, C + 2 * H * a:C + 2 * H * (a + 1)], w_nat[:, b, a * P:(a + 1) * P],
                                            a_blocks[:, b, :], start=b == 0, stop=b == 1)
            last.then_inc(a_folded, 1)
            pe.wait_ge(w_node_ready, 4)
            pe.wait_ge(dve_step, 2)

            def turn_rows(t, g):
                pe.wait_ge(xn_ready, t + 1)
                pe.wait_ge(xt_ready, t + 1)
                for a in range(2):
                    last = nc.tensor.transpose(ps_t[g % 2][:, a * P:(a + 1) * P], xn[:, g % R, a * P:(a + 1) * P], k.ident[:, :])
                last.then_inc(x_turned, 1)

            def products(t, s):
                pe.wait_ge(xt_ready, t + 3)
                pe.wait_ge(ps_h_free, t + 1)
                for a in range(2):
                    last = nc.tensor.matmul(ps_h[s][:, 0:NW], xn_t[:, s, a, :], w_node[:, a, :], start=a == 0, stop=a == 1)
                last.then_inc(h_done, 1)
                pe.wait_ge(ps_q_free, t + 1)
                for a in range(2):
                    last = nc.tensor.matmul(ps_q[s][:, 0:QW], xn_t[:, s, a, :], w_qkv[:, a, :], start=a == 0, stop=a == 1)
                last.then_inc(q_done, 1)

            turn_rows(0, 0)
            with pe.Fori(0, NT // R) as it:
                for g in range(R):
                    turn_rows(it * R + (g + 1), g + 1)
                    products(it * R + g, g % 2)
            products(NT - 1, 0)


class SourceGathers:

    def __init__(self, nc, k, sb, sem, tag, first, last):
        self.nc, self.k, self.first, self.turns = nc, k, first, (last - first) // SLOTS
        self.idx = [sb(f"src_idx_{tag}{s}", [P, BS], U32) for s in range(SLOTS)]
        self.ring = [sb(f"src_ring_{tag}{s}", [P, BS, H]) for s in range(SLOTS)]
        self.gathered = [sem(f"src_gathered_{tag}{s}") for s in range(SLOTS)]
        self.seen, self.idx_ready, self.taken = sem(f"src_seen_{tag}"), sem(f"src_idx_ready_{tag}"), sem(f"src_taken_{tag}")

    def take(self, pool, turn, s):
        pool.wait_ge(self.gathered[s], (turn + 1) * (16 * BS))
        pool.sem_inc(self.seen, 1)
        cols = bass.ds((turn * SLOTS + (self.first + s)) * BS, BS)
        self.nc.gpsimd.tensor_copy(self.k.src_all[:, cols, :], self.ring[s][:, :, :]).then_inc(self.taken, 1)

    def gather(self, pool, turn, s):
        cols = bass.ds((turn * SLOTS + (self.first + s)) * BS, BS)
        self.nc.gpsimd.tensor_copy(self.idx[s][:, :], self.k.src_col[:, cols]).then_inc(self.idx_ready, 1)
        pool.wait_ge(self.idx_ready, turn * SLOTS + (s + 1))
        pool.sem_inc(self.seen, 1)
        for b in range(BS):
            pool.indirect_dma_start(self.ring[s][:, b, :], None, self.k.src_logits[:, :],
                                    bass.IndirectOffsetOnAxis(ap=self.idx[s][:, b:b + 1], axis=0)).then_inc(self.gathered[s], 16)

    def run(self, pool):
        for s in range(SLOTS):
            self.gather(pool, 0, s)
        with pool.Fori(1, self.turns) as it:
            for s in range(SLOTS):
                self.take(pool, it - 1, s)
                pool.wait_ge(self.taken, (it - 1) * SLOTS + (s + 1))
                self.gather(pool, it, s)
        for s in range(SLOTS):
            self.take(pool, self.turns - 1, s)


def edge_logits(nc, k):
    with ExitStack() as ctx:
        sb, ps, sem = allocators(nc, ctx)
        hd_tab = sb("hd_tab", [P, NT, 3 * ROW], BF16)
        ea_t = [sb(f"ea_t{s}", [30, BS * P], BF16) for s in range(2)]
        loc_row = [sb(f"loc_row{s}", [P, BS * P], BF16) for s in range(2)]
        onehot = [sb(f"onehot{s}", [P, BS * P], BF16) for s in range(2)]
        enc = sb("enc", [P, 4, ROW])
        prod = sb("prod", [P, 4, ROW])
        outside = sb("outside", [P, V])
        outside2 = sb("outside2", [P, V])
        ps_enc = [ps(f"ps_enc{i}", [P, 512]) for i in range(4)]
        ps_hd = [ps(f"ps_hd{i}", [P, 512]) for i in range(4)]
        tab_in, set_up = sem("tab_in"), sem("set_up")
        ea_in = [sem(f"ea_in{s}") for s in range(2)]
        loc_in = [sem(f"loc_in{s}") for s in range(2)]
        sources = SourceGathers(nc, k, sb, sem, "late", EARLY, NBLK)
        enc_done, relu_done, hd_done = sem("enc_done"), sem("relu_done"), sem("hd_done")
        prod_done, reduced, onehot_ready, block_done = sem("prod_done"), sem("reduced"), sem("onehot_ready"), sem("block_done")
        out_step = sem("b_out_step")
        block = ctx.enter_context(nc.Block())

        @block.sync
        def _(sp):
            for t in range(0, NT, G):
                sp.dma_start(hd_tab[:, t:t + G, :], k.hd_parts[t * P:(t + G) * P, :].rearrange("(t p) c -> p t c", p=P)).then_inc(tab_in, 16)
            sp.wait_ge(set_up, 2)

            def bring(j, s):
                sp.wait_ge(onehot_ready, j + 1)
                sp.wait_ge(block_done, j + 1)
                for i in range(3):
                    sp.dma_start(ea_t[s][9 * i:9 * i + 9, :],
                                 k.ea_parts[:, bass.ds(j * BS, BS), :].rearrange("r v e -> r (v e)")).then_inc(ea_in[s], 16)
                sp.dma_start(loc_row[s][:, :], k.local_rows[bass.ds(j * BS, BS), :].rearrange("(a v) e -> a (v e)", a=1)
                             .to_broadcast([P, BS * P])).then_inc(loc_in[s], 16)

            with sp.Fori(0, NBLK // 2) as it:
                for s in range(2):
                    bring(it * 2 + s, s)
            bring(NBLK, 0)
            sp.wait_ge(ea_in[0], 48 * (NBLK // 2 + 1))
            sp.wait_ge(loc_in[0], 16 * (NBLK // 2 + 1))

        @block.gpsimd
        def _(pool):
            for s in range(2):
                nc.gpsimd.memset(ea_t[s][:, :], 1.0).then_inc(set_up, 1)
            sources.run(pool)

        @block.scalar
        def _(act):
            act.sem_inc(block_done, 2)
            act.sem_inc(onehot_ready, 2)
            act.sem_inc(relu_done, 4)
            act.sem_inc(prod_done, 4)
            act.sem_inc(reduced, 4)
            with act.Fori(0, NBLK // 2) as it:
                for s in range(2):
                    j = it * 2 + s
                    for b in range(BS):
                        v = j * BS + b
                        act.wait_ge(enc_done, v + 1)
                        act.wait_ge(prod_done, v + 1)
                        nc.scalar.activation(enc[:, b % 4, :], ps_enc[b % 4][:, 0:ROW], ACT.Relu).then_inc(relu_done, 1)

        @block.tensor
        def _(pe):
            pe.wait_ge(tab_in, 16 * (NT // G))
            with pe.Fori(0, NBLK // 2) as it:
                for s in range(2):
                    j = it * 2 + s
                    pe.wait_ge(ea_in[s], (it + 1) * 48)
                    for b in range(BS + 1):
                        v = j * BS + b
                        if b < BS:
                            if b % 2 == 0:
                                pe.wait_ge(relu_done, v + 2)
                            nc.tensor.matmul(ps_enc[b % 4][:, 0:ROW], ea_t[s][:, b * P:(b + 1) * P], k.enc_w[:, :],
                                             start=True, stop=True).then_inc(enc_done, 1)
                        if b == 0:
                            nts = node_tiles(pe, k, j) if s == 0 else nts_next
                            pe.wait_ge(onehot_ready, j + 3)
                            continue
                        if s == 0 and b == 4:
                            nts_next = node_tiles(pe, k, j + 1)
                        b, v = b - 1, v - 1
                        if b % 2 == 0:
                            pe.wait_ge(prod_done, v + 2)
                        for i in range(3):
                            last = nc.tensor.matmul(ps_hd[b % 4][:, 0:ROW], onehot[s][:, b * P:(b + 1) * P],
                                                    hd_tab[:, bass.ds(nts[b], 1), i * ROW:(i + 1) * ROW], start=i == 0, stop=i == 2)
                        last.then_inc(hd_done, 1)
                    pe.wait_ge(hd_done, (j + 1) * BS)
                    pe.sem_inc(block_done, 1)

        @block.vector
        def _(dve):
            link = chain(dve, out_step)

            def one_hot(s):
                nc.vector.tensor_scalar(onehot[s][:, :], loc_row[s][:, :], k.iota_col[:, 0:1], None, ALU.is_equal).then_inc(onehot_ready, 1)

            dve.wait_ge(loc_in[0], 16)
            one_hot(0)
            with dve.Fori(0, NBLK // 2) as it:
                for s in range(2):
                    j = it * 2 + s
                    for b in range(BS + 1):
                        v = j * BS + b
                        if b == BS - 2:
                            dve.wait_ge(loc_in[1 - s], (it + (1 + s)) * 16)
                            dve.wait_ge(block_done, j + 2)
                            one_hot(1 - s)
                        if b < BS:
                            dve.wait_ge(hd_done, v + 1)
                            dve.wait_ge(relu_done, v + 5)
                            dve.wait_ge(reduced, v + 1)
                            nc.vector.tensor_tensor(prod[:, b % 4, :], enc[:, b % 4, :], ps_hd[b % 4][:, 0:ROW], ALU.mult).then_inc(prod_done, 1)
                        if b >= 1:
                            dve.wait_ge(prod_done, v + 4)
                            nc.vector.tensor_reduce(k.alpha[:, bass.ds(v - 1, 1), :], heads(prod[:, (b - 1) % 4, :], HW), AX.X, ALU.add).then_inc(reduced, 1)
            dve.wait_ge(sources.taken, NBLK - EARLY)
            dve.wait_ge(reduced, V + 4)
            link(nc.vector.tensor_tensor(k.alpha[:, :, :], k.alpha[:, :, :], k.src_all[:, :, :], ALU.add))
            link(nc.vector.tensor_scalar(k.src_all[:, :, :], k.alpha[:, :, :], 0.2, None, ALU.mult))
            link(nc.vector.tensor_tensor(k.alpha[:, :, :], k.alpha[:, :, :], k.src_all[:, :, :], ALU.max))
            link(nc.vector.tensor_scalar(outside[:, :], k.local_col[:, 0:V], 0.0, -BIG, ALU.is_lt, ALU.mult))
            link(nc.vector.tensor_scalar(outside2[:, :], k.local_col[:, 0:V], float(P), -BIG, ALU.is_ge, ALU.mult))
            link(nc.vector.tensor_tensor(outside[:, :], outside[:, :], outside2[:, :], ALU.add))
            link(nc.vector.tensor_tensor(k.alpha[:, :, :], k.alpha[:, :, :], outside[:, :].unsqueeze(2).to_broadcast([P, V, H]), ALU.add))


def segment_softmax(nc, k):
    with ExitStack() as ctx:
        sb, ps, sem = allocators(nc, ctx)
        L = CT * P
        gathered_cols = [sb(f"turn_in{s}", [P, 2, P]) for s in range(2)]
        alpha_t = sb("alpha_t", [P, L])
        key_t = sb("key_t", [P, L])
        reset = sb("reset", [P, L + 1])
        fwd = sb("fwd", [P, L])
        best = sb("best", [P, L])
        edge_stat = sb("edge_stat", [P, 4])
        stat_all = sb("stat_all", [P, CH, 4])
        other = sb("other", [P, 2, 2, CH])
        across = sb("across", [P, 2])
        zeros = sb("zero_rows", [P, 2, C])
        zeroed, cleared = sem("zero_rows_set"), sem("cleared")
        ps_in = [ps(f"ps_in{s}", [P, 512]) for s in range(2)]
        ps_out = [ps(f"ps_out{s}", [P, 512]) for s in range(2)]
        keys_in, stat_ready, stat_out, stat_in = sem("keys_in"), sem("stat_ready"), sem("stat_out"), sem("stat_in")
        cols_ready, cols_turned, cols_copied = sem("s_cols_ready"), sem("s_cols_turned"), sem("s_cols_copied")
        shifted, exp_ready, exp_turned, exp_copied = sem("shifted"), sem("exp_ready"), sem("exp_turned"), sem("exp_copied")
        dve_step = sem("s_dve_step")
        block = ctx.enter_context(nc.Block())
        by_chunk = k.alpha[:, :, :].rearrange("p (j g) h -> p g j h", g=CT)

        @block.sync
        def _(sp):
            for j in range(CH):
                sp.dma_start(key_t[H * j:H * (j + 1), :], k.key_rows[j * CT:(j + 1) * CT, :].rearrange("(a v) e -> a (v e)", a=1)
                             .to_broadcast([H, L])).then_inc(keys_in, 16)
            sp.wait_ge(stat_ready, 4)
            sp.dma_start(k.chunk_stats[:, :], edge_stat[:, :]).then_inc(stat_out, 16)
            sp.wait_ge(stat_out, 16)
            for j in range(CH):
                sp.dma_start(stat_all[H * j:H * (j + 1), :, :], k.chunk_stats.rearrange("(i h) c -> h i c", h=H)).then_inc(stat_in, 16)
            sp.wait_ge(zeroed, 1)
            for b in range(0, NB, 2):
                sp.dma_start(k.list_rows[b * P:(b + 2) * P, :].rearrange("(t p) c -> p t c", p=P), zeros[:, :, :]).then_inc(cleared, 16)
            sp.wait_ge(cleared, 8 * NB)

        @block.gpsimd
        def _(pool):
            nc.gpsimd.memset(zeros[:, :, :], 0.0).then_inc(zeroed, 1)

        @block.scalar
        def _(act):
            act.sem_inc(cols_turned, 2)
            act.sem_inc(cols_copied, 2)
            with act.Fori(0, CT // 4) as it:
                for s in range(2):
                    act.wait_ge(cols_turned, it * 2 + (s + 1))
                    nc.scalar.copy(gathered_cols[s][:, :, :].rearrange("p g (j h) -> p g j h", h=H),
                                   by_chunk[:, bass.ds(it * 4 + 2 * s, 2), :, :]).then_inc(cols_ready, 1)
            act.wait_ge(shifted, 1)
            with act.Fori(0, CT // 4) as it:
                for s in range(2):
                    act.wait_ge(exp_turned, it * 2 + (s + 1))
                    nc.scalar.activation(gathered_cols[s][:, :, :].rearrange("p g e -> p (g e)"),
                                         alpha_t[:, bass.ds((it * 4 + 2 * s) * P, 2 * P)], ACT.Exp).then_inc(exp_ready, 1)

        @block.tensor
        def _(pe):
            with pe.Fori(0, CT // 4) as it:
                for s in range(2):
                    pe.wait_ge(cols_ready, it * 2 + (s + 1))
                    pe.wait_ge(cols_copied, it * 2 + (s + 1))
                    for g in range(2):
                        last = nc.tensor.transpose(ps_in[s][:, g * P:(g + 1) * P], gathered_cols[s][:, g, :], k.ident[:, :])
                    last.then_inc(cols_turned, 1)
            with pe.Fori(0, CT // 4) as it:
                for s in range(2):
                    pe.wait_ge(exp_ready, it * 2 + (s + 1))
                    pe.wait_ge(exp_copied, it * 2 + (s + 1))
                    for g in range(2):
                        last = nc.tensor.transpose(ps_out[s][:, g * P:(g + 1) * P], gathered_cols[s][:, g, :], k.ident[:, :])
                    last.then_inc(exp_turned, 1)

        @block.vector
        def _(dve):
            link = chain(dve, dve_step)
            dve.sem_inc(exp_turned, 2)
            dve.sem_inc(exp_copied, 2)
            with dve.Fori(0, CT // 4) as it:
                for s in range(2):
                    dve.wait_ge(cols_turned, it * 2 + (s + 3))
                    nc.vector.tensor_copy(alpha_t[:, bass.ds((it * 4 + 2 * s) * P, 2 * P)], ps_in[s][:, 0:2 * P]).then_inc(cols_copied, 1)
            dve.wait_ge(keys_in, 16 * CH)
            nc.vector.memset(reset[:, 0:1], 0.0)
            nc.vector.memset(reset[:, L:L + 1], 0.0)
            link(nc.vector.tensor_tensor(reset[:, 1:L], key_t[:, 1:L], key_t[:, 0:L - 1], ALU.not_equal))
            link(nc.vector.tensor_scalar(reset[:, 1:L], reset[:, 1:L], -BIG * 1e6, None, ALU.mult))
            dve.wait_ge(cols_copied, CT // 2 + 2)
            link(nc.vector.tensor_tensor_scan(fwd[:, :], reset[:, 0:L], alpha_t[:, :], -BIG * 1e6, ALU.add, ALU.max))
            link(nc.vector.tensor_tensor_scan(best[:, ::-1], reset[:, 1:L + 1][:, ::-1], fwd[:, ::-1], -BIG * 1e6, ALU.add, ALU.max))
            for c, col in enumerate((best[:, 0:1], best[:, L - 1:L], key_t[:, 0:1], key_t[:, L - 1:L])):
                nc.vector.tensor_copy(edge_stat[:, c:c + 1], col).then_inc(stat_ready, 1)
            dve.wait_ge(stat_in, 16 * CH)
            dve.wait_ge(stat_ready, 4)
            for mine in range(2):
                for theirs in range(2):
                    link(nc.vector.tensor_scalar(other[:, mine, theirs, :], stat_all[:, :, 2 + theirs], edge_stat[:, 2 + mine:3 + mine],
                                                 -BIG * 1e6, ALU.not_equal, ALU.mult))
                    link(nc.vector.tensor_tensor(other[:, mine, theirs, :], other[:, mine, theirs, :], stat_all[:, :, theirs], ALU.add))
            link(nc.vector.tensor_reduce(across[:, :], other[:, :, :, :], AX.XY, ALU.max))
            for mine in range(2):
                link(nc.vector.tensor_scalar(reset[:, 0:L], key_t[:, :], edge_stat[:, 2 + mine:3 + mine], -BIG * 1e6,
                                             ALU.not_equal, ALU.mult))
                link(nc.vector.scalar_tensor_tensor(best[:, :], reset[:, 0:L], across[:, mine:mine + 1], best[:, :], ALU.add, ALU.max))
            nc.vector.tensor_tensor(alpha_t[:, :], alpha_t[:, :], best[:, :], ALU.subtract).then_inc(shifted, 1)
            with dve.Fori(0, CT // 4) as it:
                for s in range(2):
                    dve.wait_ge(exp_turned, it * 2 + (s + 3))
                    nc.vector.tensor_copy(by_chunk[:, bass.ds(it * 4 + 2 * s, 2), :, :],
                                          ps_out[s][:, 0:2 * P].rearrange("p (g j h) -> p g j h", g=2, h=H)).then_inc(exp_copied, 1)


def aggregate(nc, k):
    with ExitStack() as ctx:
        sb, ps, sem = allocators(nc, ctx)
        src_idx = [sb(f"row_idx{s}", [P, BS], U32) for s in range(SLOTS)]
        rows = [sb(f"rows{s}", [P, BS, ROW]) for s in range(SLOTS)]
        weighted = sb("weighted", [P, 4, ROW])
        away = sb("away", [P, 4, P])
        onehot = sb("onehot_f", [P, 4, P])
        ps_sum = [ps(f"ps_sum{i}", [P, 512]) for i in range(4)]
        rows_in = [sem(f"rows_in{s}") for s in range(SLOTS)]
        idx_in = [sem(f"row_idx_in{s}") for s in range(SLOTS)]
        idx_seen, weighted_ready, onehot_ready = sem("d_idx_seen"), sem("weighted_ready"), sem("d_onehot_ready")
        summed, added, away_ready = sem("summed"), sem("added"), sem("away_ready")
        block = ctx.enter_context(nc.Block())

        @block.sync
        def _(sp):
            def bring(turn, s):
                sp.dma_start(src_idx[s][:, :], k.src_col[:, bass.ds((turn * SLOTS + s) * BS, BS)]).then_inc(idx_in[s], 16)

            for s in range(SLOTS):
                bring(0, s)
            with sp.Fori(0, NBLK // SLOTS) as it:
                for s in range(SLOTS):
                    sp.wait_ge(rows_in[s], (it + 1) * (16 * BS))
                    bring(it + 1, s)
            for s in range(SLOTS):
                sp.wait_ge(idx_in[s], 16 * (NBLK // SLOTS + 1))

        @block.gpsimd
        def _(pool):
            with pool.Fori(0, NBLK // SLOTS) as it:
                for s in range(SLOTS):
                    pool.wait_ge(idx_in[s], (it + 1) * 16)
                    pool.wait_ge(weighted_ready, (it * SLOTS + (s + 1)) * BS)
                    pool.sem_inc(idx_seen, 1)
                    for b in range(BS):
                        pool.indirect_dma_start(rows[s][:, b, :], None, k.h_rows[:, :],
                                                bass.IndirectOffsetOnAxis(ap=src_idx[s][:, b:b + 1], axis=0)).then_inc(rows_in[s], 16)

        @block.scalar
        def _(act):
            with act.Fori(0, NBLK // 2) as it:
                for s in range(2):
                    for b in range(BS):
                        v = (it * 2 + s) * BS + b
                        act.wait_ge(summed, v + 1)
                        nc.scalar.activation(away[:, b % 4, :], k.iota_row[:, :], ACT.Abs, scale=-1.0,
                                             bias=k.local_col[:, bass.ds(v, 1)]).then_inc(away_ready, 1)
                        act.wait_ge(away_ready, v + 1)
                        nc.scalar.activation(onehot[:, b % 4, :], away[:, b % 4, :], ACT.Relu, scale=-1.0, bias=1.0).then_inc(onehot_ready, 1)

        @block.tensor
        def _(pe):
            with pe.Fori(0, NBLK // 2) as it:
                for s in range(2):
                    for b in range(BS):
                        v = (it * 2 + s) * BS + b
                        pe.wait_ge(weighted_ready, v + (SLOTS * BS + 1))
                        pe.wait_ge(onehot_ready, v + 1)
                        pe.wait_ge(added, v + 1)
                        nc.tensor.matmul(ps_sum[b % 4][:, 0:ROW], onehot[:, b % 4, :], weighted[:, b % 4, :],
                                         start=True, stop=True).then_inc(summed, 1)

        @block.vector
        def _(dve):
            nc.vector.memset(k.acc[:, :, :], 0.0).then_inc(added, 4)
            dve.sem_inc(weighted_ready, SLOTS * BS)
            dve.sem_inc(summed, 4)

            def weigh(v, s, b):
                dve.wait_ge(summed, v + 1)
                nc.vector.tensor_tensor(heads(weighted[:, b % 4, :], HW), heads(rows[s][:, b, :], HW),
                                        k.alpha[:, bass.ds(v, 1), :].rearrange("p a h -> p h a").to_broadcast([P, H, HW]),
                                        ALU.mult).then_inc(weighted_ready, 1)

            def turn(it, last):
                tiles = [node_tiles(dve, k, it * SLOTS), None]
                for s in range(SLOTS):
                    for b in range(BS):
                        v = (it * SLOTS + s) * BS + b
                        ahead = s * BS + b + 2
                        at, a = ahead // BS, ahead % BS
                        if at < SLOTS or not last:
                            if a == 0:
                                dve.wait_ge(rows_in[at % SLOTS], (it + (1 + at // SLOTS)) * (16 * BS))
                            weigh(v + 2, at % SLOTS, a)
                        if b == BS // 2 and s < SLOTS - 1:
                            tiles[(s + 1) % 2] = node_tiles(dve, k, it * SLOTS + (s + 1))
                        tile = bass.ds(tiles[s % 2][b], 1)
                        dve.wait_ge(summed, v + 5)
                        dve.wait_ge(added, v + 4)
                        nc.vector.tensor_tensor(k.acc[:, tile, :], k.acc[:, tile, :], ps_sum[b % 4][:, 0:ROW], ALU.add).then_inc(added, 1)

            dve.wait_ge(rows_in[0], 16 * BS)
            weigh(0, 0, 0)
            weigh(1, 0, 1)
            with dve.Fori(0, NBLK // SLOTS - 1) as it:
                turn(it, False)
            turn(NBLK // SLOTS - 1, True)


def linear_attention(nc, k):
    with ExitStack() as ctx:
        sb, ps, sem = allocators(nc, ctx)
        q_max = sb("q_max", [P, NT * MH])
        q_sum = sb("q_sum", [P, NT * MH])
        beyond = sb("beyond", [P, 1])
        k_max = sb("k_max", [P, MHID])
        k_top = sb("k_top", [P, 4])
        k_top_b = sb("k_top_b", [P, P])
        k_top_row = sb("k_top_row", [P, P])
        mem_k = sb("mem_k", [P, MEM])
        mem_v = sb("mem_v", [P, MEM])
        mem_kt = sb("mem_kt", [MEM, P])
        mem_vt = sb("mem_vt", [MEM, P + 1])
        same_head = sb("same_head", [P, P])
        w_out = sb("w_out_sb", [P, C])
        b_out = sb("b_out_sb", [1, C])
        ones_row = sb("ones_row", [1, P])
        g_out = sb("g_out_sb", [P, C])
        bias = sb("bias_sb", [P, C])
        exp_k = sb("exp_k", [P, 4, P])
        context = sb("context", [P, P])
        context_t = sb("context_t", [P, P])
        mixer = sb("mixer", [P, C])
        k_total = sb("k_total", [P, 1])
        q_norm = sb("q_norm", [P, G, P])
        q_t = sb("q_t", [P, 2, P])
        squares = sb("squares_dump", [P, 2, C])
        out_norm = sb("out_norm", [P, NT])
        xn = sb("xn_again", [P, G, C])
        rstd_1 = sb("rstd_1", [P, NT])
        base = sb("base_ring", [P, G, C])
        ps_a = ps("m_ps_a", [P, 512])
        ps_b = ps("m_ps_b", [P, 512])
        ps_c = ps("m_ps_c", [P, 512])
        ps_qt = [ps(f"ps_qt{i}", [P, 512]) for i in range(2)]
        ps_o = [ps(f"ps_o{i}", [P, 512]) for i in range(2)]
        small_in, masks_ready, q_shifted, q_exp, q_ready = sem("small_in"), sem("masks_ready"), sem("q_shifted"), sem("q_exp"), sem("q_ready")
        kmax_ready, kmax_turned, top_ready, top_spread, k_shifted = (
            sem("kmax_ready"), sem("kmax_turned"), sem("top_ready"), sem("top_spread"), sem("k_shifted"))
        mem_exp, mem_turned, mem_ready = sem("mem_exp"), sem("mem_turned"), sem("mem_ready")
        exp_ready, exp_used, context_done = sem("m_exp_ready"), sem("m_exp_used"), sem("context_done")
        ctx_ready, ctx_turned, ctx_t_ready, mixed, mixer_ready = (
            sem("ctx_ready"), sem("ctx_turned"), sem("ctx_t_ready"), sem("mixed"), sem("mixer_ready"))
        qn_ready, qn_turned, qt_ready, out_done, out_copied, squared = (
            sem("qn_ready"), sem("qn_turned"), sem("qt_ready"), sem("m_out_done"), sem("out_copied"), sem("m_squared"))
        roots, scale_ready, xn_ready, base_step, base_ready = (
            sem("roots"), sem("m_scale_ready"), sem("m_xn_ready"), sem("base_step"), sem("base_ready"))
        sources = SourceGathers(nc, k, sb, sem, "early", 0, EARLY)
        base_out = [sem(f"base_out{g}") for g in range(G)]
        dve_step, pool_step = sem("m_dve_step"), sem("m_pool_step")
        block = ctx.enter_context(nc.Block())
        q_heads = k.qkv[:, :, 0:MHID].rearrange("p t (h d) -> p t h d", d=MD)
        keys = k.qkv[:, :, MHID:2 * MHID]
        out_raw = k.qkv[:, :, 0:C]

        @block.sync
        def _(sp):
            sp.dma_start(mem_k[:, :], k.mem_kv[0].rearrange("h d m -> (h d) m")).then_inc(small_in, 16)
            sp.dma_start(mem_v[:, :], k.mem_kv[1].rearrange("h d m -> (h d) m")).then_inc(small_in, 16)
            sp.dma_start(w_out[:, :], k.w_out[:, :]).then_inc(small_in, 16)
            sp.dma_start(b_out[:, :], k.b_out.rearrange("(a c) -> a c", a=1)).then_inc(small_in, 16)
            sp.dma_start(g_out[:, :], k.g_out.rearrange("(a c) -> a c", a=1).to_broadcast([P, C])).then_inc(small_in, 16)
            sp.dma_start(bias[:, :], k.bias.rearrange("(a c) -> a c", a=1).to_broadcast([P, C])).then_inc(small_in, 16)
            with sp.Fori(0, NT // G) as it:
                for g in range(G):
                    sp.wait_ge(base_ready, it * G + (g + 1 + G))
                    sp.dma_start(k.base_rows[bass.ds((it * G + g) * P, P), :], base[:, g, :]).then_inc(base_out[g], 16)
            for g in range(G):
                sp.wait_ge(base_out[g], 16 * (NT // G + 1))

        @block.gpsimd
        def _(pool):
            link = chain(pool, pool_step)
            nc.gpsimd.memset(ones_row[:, :], 1.0).then_inc(masks_ready, 1)
            nc.gpsimd.memset(mem_vt[:, :], 1.0).then_inc(masks_ready, 1)
            nc.gpsimd.memset(k.qkv[:, :, QW:QW + 1], 1.0).then_inc(masks_ready, 1)
            link(nc.gpsimd.memset(same_head[:, :], 1.0))
            link(nc.gpsimd.affine_select(out=heads(same_head[:, :], MD), in_=heads(same_head[:, :], MD), compare_op=ALU.is_ge,
                                         fill=0.0, base=0, pattern=[[-MD, MH], [0, MD]], channel_multiplier=1))
            nc.gpsimd.affine_select(out=heads(same_head[:, :], MD), in_=heads(same_head[:, :], MD), compare_op=ALU.is_ge,
                                    fill=0.0, base=MD - 1, pattern=[[MD, MH], [0, MD]], channel_multiplier=-1).then_inc(masks_ready, 1)
            sources.run(pool)

        @block.vector
        def _(dve):
            link = chain(dve, dve_step)
            link(nc.vector.tensor_reduce(q_max[:, :], q_heads, AX.X, ALU.max))
            nc.vector.tensor_tensor(q_heads, q_heads, q_max[:, :].rearrange("p (t h) -> p t h", h=MH).unsqueeze(3)
                                    .to_broadcast([P, NT, MH, MD]), ALU.subtract).then_inc(q_shifted, 1)
            link(nc.vector.tensor_scalar(beyond[:, :], k.iota_col[:, :], float(NLAST), -BIG, ALU.is_ge, ALU.mult))
            link(nc.vector.tensor_scalar(keys[:, NT - 1, :], keys[:, NT - 1, :], beyond[:, 0:1], None, ALU.add))
            nc.vector.tensor_reduce(k_max[:, :], keys.rearrange("p t c -> p c t"), AX.X, ALU.max).then_inc(kmax_ready, 1)
            dve.wait_ge(small_in, 96)
            link(nc.vector.tensor_reduce(k_top[:, 0:1], mem_k[:, :], AX.X, ALU.max))
            dve.wait_ge(kmax_turned, 1)
            link(nc.vector.tensor_reduce(k_top[:, 1:2], ps_a[:, 0:P], AX.X, ALU.max))
            link(nc.vector.tensor_tensor(k_top[:, 2:3], k_top[:, 0:1], k_top[:, 1:2], ALU.max))
            link(nc.vector.memset(k_top_b[:, :], 0.0))
            link(nc.vector.tensor_scalar(k_top_b[:, :], k_top_b[:, :], k_top[:, 2:3], None, ALU.add))
            nc.vector.tensor_scalar(k_top[:, 3:4], k_top[:, 2:3], -1.0, None, ALU.mult).then_inc(top_ready, 1)
            dve.wait_ge(top_spread, 1)
            link(nc.vector.tensor_copy(k_top_row[:, :], ps_b[:, 0:P]))
            nc.vector.tensor_tensor(keys, keys, k_top_row[:, :].unsqueeze(1).to_broadcast([P, NT, P]), ALU.subtract).then_inc(k_shifted, 1)
            dve.wait_ge(q_exp, 1)
            link(nc.vector.tensor_reduce(q_sum[:, :], q_heads, AX.X, ALU.add))
            link(nc.vector.reciprocal(q_sum[:, :], q_sum[:, :]))
            dve.wait_ge(mem_turned, 1)
            dve.wait_ge(masks_ready, 4)
            nc.vector.tensor_copy(mem_kt[:, :], ps_a[0:MEM, P:2 * P])
            nc.vector.tensor_copy(mem_vt[:, 0:P], ps_a[0:MEM, 2 * P:3 * P]).then_inc(mem_ready, 1)
            dve.wait_ge(context_done, 1)
            link(nc.vector.reciprocal(k_total[:, :], ps_c[:, P:P + 1]))
            link(nc.vector.tensor_scalar(k_total[:, :], k_total[:, :], float(MD) ** -0.5, None, ALU.mult))
            nc.vector.scalar_tensor_tensor(context[:, :], ps_c[:, 0:P], k_total[:, 0:1], same_head[:, :], ALU.mult, ALU.mult).then_inc(ctx_ready, 1)
            dve.wait_ge(ctx_turned, 1)
            nc.vector.tensor_copy(context_t[:, :], ps_b[:, P:2 * P]).then_inc(ctx_t_ready, 1)
            dve.wait_ge(mixed, 1)
            nc.vector.tensor_copy(mixer[:, :], ps_a[:, 0:C]).then_inc(mixer_ready, 1)
            dve.sem_inc(qn_turned, G)
            with dve.Fori(0, NT // G) as it:
                for g in range(G):
                    t = it * G + g
                    dve.wait_ge(qn_turned, t + 1)
                    nc.vector.tensor_tensor(q_norm[:, g, :].rearrange("p (a h d) -> p a h d", a=1, d=MD), q_heads[:, bass.ds(t, 1)],
                                            q_sum[:, bass.ds(t * MH, MH)].rearrange("p (a h) -> p a h", a=1).unsqueeze(3)
                                            .to_broadcast([P, 1, MH, MD]), ALU.mult).then_inc(qn_ready, 1)
            nc.vector.tensor_scalar(rstd_1[:, :], k.rstd[:, :], 1.0, None, ALU.add).then_inc(scale_ready, 1)
            dve.wait_ge(roots, 1)
            link(nc.vector.tensor_scalar(out_norm[:, :], out_norm[:, :], 1e-12, 1.0 / 16.0, ALU.max, ALU.mult))
            link(nc.vector.reciprocal(out_norm[:, :], out_norm[:, :]))
            dve.sem_inc(base_ready, G)
            for g in range(G):
                dve.sem_inc(base_out[g], 16)
            with dve.Fori(0, NT // G) as it:
                for g in range(G):
                    t = it * G + g
                    dve.wait_ge(base_out[g], it * 16 + 16)
                    nc.vector.scalar_tensor_tensor(base[:, g, :], out_raw[:, bass.ds(t, 1), :], out_norm[:, bass.ds(t, 1)],
                                                   g_out[:, :], ALU.mult, ALU.mult).then_inc(base_step, 1)
                    dve.wait_ge(xn_ready, t + 1)
                    dve.wait_ge(base_step, t * 2 + 1)
                    nc.vector.tensor_tensor(base[:, g, :], base[:, g, :], xn[:, g, :], ALU.add).then_inc(base_step, 1)
                    dve.wait_ge(base_step, t * 2 + 2)
                    nc.vector.tensor_tensor(base[:, g, :], base[:, g, :], bias[:, :], ALU.add).then_inc(base_ready, 1)

        @block.scalar
        def _(act):
            act.sem_inc(exp_used, 4)
            act.sem_inc(out_copied, 2)
            act.sem_inc(squared, 2)
            act.wait_ge(q_shifted, 1)
            nc.scalar.activation(k.qkv[:, :, 0:MHID], k.qkv[:, :, 0:MHID], ACT.Exp).then_inc(q_exp, 1)
            act.wait_ge(top_ready, 1)
            nc.scalar.activation(mem_k[:, :], mem_k[:, :], ACT.Exp, bias=k_top[:, 3:4]).then_inc(mem_exp, 1)
            act.wait_ge(k_shifted, 1)
            nc.scalar.activation(exp_k[:, 0, :], keys[:, 0, :], ACT.Exp).then_inc(exp_ready, 1)
            with act.Fori(0, (NT - 1) // 4) as it:
                for g in range(4):
                    act.wait_ge(exp_used, it * 4 + (g + 2))
                    nc.scalar.activation(exp_k[:, (g + 1) % 4, :], keys[:, bass.ds(it * 4 + (g + 1), 1), :], ACT.Exp).then_inc(exp_ready, 1)
            with act.Fori(0, NT // G) as it:
                for g in range(G + 1):
                    if g < G:
                        act.wait_ge(qn_turned, it * G + (g + 1 + G))
                        nc.scalar.copy(q_t[:, g % 2, :], ps_qt[g % 2][:, 0:P]).then_inc(qt_ready, 1)
                    if g >= 1:
                        b = g - 1
                        t = it * G + b
                        act.wait_ge(out_done, t + 1)
                        nc.scalar.copy(out_raw[:, bass.ds(t, 1), :], ps_o[b % 2][:, 0:C]).then_inc(out_copied, 1)
                        act.wait_ge(squared, t + (2 if b else 2))
                        nc.scalar.activation(squares[:, b % 2, :], ps_o[b % 2][:, 0:C], ACT.Square,
                                             accum_out=out_norm[:, bass.ds(t, 1)]).then_inc(squared, 1)
            act.wait_ge(squared, NT + 2)
            nc.scalar.activation(out_norm[:, :], out_norm[:, :], ACT.Sqrt).then_inc(roots, 1)
            act.wait_ge(scale_ready, 1)
            with act.Fori(0, NT // G) as it:
                for g in range(G):
                    t = it * G + g
                    act.wait_ge(base_ready, t + 1)
                    nc.scalar.activation(xn[:, g, :], k.x_res[:, bass.ds(t, 1), :], ACT.Identity, scale=rstd_1[:, bass.ds(t, 1)],
                                         bias=k.shift[:, bass.ds(t, 1)]).then_inc(xn_ready, 1)

        @block.tensor
        def _(pe):
            pe.wait_ge(kmax_ready, 1)
            nc.tensor.transpose(ps_a[:, 0:P], k_max[:, :], k.ident[:, :]).then_inc(kmax_turned, 1)
            pe.wait_ge(top_ready, 1)
            nc.tensor.matmul(ps_b[:, 0:P], k_top_b[:, :], k.ident[:, :], start=True, stop=True).then_inc(top_spread, 1)
            pe.wait_ge(mem_exp, 1)
            nc.tensor.transpose(ps_a[0:MEM, P:2 * P], mem_k[:, :], k.ident[:, :])
            nc.tensor.transpose(ps_a[0:MEM, 2 * P:3 * P], mem_v[:, :], k.ident[:, :]).then_inc(mem_turned, 1)
            pe.wait_ge(masks_ready, 4)
            pe.wait_ge(exp_ready, 1)
            nc.tensor.matmul(ps_c[:, 0:P + 1], exp_k[:, 0, :], k.qkv[:, 0, 2 * MHID:QW + 1], start=True, stop=False).then_inc(exp_used, 1)
            with pe.Fori(0, (NT - 1) // 4) as it:
                for g in range(4):
                    pe.wait_ge(exp_ready, it * 4 + (g + 2))
                    nc.tensor.matmul(ps_c[:, 0:P + 1], exp_k[:, (g + 1) % 4, :], k.qkv[:, bass.ds(it * 4 + (g + 1), 1), 2 * MHID:QW + 1],
                                     start=False, stop=False).then_inc(exp_used, 1)
            pe.wait_ge(mem_ready, 1)
            nc.tensor.matmul(ps_c[:, 0:P + 1], mem_kt[:, :], mem_vt[:, :], start=False, stop=True).then_inc(context_done, 1)
            pe.wait_ge(ctx_ready, 1)
            nc.tensor.transpose(ps_b[:, P:2 * P], context[:, :], k.ident[:, :]).then_inc(ctx_turned, 1)
            pe.wait_ge(ctx_t_ready, 1)
            nc.tensor.matmul(ps_a[:, 0:C], context_t[:, :], w_out[:, :], start=True, stop=True).then_inc(mixed, 1)
            pe.wait_ge(mixer_ready, 1)
            with pe.Fori(0, NT // G) as it:
                for g in range(G + 1):
                    if g < G:
                        pe.wait_ge(qn_ready, it * G + (g + 1))
                        if g >= 2:
                            pe.wait_ge(qt_ready, it * G + (g - 1))
                        nc.tensor.transpose(ps_qt[g % 2][:, 0:P], q_norm[:, g, :], k.ident[:, :]).then_inc(qn_turned, 1)
                    if g >= 1:
                        b = g - 1
                        t = it * G + b
                        back = 2 if b else 1
                        pe.wait_ge(qt_ready, t + 1)
                        pe.wait_ge(squared, t + (3 - back))
                        pe.wait_ge(out_copied, t + (3 - back))
                        nc.tensor.matmul(ps_o[b % 2][:, 0:C], q_t[:, b % 2, :], mixer[:, :], start=True, stop=False)
                        nc.tensor.matmul(ps_o[b % 2][:, 0:C], ones_row[:, :], b_out[:, :], start=False, stop=True).then_inc(out_done, 1)


def gate_and_dispatch(nc, k):
    with ExitStack() as ctx:
        sb, ps, sem = allocators(nc, ctx)
        x1 = sb("x1", [P, NT, C])
        den = sb("den", [P, NT * H])
        stats = sb("stats2", [P, NT, 6])
        mv = sb("mv2", [P, NT, 2])
        std = sb("std2", [P, NT])
        rstd = sb("rstd2", [P, NT])
        shift = sb("shift2", [P, NT])
        wg_in = sb("wg_in", [NE, C])
        wg_t = sb("wg_t", [P, 2, NE])
        bg_in = sb("bg_in", [1, NE])
        ones = sb("ones_sq", [P, P])
        before = sb("before", [P, P])
        y = sb("y", [P, G, C])
        y_t = sb("y_t", [P, 2, 2, P])
        score = sb("score", [P, NT, NE])
        score2 = sb("score2", [P, NT, NE])
        expert_i = sb("expert_i", [P, NT, NE], I32)
        expert_no = sb("expert_no", [P, NT, NE])
        cand = sb("cand", [P, NT, NE])
        first = sb("first", [P, NT, NE])
        second = sb("second", [P, NT, NE])
        both = sb("both", [P, NT, NE])
        top = sb("top", [P, 2, NT])
        which = sb("which", [P, NT])
        gap = sb("gap", [P, NT])
        totals = sb("totals", [P, NT, NE])
        upto = sb("upto", [P, NT, NE])
        place = sb("place", [P, NT, NE])
        count_i = sb("count_i", [P, NE], I32)
        padded = sb("padded_count", [P, NE])
        ends = sb("ends", [P, NE])
        starts = sb("starts", [P, NE])
        block_i = sb("block_i", [P, NB, NE], I32)
        block_no = sb("block_no", [P, NB, NE])
        expert_f = sb("expert_f", [P, NB])
        place_f = sb("place_f", [P, 2, NT])
        place_idx = [sb(f"place_idx{g}", [P, 2], U32) for g in range(G)]
        ps_w = ps("g_ps_w", [P, 512])
        ps_t = [ps(f"g_ps_t{i}", [P, 512]) for i in range(2)]
        ps_s = [ps(f"g_ps_s{i}", [P, 512]) for i in range(2)]
        ps_before = ps("ps_before", [P, 512])
        ps_total = ps("ps_total", [P, 512])
        base_in, w_in, consts_ready, dve_step, pool_step = sem("base_in"), sem("g_w_in"), sem("g_consts"), sem("g_dve_step"), sem("g_pool_step")
        x1_ready, x1_out, stat_steps, moments_ready, std_ready, rstd_ready = (
            sem("x1_ready"), sem("x1_out"), sem("g_stat_steps"), sem("g_moments"), sem("g_std"), sem("g_rstd"))
        wg_turned, wg_ready, y_ready, y_turned, yt_ready, scored, score_copied = (
            sem("wg_turned"), sem("wg_ready"), sem("y_ready"), sem("y_turned"), sem("yt_ready"), sem("scored"), sem("score_copied"))
        gap_ready, gap_exp, picked, counted, places_ready, row_ready = (
            sem("gap_ready"), sem("gap_exp"), sem("picked"), sem("counted"), sem("places_ready"), sem("row_ready"))
        y2_ready, idx_ready, pool_seen = sem("y2_ready"), sem("g_idx_ready"), sem("g_pool_seen")
        sent = [sem(f"sent{g}") for g in range(G)]
        block = ctx.enter_context(nc.Block())
        sums = k.acc[:, :, :].rearrange("p t (h w) -> p (t h) w", w=HW)

        @block.sync
        def _(sp):
            for t in range(0, NT, G):
                sp.dma_start(x1[:, t:t + G, :], k.base_rows[t * P:(t + G) * P, :].rearrange("(t p) c -> p t c", p=P)).then_inc(base_in, 16)
            sp.dma_start(wg_in[:, :], k.Wg[:, :]).then_inc(w_in, 16)
            sp.dma_start(bg_in[:, :], k.bg.rearrange("(a e) -> a e", a=1)).then_inc(w_in, 16)
            sp.wait_ge(x1_ready, 1)
            for t in range(0, NT, G):
                sp.dma_start(k.x1_rows[t * P:(t + G) * P, :].rearrange("(t p) c -> p t c", p=P), x1[:, t:t + G, :]).then_inc(x1_out, 16)
            sp.wait_ge(x1_out, 16 * (NT // G))

        @block.gpsimd
        def _(pool):
            link = chain(pool, pool_step)
            nc.gpsimd.memset(ones[:, :], 1.0).then_inc(consts_ready, 1)
            link(nc.gpsimd.memset(before[:, :], 1.0))
            nc.gpsimd.affine_select(out=before[:, :], in_=before[:, :], compare_op=ALU.is_gt, fill=0.0, base=0,
                                    pattern=[[1, P]], channel_multiplier=-1).then_inc(consts_ready, 1)
            link(nc.gpsimd.iota(expert_i[:, :, :], [[0, NT], [1, NE]], 0, 0))
            nc.gpsimd.tensor_copy(expert_no[:, :, :], expert_i[:, :, :]).then_inc(consts_ready, 1)
            link(nc.gpsimd.iota(block_i[:, :, :], [[1, NB], [0, NE]], 0, 0))
            nc.gpsimd.tensor_copy(block_no[:, :, :], block_i[:, :, :]).then_inc(consts_ready, 1)
            pool.wait_ge(places_ready, 1)

            def dispatch(it, g):
                t = it * G + g
                nc.gpsimd.tensor_copy(place_idx[g][:, :], k.places[:, :, bass.ds(t, 1)].rearrange("p a t -> p (a t)")).then_inc(idx_ready, 1)
                pool.wait_ge(idx_ready, t + 1)
                pool.wait_ge(y2_ready, t + 1)
                pool.sem_inc(pool_seen, 1)
                for a in range(2):
                    pool.indirect_dma_start(k.list_rows[:, :], bass.IndirectOffsetOnAxis(ap=place_idx[g][:, a:a + 1], axis=0),
                                            y[:, g, :], None).then_inc(sent[g], 16)

            for g in range(G):
                dispatch(0, g)
            with pool.Fori(1, NT // G) as it:
                for g in range(G):
                    pool.wait_ge(sent[g], it * 32)
                    pool.sem_inc(pool_seen, 1)
                    dispatch(it, g)
            for g in range(G):
                pool.wait_ge(sent[g], 32 * (NT // G))

        @block.vector
        def _(dve):
            link = chain(dve, dve_step)
            link(nc.vector.tensor_scalar(den[:, :], sums[:, :, D], 1e-10, None, ALU.max))
            link(nc.vector.reciprocal(den[:, :], den[:, :]))
            link(nc.vector.tensor_tensor(sums[:, :, 0:D], sums[:, :, 0:D], den[:, :].unsqueeze(2).to_broadcast([P, NT * H, D]), ALU.mult))
            dve.wait_ge(base_in, 16 * (NT // G))
            x1_heads = x1[:, :, :].rearrange("p t (h d) -> p (t h) d", d=D)
            link(nc.vector.tensor_tensor(x1_heads, x1_heads, sums[:, :, 0:D], ALU.add))
            dve.sem_inc(x1_ready, 1)
            with dve.Fori(0, NT) as t:
                nc.vector.bn_stats(stats[:, bass.ds(t, 1), :], x1[:, bass.ds(t, 1), :]).then_inc(stat_steps, 1)
            dve.wait_ge(stat_steps, NT)
            moments(nc, link, stats, mv, moments_ready)
            dve.wait_ge(moments_ready, 1)
            dve.wait_ge(std_ready, 1)
            link(nc.vector.reciprocal(rstd[:, :], std[:, :]))
            nc.vector.scalar_tensor_tensor(shift[:, :], mv[:, :, 0], -1.0, rstd[:, :], ALU.mult, ALU.mult).then_inc(rstd_ready, 1)
            dve.wait_ge(wg_turned, 1)
            nc.vector.tensor_copy(wg_t[:, :, :], ps_w[:, 0:2 * NE].rearrange("p (a e) -> p a e", a=2)).then_inc(wg_ready, 1)
            dve.sem_inc(score_copied, 2)
            with dve.Fori(0, NT // G) as it:
                for g in range(G):
                    t = it * G + g
                    dve.wait_ge(scored, t + 1)
                    nc.vector.tensor_copy(score[:, bass.ds(t, 1), :], ps_s[g % 2][:, 0:NE]).then_inc(score_copied, 1)
            dve.wait_ge(score_copied, NT + 2)
            dve.wait_ge(consts_ready, 4)

            def across(ap):
                return ap.unsqueeze(2).to_broadcast([P, NT, NE])

            for n, (s, hot) in enumerate(((score, first), (score2, second))):
                link(nc.vector.tensor_reduce(top[:, n, :], s[:, :, :], AX.X, ALU.max))
                link(nc.vector.tensor_tensor(cand[:, :, :], s[:, :, :], across(top[:, n, :]), ALU.is_equal))
                link(nc.vector.tensor_scalar(cand[:, :, :], cand[:, :, :], -100.0, None, ALU.mult))
                link(nc.vector.tensor_tensor(cand[:, :, :], cand[:, :, :], expert_no[:, :, :], ALU.add))
                link(nc.vector.tensor_reduce(which[:, :], cand[:, :, :], AX.X, ALU.min))
                link(nc.vector.tensor_scalar(which[:, :], which[:, :], 100.0, None, ALU.add))
                link(nc.vector.tensor_tensor(hot[:, :, :], expert_no[:, :, :], across(which[:, :]), ALU.is_equal))
                if n == 0:
                    link(nc.vector.tensor_scalar(cand[:, :, :], hot[:, :, :], -BIG, None, ALU.mult))
                    link(nc.vector.tensor_tensor(score2[:, :, :], score[:, :, :], cand[:, :, :], ALU.add))
            nc.vector.tensor_tensor(gap[:, :], top[:, 1, :], top[:, 0, :], ALU.subtract).then_inc(gap_ready, 1)
            nc.vector.tensor_tensor(both[:, :, :], first[:, :, :], second[:, :, :], ALU.add).then_inc(picked, 1)
            dve.wait_ge(gap_exp, 1)
            link(nc.vector.tensor_scalar(k.weights[:, 0, :], gap[:, :], 1.0, None, ALU.add))
            link(nc.vector.reciprocal(k.weights[:, 0, :], k.weights[:, 0, :]))
            link(nc.vector.tensor_tensor(k.weights[:, 1, :], k.weights[:, 0, :], gap[:, :], ALU.mult))
            dve.wait_ge(counted, 1)
            link(nc.vector.tensor_copy(totals[:, :, :], ps_total[:, 0:NT * NE].rearrange("p (t e) -> p t e", e=NE)))
            for e in range(NE):
                link(nc.vector.tensor_tensor_scan(upto[:, :, e], ones[:, 0:NT], totals[:, :, e], 0.0, ALU.mult, ALU.add))
            link(nc.vector.tensor_scalar(count_i[:, :], upto[:, NT - 1, :], float(P - 1), None, ALU.add))
            link(nc.vector.tensor_scalar(count_i[:, :], count_i[:, :], 7, None, ALU.arith_shift_right))
            link(nc.vector.tensor_copy(padded[:, :], count_i[:, :]))
            link(nc.vector.tensor_tensor_scan(ends[:, :], ones[:, 0:NE], padded[:, :], 0.0, ALU.mult, ALU.add))
            link(nc.vector.tensor_tensor(starts[:, :], ends[:, :], padded[:, :], ALU.subtract))
            link(nc.vector.tensor_scalar(starts[:, :], starts[:, :], float(P), None, ALU.mult))
            link(nc.vector.tensor_tensor(upto[:, :, :], upto[:, :, :], totals[:, :, :], ALU.subtract))
            link(nc.vector.tensor_tensor(upto[:, :, :], upto[:, :, :], starts[:, :].unsqueeze(1).to_broadcast([P, NT, NE]), ALU.add))
            link(nc.vector.tensor_tensor(upto[:, :, :], upto[:, :, :], ps_before[:, 0:NT * NE].rearrange("p (t e) -> p t e", e=NE), ALU.add))
            for n, hot in enumerate((first, second)):
                link(nc.vector.tensor_tensor(place[:, :, :], upto[:, :, :], hot[:, :, :], ALU.mult))
                link(nc.vector.tensor_reduce(place_f[:, n, :], place[:, :, :], AX.X, ALU.add))
            nc.vector.tensor_copy(k.places[:, :, :], place_f[:, :, :]).then_inc(places_ready, 1)
            link(nc.vector.tensor_tensor(block_no[:, :, :], block_no[:, :, :], ends[:, :].unsqueeze(1).to_broadcast([P, NB, NE]), ALU.is_ge))
            link(nc.vector.tensor_reduce(expert_f[:, :], block_no[:, :, :], AX.X, ALU.add))
            link(nc.vector.tensor_scalar(expert_f[:, :], expert_f[:, :], float(NE - 1), None, ALU.min))
            link(nc.vector.tensor_copy(k.expert_row[:, :], expert_f[0:1, :]))

        @block.scalar
        def _(act):
            act.wait_ge(moments_ready, 1)
            nc.scalar.activation(std[:, :], mv[:, :, 1], ACT.Sqrt, bias=k.eps[:, 0:1]).then_inc(std_ready, 1)
            act.wait_ge(rstd_ready, 1)
            act.sem_inc(y_turned, G)
            with act.Fori(0, NT // G) as it:
                for g in range(G):
                    t = it * G + g
                    act.wait_ge(y_turned, t + 1)
                    nc.scalar.activation(y[:, g, :], x1[:, bass.ds(t, 1), :], ACT.Identity, scale=rstd[:, bass.ds(t, 1)],
                                         bias=shift[:, bass.ds(t, 1)]).then_inc(y_ready, 1)
                    act.wait_ge(y_turned, t + (1 + G))
                    nc.scalar.copy(y_t[:, g % 2].rearrange("p a n -> p (a n)"), ps_t[g % 2][:, 0:C]).then_inc(yt_ready, 1)
            act.wait_ge(gap_ready, 1)
            nc.scalar.activation(gap[:, :], gap[:, :], ACT.Exp).then_inc(gap_exp, 1)
            act.wait_ge(y_turned, NT + G)

            def normed(it, g):
                t = it * G + g
                nc.scalar.activation(y[:, g, :], x1[:, bass.ds(t, 1), :], ACT.Identity, scale=rstd[:, bass.ds(t, 1)],
                                     bias=shift[:, bass.ds(t, 1)]).then_inc(y2_ready, 1)

            for g in range(G):
                normed(0, g)
            with act.Fori(1, NT // G) as it:
                for g in range(G):
                    act.wait_ge(sent[g], it * 32)
                    normed(it, g)

        @block.tensor
        def _(pe):
            pe.wait_ge(w_in, 32)
            for a in range(2):
                last = nc.tensor.transpose(ps_w[:, NE * a:NE * (a + 1)], wg_in[:, a * P:(a + 1) * P], k.ident[0:NE, 0:NE])
            last.then_inc(wg_turned, 1)
            pe.wait_ge(wg_ready, 1)
            pe.wait_ge(consts_ready, 2)
            with pe.Fori(0, NT // G) as it:
                for g in range(G + 1):
                    if g < G:
                        pe.wait_ge(y_ready, it * G + (g + 1))
                        if g >= 2:
                            pe.wait_ge(yt_ready, it * G + (g - 1))
                        for a in range(2):
                            last = nc.tensor.transpose(ps_t[g % 2][:, a * P:(a + 1) * P], y[:, g, a * P:(a + 1) * P], k.ident[:, :])
                        last.then_inc(y_turned, 1)
                    if g >= 1:
                        b = g - 1
                        t = it * G + b
                        pe.wait_ge(yt_ready, t + 1)
                        pe.wait_ge(score_copied, t + (1 if b else 2))
                        for a in range(2):
                            nc.tensor.matmul(ps_s[b % 2][:, 0:NE], y_t[:, b % 2, a, :], wg_t[:, a, :], start=a == 0, stop=False)
                        nc.tensor.matmul(ps_s[b % 2][:, 0:NE], ones[0:1, :], bg_in[:, :], start=False, stop=True).then_inc(scored, 1)
            pe.wait_ge(picked, 1)
            flat = both[:, :, :].rearrange("p t e -> p (t e)")
            nc.tensor.matmul(ps_before[:, 0:NT * NE], before[:, :], flat, start=True, stop=True)
            nc.tensor.matmul(ps_total[:, 0:NT * NE], ones[:, :], flat, start=True, stop=True).then_inc(counted, 1)


def expert_weights(nc, k):
    with ExitStack() as ctx:
        sb, ps, sem = allocators(nc, ctx)
        w1_in = [sb(f"w1_in{s}", [P, 8, C]) for s in range(2)]
        w2_in = [sb(f"w2_in{s}", [P, 2, HID]) for s in range(2)]
        b_in_sb = sb("b_in_sb", [BROWS, P])
        b_rest = sb("b_rest", [BROWS, P])
        b_parts = sb("b_parts", [BROWS, 3, P], BF16)
        ps_a = [ps(f"w_ps_a{i}", [P, 512]) for i in range(4)]
        ps_d = [ps(f"w_ps_d{i}", [P, 512]) for i in range(4)]
        w_in = [sem(f"ew_in{s}") for s in range(2)]
        turned_a, turned_d, copied_a, copied_d = sem("turned_a"), sem("turned_d"), sem("copied_a"), sem("copied_d")
        b_in, b_split, b_out, dve_step = sem("b_in"), sem("b_split"), sem("b_out"), sem("w_dve_step")
        block = ctx.enter_context(nc.Block())

        @block.sync
        def _(sp):
            sp.dma_start(b_in_sb[0:NE * HID // P, :], k.b1.rearrange("e (i p) -> (e i) p", p=P)).then_inc(b_in, 16)
            sp.dma_start(b_in_sb[NE * HID // P:BROWS, :], k.b2.rearrange("e (i p) -> (e i) p", p=P)).then_inc(b_in, 16)
            with sp.Fori(0, NE // 2) as it:
                for s in range(2):
                    e = it * 2 + s
                    sp.wait_ge(w_in[s], it * 32 + 1)
                    sp.wait_ge(turned_a, e * 4 + 4)
                    sp.wait_ge(turned_d, e * 4 + 4)
                    sp.dma_start(w1_in[s][:, :, :], k.W1[bass.ds(e, 1), :, :].rearrange("e (i p) c -> p (e i) c", p=P)).then_inc(w_in[s], 16)
                    sp.dma_start(w2_in[s][:, :, :], k.W2[bass.ds(e, 1), :, :].rearrange("e (i p) c -> p (e i) c", p=P)).then_inc(w_in[s], 16)
            sp.wait_ge(b_split, 1)
            sp.dma_start(k.bias_rows.rearrange("j (r p) -> r j p", p=P), b_parts[:, :, :]).then_inc(b_out, 16)
            sp.wait_ge(b_out, 16)
            sp.dma_start(k.biases[:, :], k.bias_rows[:, :]).then_inc(b_out, 16)
            sp.wait_ge(b_out, 32)

        @block.tensor
        def _(pe):
            with pe.Fori(0, NE // 2) as it:
                for s in range(2):
                    e = it * 2 + s
                    pe.wait_ge(w_in[s], it * 32 + 33)
                    for n in range(4):
                        pe.wait_ge(copied_a, e * 4 + (n + 1))
                        for i in range(4):
                            a, chunk = n // 2, (n % 2) * 4 + i
                            last = nc.tensor.transpose(ps_a[n][:, i * P:(i + 1) * P], w1_in[s][:, chunk, a * P:(a + 1) * P], k.ident[:, :])
                        last.then_inc(turned_a, 1)
                        pe.wait_ge(copied_d, e * 4 + (n + 1))
                        for i in range(4):
                            chunk, a = n * 2 + i // 2, i % 2
                            last = nc.tensor.transpose(ps_d[n][:, i * P:(i + 1) * P], w2_in[s][:, a, chunk * P:(chunk + 1) * P], k.ident[:, :])
                        last.then_inc(turned_d, 1)

        @block.scalar
        def _(act):
            act.sem_inc(w_in[0], 1)
            act.sem_inc(w_in[1], 1)
            act.sem_inc(turned_a, 8)
            act.sem_inc(copied_a, 4)
            with act.Fori(0, NE) as e:
                for n in range(4):
                    act.wait_ge(turned_a, e * 4 + (n + 9))
                    nc.scalar.copy(k.w1_t[:, bass.ds(e * 4 + n, 1), :], ps_a[n][:, :]).then_inc(copied_a, 1)

        @block.vector
        def _(dve):
            link = chain(dve, dve_step)
            dve.wait_ge(b_in, 32)
            link(nc.vector.tensor_copy(b_parts[:, 0, :], b_in_sb[:, :]))
            link(nc.vector.tensor_tensor(b_rest[:, :], b_in_sb[:, :], b_parts[:, 0, :], ALU.subtract))
            link(nc.vector.tensor_copy(b_parts[:, 1, :], b_rest[:, :]))
            nc.vector.tensor_tensor(b_parts[:, 2, :], b_rest[:, :], b_parts[:, 1, :], ALU.subtract).then_inc(b_split, 1)
            dve.sem_inc(turned_d, 8)
            dve.sem_inc(copied_d, 4)
            with dve.Fori(0, NE) as e:
                for n in range(4):
                    dve.wait_ge(turned_d, e * 4 + (n + 9))
                    nc.vector.tensor_copy(k.w2_t[:, bass.ds(e * 4 + n, 1), :], ps_d[n][:, :]).then_inc(copied_d, 1)


def experts(nc, k):
    with ExitStack() as ctx:
        sb, ps, sem = allocators(nc, ctx)
        rows = [sb(f"e_rows{s}", [P, C]) for s in range(2)]
        rows_t = [sb(f"e_rows_t{s}", [P, C]) for s in range(2)]
        hidden = sb("hidden", [P, HID])
        hidden_t = sb("hidden_t", [P, 8, P])
        out = [sb(f"e_out{s}", [P, C]) for s in range(2)]
        ones = sb("e_ones", [3, P], BF16)
        ps_x = ps("e_ps_x", [P, 512])
        ps_h = [ps(f"e_ps_h{i}", [P, 512]) for i in range(2)]
        ps_ht = [ps(f"e_ps_ht{i}", [P, 512]) for i in range(2)]
        ps_y = ps("e_ps_y", [P, 512])
        rows_in = [sem(f"e_rows_in{s}") for s in range(2)]
        out_sent = [sem(f"e_out_sent{s}") for s in range(2)]
        turned, xt_ready, h_done = sem("e_turned"), sem("e_xt_ready"), sem("e_h_done")
        relu_a, relu_d, ht_done, ht_a, ht_d, y_done, y_copied, set_up = (
            sem("relu_a"), sem("relu_d"), sem("ht_done"), sem("ht_a"), sem("ht_d"), sem("y_done"), sem("y_copied"), sem("e_set_up"))
        pool_seen = sem("e_pool_seen")
        block = ctx.enter_context(nc.Block())
        pairs = (NB - 2) // 2

        @block.sync
        def _(sp):
            for i in range(2):
                sp.dma_start(rows[i][:, :], k.list_rows[i * P:(i + 1) * P, :]).then_inc(rows_in[i], 16)
            with sp.Fori(0, pairs) as it:
                for s in range(2):
                    i = it * 2 + (2 + s)
                    sp.wait_ge(turned, i - 1)
                    sp.dma_start(rows[s][:, :], k.list_rows[bass.ds(i * P, P), :]).then_inc(rows_in[s], 16)

        @block.gpsimd
        def _(pool):
            with pool.Fori(0, pairs) as it:
                for s in range(2):
                    i = it * 2 + s
                    pool.wait_ge(y_copied, i + 2)
                    pool.sem_inc(pool_seen, 1)
                    pool.dma_start(k.expert_out[bass.ds(i * P, P), :], out[s][:, :]).then_inc(out_sent[s], 16)
            last = NB - 2
            pool.wait_ge(y_copied, last + 2)
            pool.dma_start(k.expert_out[last * P:(last + 1) * P, :], out[0][:, :]).then_inc(out_sent[0], 16)
            pool.wait_ge(out_sent[0], 16 * (pairs + 1))
            pool.wait_ge(out_sent[1], 16 * pairs)

        def turn(pe, s, i, n):
            pe.wait_ge(rows_in[s], n * 16)
            pe.wait_ge(xt_ready, i + 1)
            for a in range(2):
                last = nc.tensor.transpose(ps_x[:, a * P:(a + 1) * P], rows[s][:, a * P:(a + 1) * P], k.ident[:, :])
            last.then_inc(turned, 1)

        def up(pe, s, i, e):
            pe.wait_ge(xt_ready, i + 2)
            pe.wait_ge(relu_a, i + 1)
            pe.wait_ge(relu_d, i + 1)
            for n in range(2):
                nc.tensor.matmul(ps_h[n][:, :], ones[:, :], k.biases[:, bass.ds(e * HID + n * 512, 512)], start=True, stop=False)
                for a in range(2):
                    last = nc.tensor.matmul(ps_h[n][:, :], rows_t[s][:, a * P:(a + 1) * P],
                                            k.w1_t[:, bass.ds(e * 4 + (2 * a + n), 1), :], start=False, stop=a == 1)
                last.then_inc(h_done, 1)

        def turn_hidden(pe, i):
            for n in range(2):
                pe.wait_ge((relu_a, relu_d)[n], i + 2)
                pe.wait_ge((ht_a, ht_d)[n], i + 1)
                for m in range(4):
                    last = nc.tensor.transpose(ps_ht[n][:, m * P:(m + 1) * P], hidden[:, (4 * n + m) * P:(4 * n + m + 1) * P], k.ident[:, :])
                last.then_inc(ht_done, 1)

        def down(pe, i, e):
            pe.wait_ge(y_copied, i + 1)
            nc.tensor.matmul(ps_y[:, 0:C], ones[:, :], k.biases[:, bass.ds(e * C + NE * HID, C)], start=True, stop=False)
            for m in range(8):
                if m % 4 == 0:
                    pe.wait_ge((ht_a, ht_d)[m // 4], i + 2)
                last = nc.tensor.matmul(ps_y[:, 0:C], hidden_t[:, m, :],
                                        k.w2_t[:, bass.ds(e * 4 + m // 2, 1), (m % 2) * C:(m % 2 + 1) * C], start=False, stop=m == 7)
            last.then_inc(y_done, 1)

        @block.tensor
        def _(pe):
            pe.wait_ge(set_up, 1)
            turn(pe, 0, 0, 1)
            turn(pe, 1, 1, 1)
            e = pe.value_load(k.expert_row[0:1, 0:1], min_val=0, max_val=NE - 1)
            up(pe, 0, 0, e)
            turn_hidden(pe, 0)
            with pe.Fori(0, pairs) as it:
                for s in range(2):
                    i = it * 2 + (1 + s)
                    e = pe.value_load(k.expert_row[0:1, bass.ds(i, 1)], min_val=0, max_val=NE - 1)
                    before = pe.value_load(k.expert_row[0:1, bass.ds(i - 1, 1)], min_val=0, max_val=NE - 1)
                    turn(pe, s, i + 1, it + 2)
                    up(pe, (1 + s) % 2, i, e)
                    down(pe, i - 1, before)
                    turn_hidden(pe, i)
            e = pe.value_load(k.expert_row[0:1, NB - 2:NB - 1], min_val=0, max_val=NE - 1)
            down(pe, NB - 2, e)

        def rows_copy(act, s, i):
            act.wait_ge(turned, i + 1)
            act.wait_ge(h_done, 2 * i + 1)
            nc.scalar.copy(rows_t[s][:, :], ps_x[:, 0:C]).then_inc(xt_ready, 1)

        def out_copy(act, s, i, n):
            act.wait_ge(y_done, i + 1)
            if n is not None:
                act.wait_ge(out_sent[s], n * 16)
            nc.scalar.copy(out[s][:, :], ps_y[:, 0:C]).then_inc(y_copied, 1)

        def relu_first(act, i):
            act.wait_ge(h_done, 2 * i + 4)
            nc.scalar.activation(hidden[:, 0:512], ps_h[0][:, :], ACT.Relu).then_inc(relu_a, 1)

        def hidden_copy(act, i):
            act.wait_ge(ht_done, 2 * i + 1)
            nc.scalar.copy(hidden_t[:, 0:4, :].rearrange("p m n -> p (m n)"), ps_ht[0][:, :]).then_inc(ht_a, 1)

        @block.scalar
        def _(act):
            act.sem_inc(xt_ready, 1)
            act.sem_inc(relu_a, 1)
            act.sem_inc(relu_d, 1)
            act.sem_inc(ht_a, 1)
            act.sem_inc(ht_d, 1)
            act.sem_inc(y_copied, 1)
            act.sem_inc(h_done, 3)
            rows_copy(act, 0, 0)
            rows_copy(act, 1, 1)
            relu_first(act, 0)
            hidden_copy(act, 0)

            def turn_of_two(it, n):
                for s in range(2):
                    i = it * 2 + (1 + s)
                    rows_copy(act, s, i + 1)
                    relu_first(act, i)
                    out_copy(act, s, i - 1, n)
                    hidden_copy(act, i)

            turn_of_two(0, None)
            with act.Fori(1, pairs) as it:
                turn_of_two(it, it)
            out_copy(act, 0, NB - 2, pairs)

        @block.vector
        def _(dve):
            nc.vector.memset(ones[:, :], 1.0).then_inc(set_up, 1)

            def relu_second(i):
                dve.wait_ge(h_done, 2 * i + 5)
                nc.vector.tensor_scalar(hidden[:, 512:HID], ps_h[1][:, :], 0.0, None, ALU.max).then_inc(relu_d, 1)

            def hidden_copy_second(i):
                dve.wait_ge(ht_done, 2 * i + 2)
                nc.vector.tensor_copy(hidden_t[:, 4:8, :].rearrange("p m n -> p (m n)"), ps_ht[1][:, :]).then_inc(ht_d, 1)

            relu_second(0)
            hidden_copy_second(0)
            with dve.Fori(0, pairs) as it:
                for s in range(2):
                    i = it * 2 + (1 + s)
                    relu_second(i)
                    hidden_copy_second(i)


def combine(nc, k):
    with ExitStack() as ctx:
        sb, ps, sem = allocators(nc, ctx)
        x1 = sb("x1_again", [P, G, C])
        picked = sb("picked_rows", [P, G, 2, C])
        out = sb("out_ring", [P, G, C])
        place_idx = [sb(f"c_place_idx{g}", [P, 2], U32) for g in range(G)]
        x1_in = [sem(f"x1_in{g}") for g in range(G)]
        rows_in = [sem(f"c_rows_in{g}") for g in range(G)]
        out_sent = [sem(f"c_out_sent{g}") for g in range(G)]
        idx_ready, pool_seen, half, added = sem("c_idx_ready"), sem("c_pool_seen"), sem("c_half"), sem("c_added")
        block = ctx.enter_context(nc.Block())
        turns = NT // G - 1

        @block.sync
        def _(sp):
            def store(t, it, g, n):
                sp.wait_ge(added, t + (1 + G))
                rows = k.out[bass.ds(t * P, P), :] if n == P else k.out[t * P:t * P + n, :]
                sp.dma_start(rows, out[0:n, g, :]).then_inc(out_sent[g], 16)

            with sp.Fori(0, turns) as it:
                for g in range(G):
                    t = it * G + g
                    sp.wait_ge(added, t + 1)
                    sp.dma_start(x1[:, g, :], k.x1_rows[bass.ds(t * P, P), :]).then_inc(x1_in[g], 16)
                for g in range(G):
                    store(it * G + g, it, g, P)
            for g in range(G):
                t = turns * G + g
                sp.wait_ge(added, t + 1)
                sp.dma_start(x1[:, g, :], k.x1_rows[t * P:(t + 1) * P, :]).then_inc(x1_in[g], 16)
            for g in range(G):
                t = turns * G + g
                store(t, turns, g, P if t < NT - 1 else NLAST)
            for g in range(G):
                sp.wait_ge(out_sent[g], 16 * (NT // G + 1))

        @block.gpsimd
        def _(pool):
            with pool.Fori(0, NT // G) as it:
                for g in range(G):
                    t = it * G + g
                    pool.wait_ge(added, t + 1)
                    pool.sem_inc(pool_seen, 1)
                    nc.gpsimd.tensor_copy(place_idx[g][:, :], k.places[:, :, bass.ds(t, 1)].rearrange("p a t -> p (a t)")).then_inc(idx_ready, 1)
                    pool.wait_ge(idx_ready, t + 1)
                    pool.sem_inc(pool_seen, 1)
                    for a in range(2):
                        pool.indirect_dma_start(picked[:, g, a, :], None, k.expert_out[:, :],
                                                bass.IndirectOffsetOnAxis(ap=place_idx[g][:, a:a + 1], axis=0)).then_inc(rows_in[g], 16)

        @block.vector
        def _(dve):
            dve.sem_inc(added, G)
            for g in range(G):
                dve.sem_inc(out_sent[g], 16)
            with dve.Fori(0, NT // G) as it:
                for g in range(G):
                    t = it * G + g
                    dve.wait_ge(x1_in[g], it * 16 + 16)
                    dve.wait_ge(rows_in[g], it * 32 + 32)
                    dve.wait_ge(out_sent[g], it * 16 + 16)
                    nc.vector.scalar_tensor_tensor(x1[:, g, :], picked[:, g, 0, :], k.weights[:, 0, bass.ds(t, 1)], x1[:, g, :],
                                                   ALU.mult, ALU.add).then_inc(half, 1)
                    dve.wait_ge(half, t + 1)
                    nc.vector.scalar_tensor_tensor(out[:, g, :], picked[:, g, 1, :], k.weights[:, 1, bass.ds(t, 1)], x1[:, g, :],
                                                   ALU.mult, ALU.add).then_inc(added, 1)


def program(nc, k):
    with ExitStack() as ctx:
        sb, ps, sem = allocators(nc, ctx)
        dram = lambda name, shape, dt=F32: nc.dram_tensor(name, shape, dt, kind="Internal").ap()
        k.dst_rows = dram("dst_rows", [EROWS, P], I32)
        k.src_rows = dram("src_rows", [EROWS, P], I32)
        k.ea_rows = dram("ea_rows", [EROWS, 3 * P])
        k.nt_list = dram("nt_list", [VPAD], I32)
        k.local_rows = dram("local_rows", [VPAD, P], BF16)
        k.key_rows = dram("key_rows", [VPAD, P])
        k.ea_parts = dram("ea_part_rows", [9, VPAD, P], BF16)
        k.ew_rows = dram("ew_rows", [3, 3, ROW], BF16)
        k.eb_rows = dram("eb_rows", [3, ROW], BF16)
        k.h_rows = dram("h_rows", [NPAD, ROW])
        k.hd_parts = dram("hd_part_rows", [NPAD, 3 * ROW], BF16)
        k.chunk_stats = dram("chunk_stats", [P, 4])
        k.src_logits = dram("src_logits", [NPAD, H])
        k.base_rows = dram("base_rows", [NPAD, C])
        k.x1_rows = dram("x1_rows", [NPAD, C])
        k.bias_rows = dram("bias_rows", [3, BROWS * P], BF16)
        k.list_rows = dram("list_rows", [NB * P, C])
        k.expert_out = dram("expert_out", [(NB - 1) * P, C])

        k.ident = sb("ident", [P, P])
        k.zero = sb("zero", [P, 1])
        k.eps = sb("eps", [P, 1])
        k.iota_row = sb("iota_row", [P, P])
        k.iota_col = sb("iota_col", [P, 1])
        k.enc_w = sb("enc_w", [30, ROW], BF16)
        k.nt_words = sb("nt_words", [1, VPAD // 4], I32)
        k.places = sb("places", [P, 2, NT], U32)
        k.weights = sb("weights", [P, 2, NT])
        k.expert_row = sb("expert_row", [1, NB], I32)
        constants(nc, k)
        with ExitStack() as edges:
            k.local_col = edges.enter_context(nc.sbuf_tensor("local_col", [P, VPAD], F32))
            k.src_col = edges.enter_context(nc.sbuf_tensor("src_col", [P, VPAD], U32))
            edge_tables(nc, k)
            k.src_all = edges.enter_context(nc.sbuf_tensor("src_all", [P, V, H], F32))
            with ExitStack() as nodes:
                k.rstd = nodes.enter_context(nc.sbuf_tensor("rstd", [P, NT], F32))
                k.shift = nodes.enter_context(nc.sbuf_tensor("shift", [P, NT], F32))
                k.norm = nodes.enter_context(nc.sbuf_tensor("norm", [P, NT], F32))
                k.x_res = nodes.enter_context(nc.sbuf_tensor("x_res", [P, NT, C], F32))
                k.qkv = nodes.enter_context(nc.sbuf_tensor("qkv", [P, NT, QW + 1], F32))
                node_rows(nc, k)
                linear_attention(nc, k)
            k.alpha = edges.enter_context(nc.sbuf_tensor("alpha", [P, V, H], F32))
            edge_logits(nc, k)
            segment_softmax(nc, k)
            k.acc = edges.enter_context(nc.sbuf_tensor("acc", [P, NT, ROW], F32))
            aggregate(nc, k)
            gate_and_dispatch(nc, k)
        k.w1_t = sb("w1_t", [P, NE * 4, 512])
        k.w2_t = sb("w2_t", [P, NE * 4, 512])
        k.biases = sb("biases", [3, BROWS * P], BF16)
        expert_weights(nc, k)
        experts(nc, k)
        combine(nc, k)


_NAMES = {"x": "x", "src": "src", "dst": "dst", "edge_attr_3": "edge_attr", "L0_gnn_W": "W", "L0_gnn_a_src": "a_src",
          "L0_gnn_a_dst": "a_dst", "L0_gnn_edge_W": "edge_W", "L0_gnn_edge_b": "edge_b", "L0_gnn_bias": "bias",
          "L0_mix_w_qkv": "w_qkv", "L0_mix_mem_kv": "mem_kv", "L0_mix_w_out": "w_out", "L0_mix_b_out": "b_out",
          "L0_mix_g_out": "g_out", "L0_mix_g_pre": "g_pre", "L0_ffn_Wg": "Wg", "L0_ffn_bg": "bg", "L0_ffn_W1": "W1",
          "L0_ffn_b1": "b1", "L0_ffn_W2": "W2", "L0_ffn_b2": "b2"}


def kernel(**inputs):
    import numpy as np
    import concourse.bacc as bacc
    from concourse.bass_utils import run_bass_kernel_spmd as run

    nc = bacc.Bacc("TRN2", target_bir_lowering=False, num_devices=1)
    arrays, k = {}, Ctx()
    for name, short in _NAMES.items():
        a = np.ascontiguousarray(inputs[name])
        arrays["in_" + short] = a
        k.__dict__[short] = nc.dram_tensor("in_" + short, a.shape, mybir.dt.from_np(a.dtype), kind="ExternalInput").ap()
    k.out = nc.dram_tensor("out", (N, C), F32, kind="ExternalOutput").ap()
    program(nc, k)
    r = run(nc, [arrays], core_ids=[0])
    return r.results[0]["out"]
```

```python
from contextlib import ExitStack

import concourse.bass as bass
from concourse import mybir

F32 = mybir.dt.float32
BF16 = mybir.dt.bfloat16
I32 = mybir.dt.int32
U32 = mybir.dt.uint32
ALU = mybir.AluOpType
ACT = mybir.ActivationFunctionType
AX = mybir.AxisListType

P = 128
N, C = 6250, 256
E = 100000
H, D = 8, 32
HW = D + 1
ROW = H * HW
NT = -(-N // P)
NPAD = NT * P
NLAST = N - (NT - 1) * P
ETILES = -(-E // P)
ER = 7
EP = 112
EROWS = EP * ER
EFULL = E // (ER * P)
EREST = E - EFULL * ER * P
CH = 16
CT = -(-(ETILES + NT - 1) // CH)
V = CH * CT
VC = -(-V // P)
VPAD = VC * P
NOWHERE = 7000
BIG = 1e30
EPS = 1e-5
MH, MD, MEM = 4, 32, 4
MHID = MH * MD
QW = 3 * MHID
NE = 8
HID = 1024
B1_ROWS = NE * HID // P
B2_ROWS = NE * C // P
NB = (2 * NPAD + NE * (P - 1)) // P + 1
LW = C + 4
NW = C + 2 * H
BS = 8
NBLK = V // BS
SLOTS = 4
GS = 16
EARLY = 10
G = 7
R = 8
assert NBLK % SLOTS == 0 and V % (2 * GS) == 0 and EARLY % 2 == 0 and (NBLK + SLOTS) * BS <= VPAD
assert NT % G == 0 and NT % R == 1 and V % BS == 0 and ETILES + NT - 1 <= V and ETILES < EROWS


class Ctx:
    pass


def allocators(nc, ctx):
    def sb(name, shape, dt=F32):
        return ctx.enter_context(nc.sbuf_tensor(name, shape, dt))

    def ps(name, shape, dt=F32):
        return ctx.enter_context(nc.psum_tensor(name, shape, dt))

    used = []

    def sem(name):
        used.append(nc.alloc_semaphore(name))
        return used[-1]

    def give_back():
        if used:
            nc.clear_and_free_semaphores(used)
            nc.all_engine_barrier()

    ctx.callback(give_back)
    return sb, ps, sem


def chain(eng, sem):
    count = [0]

    def link(ins):
        count[0] += 1
        ins.then_inc(sem, 1)
        eng.wait_ge(sem, count[0])

    return link


def node_tiles(eng, k, j):
    words = [eng.value_load(k.nt_words[0:1, bass.ds(j * (BS // 4) + w, 1)]) for w in range(BS // 4)]
    return [((words[b // 4] >> (6 * (b % 4))) & 63).with_bounds(min_val=0, max_val=NT - 1) for b in range(BS)]


def heads(ap, width=D):
    return ap.rearrange("p (h d) -> p h d", d=width)


def moments(nc, link, stats, mv, ready):
    even, odd = stats[:, :, 1], stats[:, :, 4]
    link(nc.vector.tensor_tensor(mv[:, :, 0], even, odd, ALU.subtract))
    link(nc.vector.tensor_scalar(mv[:, :, 0], mv[:, :, 0], 0.5, None, ALU.mult))
    link(nc.vector.tensor_tensor(mv[:, :, 1], mv[:, :, 0], mv[:, :, 0], ALU.mult))
    link(nc.vector.tensor_tensor(mv[:, :, 0], stats[:, :, 2], stats[:, :, 5], ALU.add))
    link(nc.vector.scalar_tensor_tensor(mv[:, :, 1], mv[:, :, 0], 1.0 / C, mv[:, :, 1], ALU.mult, ALU.add))
    link(nc.vector.tensor_tensor(mv[:, :, 0], even, odd, ALU.add))
    nc.vector.tensor_scalar(mv[:, :, 0], mv[:, :, 0], 0.5, None, ALU.mult).then_inc(ready, 1)


def edge_tables(nc, k):
    with ExitStack() as ctx:
        sb, ps, sem = allocators(nc, ctx)
        dst_in = sb("dst_in", [EP, ER * P], I32)
        src_in = sb("src_in", [EP, ER * P], I32)
        ea_in = sb("ea_in", [EP, ER * P * 3])
        iota_i = sb("iota_i", [P, VPAD], I32)
        nt_row = sb("nt_row", [1, VPAD], I32)
        words_f = sb("words_f", [1, VPAD // 4])
        iota_v = sb("iota_v", [P, VPAD])
        iota_e = sb("iota_e", [P, ER])
        iota_s = sb("iota_s", [P, VC])
        last_tile = sb("last_tile", [EP, ER], I32)
        ends_at = sb("ends_at", [EP, ER])
        passed = sb("passed", [EP, VPAD])
        passed_b = sb("passed_b", [EP, VPAD], BF16)
        ones_b = sb("ones_b", [P, 1], BF16)
        et_raw = sb("et_raw", [P, VC])
        et_f = sb("et_f", [P, VC])
        et_u = sb("et_u", [P, VC], U32)
        nt_f = sb("nt_f", [P, VC])
        nt_i = sb("nt_i", [P, VC], I32)
        nt_base = sb("nt_base", [P, VC])
        dst_g = sb("dst_g", [P, VC, P], I32)
        src_g = sb("src_g", [P, VC, P], I32)
        ea_g = sb("ea_g", [P, VC, P * 3])
        local = sb("local", [P, VC, P])
        local_c = sb("local_c", [P, VC, P])
        local_b = sb("local_b", [P, VC, P], BF16)
        key = sb("key", [P, VC, P])
        src_f = sb("src_f", [P, VC, P])
        ea_rest = sb("ea_rest", [P, VC, 3, P])
        ea_parts = sb("ea_parts", [P, VC, 3, 3, P], BF16)
        ew_t = sb("ew_t", [3, C])
        ew_33 = sb("ew_33", [3, ROW])
        ew_rest = sb("ew_rest", [3, ROW])
        ew_parts = sb("ew_parts", [3, 3, ROW], BF16)
        eb_in = sb("eb_in", [1, C])
        eb_33 = sb("eb_33", [1, ROW])
        eb_rest = sb("eb_rest", [1, ROW])
        eb_parts = sb("eb_parts", [1, 3, ROW], BF16)
        ps_et = ps("ps_et", [P, 512])
        ps_local = ps("ps_local", [P, 2, 512])
        ps_src = ps("ps_src", [P, 2, 512])

        x_pad, x_in = sem("x_pad"), sem("x_in")
        padded, edges_in, edge_w_in = sem("padded"), sem("edges_in"), sem("edge_w_in")
        tables_out, iotas = sem("tables_out"), sem("iotas")
        passed_ready, et_counted, et_ready = sem("passed_ready"), sem("et_counted"), sem("et_ready")
        gathered = [sem(f"gathered{i}") for i in range(3)]
        dve_step, pool_step = sem("et_dve_step"), sem("et_pool_step")
        nt_out, row_in, locals_ready, parts_ready = sem("nt_out"), sem("row_in"), sem("locals_ready"), sem("parts_ready")
        turned, cols_ready, vt_out, w_split, w_out, w_rows = (
            sem("turned"), sem("cols_ready"), sem("vt_out"), sem("w_split"), sem("w_out"), sem("w_rows"))
        block = ctx.enter_context(nc.Block())

        @block.sync
        def _(sp):
            with nc.allow_non_contiguous_dma("a small weight and a short list are read across"):
                sp.dma_start(ew_t[:, :], k.edge_W.rearrange("c f -> f c")).then_inc(edge_w_in, 16)
                sp.dma_start(eb_in[:, :], k.edge_b.rearrange("(a c) -> a c", a=1)).then_inc(edge_w_in, 16)
                sp.wait_ge(padded, 3)
                full = EFULL * ER * P
                for buf, src, w in ((dst_in, k.dst, 1), (src_in, k.src, 1),
                                    (ea_in, k.edge_attr.rearrange("e f -> (e f)"), 3)):
                    sp.dma_start(buf[0:EFULL, :], src[0:full * w].rearrange("(p n) -> p n", p=EFULL)).then_inc(edges_in, 16)
                    sp.dma_start(buf[EFULL:EFULL + 1, 0:EREST * w],
                                 src[full * w:E * w].rearrange("(a n) -> a n", a=1)).then_inc(edges_in, 16)
                sp.wait_ge(edges_in, 96)
                for buf, out in ((dst_in, k.dst_rows), (src_in, k.src_rows), (ea_in, k.ea_rows)):
                    sp.dma_start(out.rearrange("(p r) e -> p (r e)", r=ER), buf[:, :]).then_inc(tables_out, 16)
                sp.wait_ge(w_split, 2)
                sp.dma_start(k.ew_rows.rearrange("j f c -> f j c"), ew_parts[:, :, :]).then_inc(w_out, 16)
                sp.dma_start(k.eb_rows.rearrange("(a j) c -> a j c", a=1), eb_parts[:, :, :]).then_inc(w_out, 16)
                sp.wait_ge(w_out, 32)
                for j in range(3):
                    for f in range(3):
                        r = 9 * j + 3 * f
                        sp.dma_start(k.enc_w[r:r + 3, :], k.ew_rows[j, f:f + 1, :].to_broadcast([3, ROW])).then_inc(w_rows, 16)
                sp.dma_start(k.enc_w[27:30, :], k.eb_rows[:, :]).then_inc(w_rows, 16)
                sp.wait_ge(et_ready, 1)
                sp.dma_start(k.nt_list.rearrange("(c p) -> p c", p=P), nt_i[:, :]).then_inc(nt_out, 16)
                sp.wait_ge(nt_out, 16)
                sp.dma_start(nt_row[:, :], k.nt_list.rearrange("(a v) -> a v", a=1)).then_inc(row_in, 16)
                sp.wait_ge(parts_ready, 1)
                for c in range(VC):
                    sp.dma_start(k.ea_parts[:, c * P:(c + 1) * P, :].rearrange("r v e -> v r e"),
                                 ea_parts[:, c].rearrange("p f i e -> p (f i) e")).then_inc(vt_out, 16)
                sp.wait_ge(locals_ready, 1)
                sp.dma_start(k.local_rows.rearrange("(c p) e -> p c e", p=P), local_b[:, :, :]).then_inc(vt_out, 16)
                sp.dma_start(k.key_rows.rearrange("(c p) e -> p c e", p=P), key[:, :, :]).then_inc(vt_out, 16)
                sp.wait_ge(w_rows, 160)
                sp.wait_ge(row_in, 16)
                sp.wait_ge(vt_out, 16 * (2 + VC))

        @block.gpsimd
        def _(pool):
            link = chain(pool, pool_step)
            nc.gpsimd.memset(dst_in[:, :], NOWHERE).then_inc(padded, 1)
            nc.gpsimd.memset(k.x_res[:, NT - 1, :], 0.0).then_inc(x_pad, 1)
            nc.gpsimd.memset(src_in[:, :], 0).then_inc(padded, 1)
            nc.gpsimd.memset(ea_in[:, :], 0.0).then_inc(padded, 1)
            nc.gpsimd.memset(ones_b[:, :], 1.0).then_inc(iotas, 1)
            link(nc.gpsimd.iota(iota_i[:, :], [[1, VPAD]], 0, 0))
            nc.gpsimd.tensor_copy(iota_v[:, :], iota_i[:, :]).then_inc(iotas, 1)
            nc.gpsimd.tensor_copy(k.iota_row[:, :], iota_i[:, 0:P]).then_inc(iotas, 1)
            pool.wait_ge(iotas, 3)
            link(nc.gpsimd.iota(iota_i[:, 0:ER], [[1, ER]], 0, ER))
            nc.gpsimd.tensor_copy(iota_e[:, :], iota_i[:, 0:ER]).then_inc(iotas, 1)
            link(nc.gpsimd.iota(iota_i[:, P:P + VC], [[P, VC]], 0, 1))
            nc.gpsimd.tensor_copy(iota_s[:, :], iota_i[:, P:P + VC]).then_inc(iotas, 1)
            nc.gpsimd.tensor_copy(k.iota_col[:, :], iota_i[:, P:P + 1]).then_inc(iotas, 1)
            pool.wait_ge(et_ready, 1)
            pool.wait_ge(tables_out, 48)
            for n, out, rows in ((2, ea_g, k.ea_rows), (0, dst_g, k.dst_rows), (1, src_g, k.src_rows)):
                for c in range(VC):
                    pool.indirect_dma_start(out[:, c, :], None, rows[:, :],
                                            bass.IndirectOffsetOnAxis(ap=et_u[:, c:c + 1], axis=0)).then_inc(gathered[n], 16)

        @block.scalar
        def _(act):
            act.wait_ge(gathered[2], 16 * VC)
            act.wait_ge(x_pad, 1)
            for t in range(0, NT - 1, 8):
                act.dma_start(k.x_res[:, t:t + 8, :], k.x[t * P:(t + 8) * P, :].rearrange("(t p) c -> p t c", p=P)).then_inc(x_in, 16)
            act.dma_start(k.x_res[0:NLAST, NT - 1, :], k.x[(NT - 1) * P:N, :]).then_inc(x_in, 16)
            act.wait_ge(x_in, 16 * 7)

        @block.vector
        def _(dve):
            link = chain(dve, dve_step)
            link(nc.vector.memset(ew_33[:, :], 0.0))
            link(nc.vector.memset(eb_33[:, :], 1.0))
            dve.wait_ge(edge_w_in, 32)
            link(nc.vector.tensor_copy(heads(ew_33[:, :], HW)[:, :, 0:D], heads(ew_t[:, :])))
            link(nc.vector.tensor_copy(heads(eb_33[:, :], HW)[:, :, 0:D], heads(eb_in[:, :])))
            for full, rest, parts in ((ew_33, ew_rest, ew_parts), (eb_33, eb_rest, eb_parts)):
                link(nc.vector.tensor_copy(parts[:, 0, :], full[:, :]))
                link(nc.vector.tensor_tensor(rest[:, :], full[:, :], parts[:, 0, :], ALU.subtract))
                link(nc.vector.tensor_copy(parts[:, 1, :], rest[:, :]))
                nc.vector.tensor_tensor(parts[:, 2, :], rest[:, :], parts[:, 1, :], ALU.subtract).then_inc(w_split, 1)
            dve.wait_ge(edges_in, 96)
            dve.wait_ge(iotas, 6)
            link(nc.vector.tensor_scalar(last_tile[:, :], dst_in[:, :].rearrange("p (r e) -> p r e", r=ER)[:, :, P - 1],
                                         7, None, ALU.arith_shift_right))
            link(nc.vector.tensor_scalar(ends_at[:, :], last_tile[:, :], float(NT - 1), None, ALU.min))
            link(nc.vector.tensor_tensor(ends_at[:, :], ends_at[:, :], iota_e[0:EP, :], ALU.add))
            link(nc.vector.tensor_scalar(passed[:, :], iota_v[0:EP, :], ends_at[:, 0:1], None, ALU.is_gt))
            for r in range(1, ER):
                out = passed if r < ER - 1 else passed_b
                ins = nc.vector.scalar_tensor_tensor(out[:, :], iota_v[0:EP, :], ends_at[:, r:r + 1], passed[:, :],
                                                     ALU.is_gt, ALU.add)
                if r < ER - 1:
                    link(ins)
            ins.then_inc(passed_ready, 1)
            dve.wait_ge(et_counted, 1)
            link(nc.vector.tensor_copy(et_raw[:, :], ps_et[:, 0:VC]))
            link(nc.vector.tensor_scalar(et_f[:, :], et_raw[:, :], float(EROWS - 1), 0.0, ALU.min, ALU.max))
            link(nc.vector.tensor_copy(et_u[:, :], et_f[:, :]))
            link(nc.vector.tensor_tensor(nt_f[:, :], iota_s[:, :], et_raw[:, :], ALU.subtract))
            link(nc.vector.tensor_scalar(nt_f[:, :], nt_f[:, :], float(NT - 1), 0.0, ALU.min, ALU.max))
            link(nc.vector.tensor_scalar(nt_base[:, :], nt_f[:, :], float(P), None, ALU.mult))
            nc.vector.tensor_copy(nt_i[:, :], nt_f[:, :]).then_inc(et_ready, 1)
            dve.wait_ge(gathered[2], 16 * VC)
            ea_v = ea_g[:, :, :].rearrange("p c (e f) -> p c f e", f=3)
            link(nc.vector.tensor_copy(ea_parts[:, :, :, 0, :], ea_v))
            link(nc.vector.tensor_tensor(ea_rest[:, :, :, :], ea_v, ea_parts[:, :, :, 0, :], ALU.subtract))
            link(nc.vector.tensor_copy(ea_parts[:, :, :, 1, :], ea_rest[:, :, :, :]))
            nc.vector.tensor_tensor(ea_parts[:, :, :, 2, :], ea_rest[:, :, :, :], ea_parts[:, :, :, 1, :],
                                    ALU.subtract).then_inc(parts_ready, 1)
            dve.wait_ge(gathered[0], 16 * VC)
            for c in range(VC):
                link(nc.vector.tensor_scalar(local[:, c, :], dst_g[:, c, :], nt_base[:, c:c + 1], None, ALU.subtract))
            link(nc.vector.tensor_scalar(local_c[:, :, :], local[:, :, :], -1.0, float(P), ALU.max, ALU.min))
            link(nc.vector.tensor_copy(local_b[:, :, :], local_c[:, :, :]))
            link(nc.vector.tensor_scalar(local[:, :, :], local[:, :, :], 0.0, float(P - 1), ALU.max, ALU.min))
            dve.wait_ge(gathered[1], 16 * VC)
            link(nc.vector.tensor_copy(src_f[:, :, :], src_g[:, :, :]))
            for c in range(VC):
                link(nc.vector.tensor_scalar(key[:, c, :], local[:, c, :], nt_base[:, c:c + 1], None, ALU.add))
            dve.sem_inc(locals_ready, 1)
            dve.wait_ge(row_in, 16)
            by_four = nt_row[:, :].rearrange("a (w i) -> a w i", i=4)
            link(nc.vector.tensor_copy(words_f[:, :], by_four[:, :, 3]))
            for i in (2, 1, 0):
                out = words_f if i else k.nt_words
                link(nc.vector.scalar_tensor_tensor(out[:, :], words_f[:, :], 64.0, by_four[:, :, i], ALU.mult, ALU.add))
            dve.wait_ge(turned, 1)
            for a in range(2):
                n = 4 * P if a == 0 else (VC - 4) * P
                nc.vector.tensor_copy(k.local_col[:, 4 * P * a:4 * P * a + n], ps_local[:, a, 0:n])
                nc.vector.tensor_copy(k.src_col[:, 4 * P * a:4 * P * a + n], ps_src[:, a, 0:n]).then_inc(cols_ready, 1)
            dve.wait_ge(cols_ready, 2)

        @block.tensor
        def _(pe):
            pe.wait_ge(passed_ready, 1)
            pe.wait_ge(iotas, 6)
            for c in range(VC):
                last = nc.tensor.matmul(ps_et[:, c:c + 1], passed_b[:, c * P:(c + 1) * P], ones_b[0:EP, :],
                                        start=True, stop=True)
            last.then_inc(et_counted, 1)
            pe.wait_ge(locals_ready, 1)
            for c in range(VC):
                nc.tensor.transpose(ps_local[:, c // 4, (c % 4) * P:(c % 4 + 1) * P], local_c[:, c, :], k.ident[:, :])
                last = nc.tensor.transpose(ps_src[:, c // 4, (c % 4) * P:(c % 4 + 1) * P], src_f[:, c, :], k.ident[:, :])
            last.then_inc(turned, 1)


def constants(nc, k):
    with ExitStack() as ctx:
        sb, ps, sem = allocators(nc, ctx)
        zeroed = sem("zeroed")
        made = sem("consts_made")
        block = ctx.enter_context(nc.Block())

        @block.gpsimd
        def _(pool):
            nc.gpsimd.memset(k.ident[:, :], 0.0).then_inc(zeroed, 1)
            nc.gpsimd.memset(k.eps[:, :], EPS)
            pool.wait_ge(zeroed, 1)
            nc.gpsimd.affine_select(out=k.ident[:, :], in_=k.ident[:, :], compare_op=ALU.not_equal, fill=1.0, base=0,
                                    pattern=[[-1, P]], channel_multiplier=1).then_inc(made, 1)
            pool.wait_ge(made, 1)


def node_rows(nc, k):
    with ExitStack() as ctx:
        sb, ps, sem = allocators(nc, ctx)
        w_nat = sb("w_nat", [P, 2, C])
        a_cols = sb("a_cols", [P, 2, 2])
        a_mask = sb("a_mask", [P, 2, H])
        a_blocks = sb("a_blocks", [P, 2, 2 * H])
        w_node = sb("w_node", [P, 2, NW])
        w_qkv = sb("w_qkv", [P, 2, QW])
        g_pre = sb("g_pre", [P, 2])
        stats = sb("stats", [P, NT, 6])
        mv = sb("mv", [P, NT, 2])
        std = sb("std", [P, NT])
        xn = sb("xn", [P, 4, C])
        xn_t = sb("xn_t", [P, 2, 2, P])
        h_row = sb("h_row", [P, R, ROW])
        h_out = sb("h_out", [P, 2, NW])
        h_dst = sb("h_dst", [P, 2, ROW])
        h_rest = sb("h_rest", [P, 2, ROW])
        h_parts = sb("h_parts", [P, R, 3, ROW], BF16)
        s_src = sb("s_src", [P, NT, H])
        ps_w = ps("ps_w", [P, 512])
        ps_t = [ps(f"ps_t{i}", [P, 512]) for i in range(2)]
        ps_h = [ps(f"ps_h{i}", [P, 512]) for i in range(2)]
        ps_q = [ps(f"ps_q{i}", [P, 512]) for i in range(2)]

        w_in = sem("w_in")
        pool_step, dve_step = sem("n_pool_step"), sem("n_dve_step")
        mask_ready, blocks_ready = sem("mask_ready"), sem("blocks_ready")
        w_turned, w_node_ready, a_folded = sem("w_turned"), sem("w_node_ready"), sem("a_folded")
        stats_ready, std_ready, rstd_ready, norm_ready = (
            sem("stats_ready"), sem("std_ready"), sem("rstd_ready"), sem("norm_ready"))
        xn_ready, x_turned, xt_ready, h_done, q_done = (
            sem("xn_ready"), sem("x_turned"), sem("xt_ready"), sem("h_done"), sem("q_done"))
        ps_h_free, h_taken, ps_q_free, dve_split = sem("ps_h_free"), sem("h_taken"), sem("ps_q_free"), sem("dve_split")
        pool_seen = sem("pool_seen")
        rows_ready, parts_ready = sem("rows_ready"), sem("h_parts_ready")
        rows_out = [sem(f"rows_out{g}") for g in range(R)]
        parts_out = [sem(f"parts_out{g}") for g in range(R)]
        ones_set, src_out, stat_steps, squared, rooted = sem("ones_set"), sem("src_out"), sem("stat_steps"), sem("squared"), sem("rooted")
        block = ctx.enter_context(nc.Block())

        @block.sync
        def _(sp):
            with nc.allow_non_contiguous_dma("vectors laid down the partitions"):
                sp.dma_start(w_nat[:, :, :], k.W.rearrange("(a p) c -> p a c", p=P)).then_inc(w_in, 16)
                sp.dma_start(a_cols[:, :, 0], k.a_src.rearrange("h d -> (h d)").rearrange("(a p) -> p a", p=P)).then_inc(w_in, 16)
                sp.dma_start(a_cols[:, :, 1], k.a_dst.rearrange("h d -> (h d)").rearrange("(a p) -> p a", p=P)).then_inc(w_in, 16)
                sp.dma_start(w_qkv[:, :, :], k.w_qkv.rearrange("(a p) c -> p a c", p=P)).then_inc(w_in, 16)
                sp.dma_start(g_pre[:, :], k.g_pre.rearrange("(a p) -> p a", p=P)).then_inc(w_in, 16)

            def store(it, g):
                t = it * R + g
                sp.wait_ge(rows_ready, t + 3)
                sp.dma_start(k.h_rows[bass.ds(t * P, P), :], h_row[:, g, :]).then_inc(rows_out[g], 16)
                sp.wait_ge(parts_ready, t + 1)
                sp.dma_start(k.hd_parts[bass.ds(t * P, P), :], h_parts[:, g].rearrange("p i c -> p (i c)")).then_inc(parts_out[g], 16)

            with sp.Fori(0, NT // R) as it:
                for g in range(R):
                    store(it, g)
            store(NT // R, 0)
            sp.wait_ge(rows_ready, NT + 2)
            sp.dma_start(k.src_logits.rearrange("(t p) h -> p t h", p=P), s_src[:, :, :]).then_inc(src_out, 16)
            for g in range(R):
                n = NT // R + (2 if g == 0 else 1)
                sp.wait_ge(rows_out[g], 16 * n)
                sp.wait_ge(parts_out[g], 16 * n)
            sp.wait_ge(src_out, 16)

        @block.gpsimd
        def _(pool):
            link = chain(pool, pool_step)
            nc.gpsimd.memset(h_row[:, :, :], 1.0).then_inc(ones_set, 1)
            link(nc.gpsimd.memset(a_mask[:, :, :], 1.0))
            link(nc.gpsimd.affine_select(out=a_mask[:, :, :], in_=a_mask[:, :, :], compare_op=ALU.is_ge, fill=0.0, base=0,
                                         pattern=[[P, 2], [-D, H]], channel_multiplier=1))
            nc.gpsimd.affine_select(out=a_mask[:, :, :], in_=a_mask[:, :, :], compare_op=ALU.is_ge, fill=0.0, base=D - 1,
                                    pattern=[[-P, 2], [D, H]], channel_multiplier=-1).then_inc(mask_ready, 1)
            pool.wait_ge(ones_set, 1)

            def source_rows(it, g):
                t = it * R + g
                pool.wait_ge(ps_h_free, t + 3)
                pool.wait_ge(rows_out[g], it * 16 + 16)
                pool.sem_inc(pool_seen, 1)
                nc.gpsimd.tensor_copy(heads(h_row[:, g, :], HW)[:, :, 0:D], heads(h_out[:, g % 2, 0:C]))
                nc.gpsimd.tensor_copy(s_src[:, bass.ds(t, 1), :], h_out[:, g % 2, C:C + H]).then_inc(rows_ready, 1)

            with pool.Fori(0, NT // R) as it:
                for g in range(R):
                    source_rows(it, g)
            source_rows(NT // R, 0)

        @block.vector
        def _(dve):
            link = chain(dve, dve_step)
            dve.wait_ge(w_in, 80)
            dve.wait_ge(mask_ready, 1)
            for a in range(2):
                nc.vector.tensor_scalar(a_blocks[:, a, 0:H], a_mask[:, a, :], a_cols[:, a, 0:1], None, ALU.mult)
                last = nc.vector.tensor_scalar(a_blocks[:, a, H:2 * H], a_mask[:, a, :], a_cols[:, a, 1:2], None, ALU.mult)
            last.then_inc(blocks_ready, 1)
            for a in range(2):
                link(nc.vector.tensor_scalar(w_qkv[:, a, :], w_qkv[:, a, :], g_pre[:, a:a + 1], None, ALU.mult))
            for a in range(2):
                dve.wait_ge(w_turned, a + 1)
                last = nc.vector.tensor_copy(w_node[:, a, 0:C], ps_w[:, 0:C])
                last.then_inc(w_node_ready, 1)
            dve.wait_ge(a_folded, 1)
            for a in range(2):
                nc.vector.tensor_copy(w_node[:, a, C:NW], ps_w[:, C + 2 * H * a:C + 2 * H * (a + 1)]).then_inc(w_node_ready, 1)
            with dve.Fori(0, NT // G) as it:
                for g in range(G):
                    t = it * G + g
                    nc.vector.bn_stats(stats[:, bass.ds(t, 1), :], k.x_res[:, bass.ds(t, 1), :]).then_inc(stat_steps, 1)
            dve.wait_ge(stat_steps, NT)
            moments(nc, link, stats, mv, stats_ready)
            dve.wait_ge(stats_ready, 1)
            dve.wait_ge(std_ready, 1)
            link(nc.vector.reciprocal(k.rstd[:, :], std[:, :]))
            nc.vector.scalar_tensor_tensor(k.shift[:, :], mv[:, :, 0], -1.0, k.rstd[:, :], ALU.mult, ALU.mult).then_inc(rstd_ready, 1)
            link(nc.vector.tensor_tensor(k.norm[:, :], k.rstd[:, :], k.rstd[:, :], ALU.mult))
            nc.vector.tensor_tensor(k.norm[:, :], k.norm[:, :], mv[:, :, 1], ALU.mult).then_inc(squared, 1)
            dve.wait_ge(rooted, 1)
            link(nc.vector.tensor_scalar(k.norm[:, :], k.norm[:, :], 1e-12, float(C) ** -0.5, ALU.max, ALU.mult))
            nc.vector.reciprocal(k.norm[:, :], k.norm[:, :]).then_inc(norm_ready, 1)

            def destination_rows(it, g):
                t = it * R + g
                s = g % 2
                dve.wait_ge(ps_h_free, t + 3)
                nc.vector.tensor_copy(heads(h_dst[:, s, :], HW)[:, :, D], h_out[:, s, C + H:NW])
                nc.vector.tensor_copy(heads(h_dst[:, s, :], HW)[:, :, 0:D], heads(h_out[:, s, 0:C])).then_inc(h_taken, 1)
                dve.wait_ge(h_taken, t + 3)
                dve.wait_ge(parts_out[g], it * 16 + 16)
                nc.vector.tensor_copy(h_parts[:, g, 0, :], h_dst[:, s, :]).then_inc(dve_split, 1)
                dve.wait_ge(dve_split, t * 3 + 1)
                nc.vector.tensor_tensor(h_rest[:, s, :], h_dst[:, s, :], h_parts[:, g, 0, :], ALU.subtract).then_inc(dve_split, 1)
                dve.wait_ge(dve_split, t * 3 + 2)
                nc.vector.tensor_copy(h_parts[:, g, 1, :], h_rest[:, s, :]).then_inc(dve_split, 1)
                dve.wait_ge(dve_split, t * 3 + 3)
                nc.vector.tensor_tensor(h_parts[:, g, 2, :], h_rest[:, s, :], h_parts[:, g, 1, :], ALU.subtract).then_inc(parts_ready, 1)

            with dve.Fori(0, NT // R) as it:
                for g in range(R):
                    destination_rows(it, g)
            destination_rows(NT // R, 0)

        @block.scalar
        def _(act):
            for g in range(R):
                act.sem_inc(parts_out[g], 16)
                act.sem_inc(rows_out[g], 16)
            for free in (ps_h_free, h_taken, rows_ready, ps_q_free, xt_ready):
                act.sem_inc(free, 2)
            act.wait_ge(stats_ready, 1)
            nc.scalar.activation(std[:, :], mv[:, :, 1], ACT.Sqrt, bias=k.eps[:, 0:1]).then_inc(std_ready, 1)
            act.wait_ge(squared, 1)
            nc.scalar.activation(k.norm[:, :], k.norm[:, :], ACT.Sqrt, scale=float(C)).then_inc(rooted, 1)
            act.wait_ge(norm_ready, 1)
            act.wait_ge(ones_set, 1)

            def normed(t, g):
                nc.scalar.activation(xn[:, g % 4, :], k.x_res[:, bass.ds(t, 1), :], ACT.Identity, scale=k.rstd[:, bass.ds(t, 1)],
                                     bias=k.shift[:, bass.ds(t, 1)]).then_inc(xn_ready, 1)

            def turned_copy(t, g):
                act.wait_ge(x_turned, t + 1)
                nc.scalar.copy(xn_t[:, g % 2].rearrange("p a n -> p (a n)"), ps_t[g % 2][:, 0:C]).then_inc(xt_ready, 1)

            def node_tile(it, g, ahead=2):
                t = it * R + g
                s = g % 2
                if ahead >= 1:
                    turned_copy(t + 1, g + 1)
                if ahead >= 2:
                    normed(t + 2, g + 2)
                act.wait_ge(h_done, t + 1)
                act.wait_ge(rows_ready, t + 1)
                act.wait_ge(h_taken, t + 1)
                nc.scalar.copy(h_out[:, s, :], ps_h[s][:, 0:NW]).then_inc(ps_h_free, 1)
                act.wait_ge(q_done, t + 1)
                nc.scalar.activation(k.qkv[:, bass.ds(t, 1), 0:QW], ps_q[s][:, 0:QW], ACT.Copy,
                                     scale=k.norm[:, bass.ds(t, 1)]).then_inc(ps_q_free, 1)

            normed(0, 0)
            normed(1, 1)
            turned_copy(0, 0)
            with act.Fori(0, NT // R - 1) as it:
                for g in range(R):
                    node_tile(it, g)
            for t in range(NT - 1 - R, NT):
                node_tile(t // R, t % R, min(2, NT - 1 - t))

        @block.tensor
        def _(pe):
            pe.wait_ge(w_in, 80)
            for a in range(2):
                if a:
                    pe.wait_ge(w_node_ready, 1)
                for b in range(2):
                    last = nc.tensor.transpose(ps_w[:, b * P:(b + 1) * P], w_nat[:, b, a * P:(a + 1) * P], k.ident[:, :])
                last.then_inc(w_turned, 1)
            pe.wait_ge(blocks_ready, 1)
            pe.wait_ge(w_node_ready, 2)
            for a in range(2):
                for b in range(2):
                    last = nc.tensor.matmul(ps_w[:, C + 2 * H * a:C + 2 * H * (a + 1)], w_nat[:, b, a * P:(a + 1) * P],
                                            a_blocks[:, b, :], start=b == 0, stop=b == 1)
            last.then_inc(a_folded, 1)
            pe.wait_ge(w_node_ready, 4)
            pe.wait_ge(dve_step, 2)

            def turn_rows(t, g):
                pe.wait_ge(xn_ready, t + 1)
                pe.wait_ge(xt_ready, t + 1)
                for a in range(2):
                    last = nc.tensor.transpose(ps_t[g % 2][:, a * P:(a + 1) * P], xn[:, g % 4, a * P:(a + 1) * P], k.ident[:, :])
                last.then_inc(x_turned, 1)

            def products(t, s):
                pe.wait_ge(xt_ready, t + 3)
                pe.wait_ge(ps_h_free, t + 1)
                for a in range(2):
                    last = nc.tensor.matmul(ps_h[s][:, 0:NW], xn_t[:, s, a, :], w_node[:, a, :], start=a == 0, stop=a == 1)
                last.then_inc(h_done, 1)
                pe.wait_ge(ps_q_free, t + 1)
                for a in range(2):
                    last = nc.tensor.matmul(ps_q[s][:, 0:QW], xn_t[:, s, a, :], w_qkv[:, a, :], start=a == 0, stop=a == 1)
                last.then_inc(q_done, 1)

            turn_rows(0, 0)
            with pe.Fori(0, NT // R) as it:
                for g in range(R):
                    turn_rows(it * R + (g + 1), g + 1)
                    products(it * R + g, g % 2)
            products(NT - 1, 0)


class SourceGathers:

    def __init__(self, nc, k, sb, sem, tag, first, last):
        self.nc, self.k, self.first, self.turns = nc, k, first, (last - first) // 2
        self.idx = [sb(f"src_idx_{tag}{s}", [P, GS], U32) for s in range(2)]
        self.ring = [sb(f"src_ring_{tag}{s}", [P, GS, H]) for s in range(2)]
        self.gathered = [sem(f"src_gathered_{tag}{s}") for s in range(2)]
        self.seen, self.idx_ready, self.taken = sem(f"src_seen_{tag}"), sem(f"src_idx_ready_{tag}"), sem(f"src_taken_{tag}")

    def take(self, pool, turn, s):
        pool.wait_ge(self.gathered[s], (turn + 1) * (16 * GS))
        pool.sem_inc(self.seen, 1)
        cols = bass.ds((turn * 2 + (self.first + s)) * GS, GS)
        self.nc.gpsimd.tensor_copy(self.k.src_all[:, cols, :], self.ring[s][:, :, :]).then_inc(self.taken, 1)

    def gather(self, pool, turn, s):
        cols = bass.ds((turn * 2 + (self.first + s)) * GS, GS)
        self.nc.gpsimd.tensor_copy(self.idx[s][:, :], self.k.src_col[:, cols]).then_inc(self.idx_ready, 1)
        pool.wait_ge(self.idx_ready, turn * 2 + (s + 1))
        pool.sem_inc(self.seen, 1)
        for b in range(GS):
            pool.indirect_dma_start(self.ring[s][:, b, :], None, self.k.src_logits[:, :],
                                    bass.IndirectOffsetOnAxis(ap=self.idx[s][:, b:b + 1], axis=0)).then_inc(self.gathered[s], 16)

    def run(self, pool):
        for s in range(2):
            self.gather(pool, 0, s)
        with pool.Fori(1, self.turns) as it:
            for s in range(2):
                self.take(pool, it - 1, s)
                pool.wait_ge(self.taken, (it - 1) * 2 + (s + 1))
                self.gather(pool, it, s)
        for s in range(2):
            self.take(pool, self.turns - 1, s)


def edge_logits(nc, k):
    with ExitStack() as ctx:
        sb, ps, sem = allocators(nc, ctx)
        hd_tab = sb("hd_tab", [P, NT, 3 * ROW], BF16)
        ea_t = [sb(f"ea_t{s}", [30, BS * P], BF16) for s in range(2)]
        loc_row = [sb(f"loc_row{s}", [P, BS * P], BF16) for s in range(2)]
        onehot = [sb(f"onehot{s}", [P, BS * P], BF16) for s in range(2)]
        enc = sb("enc", [P, 4, ROW])
        prod = sb("prod", [P, 4, ROW])
        outside = sb("outside", [P, V])
        outside2 = sb("outside2", [P, V])
        ps_enc = [ps(f"ps_enc{i}", [P, 512]) for i in range(4)]
        ps_hd = [ps(f"ps_hd{i}", [P, 512]) for i in range(4)]
        tab_in, set_up = sem("tab_in"), sem("set_up")
        ea_in = [sem(f"ea_in{s}") for s in range(2)]
        loc_in = [sem(f"loc_in{s}") for s in range(2)]
        sources = SourceGathers(nc, k, sb, sem, "late", EARLY, V // GS)
        enc_done, taken_done, hd_done = sem("enc_done"), sem("taken_done"), sem("hd_done")
        prod_done, reduced, onehot_ready = sem("prod_done"), sem("reduced"), sem("onehot_ready")
        out_step, sp_seen = sem("b_out_step"), sem("sp_seen")
        block = ctx.enter_context(nc.Block())

        @block.sync
        def _(sp):
            for t in range(0, NT, G):
                sp.dma_start(hd_tab[:, t:t + G, :], k.hd_parts[t * P:(t + G) * P, :].rearrange("(t p) c -> p t c", p=P)).then_inc(tab_in, 16)
            sp.wait_ge(set_up, 2)

            def bring(j, s):
                sp.wait_ge(onehot_ready, j + 1)
                sp.sem_inc(sp_seen, 1)
                sp.wait_ge(hd_done, (j + 1) * BS)
                sp.dma_start(ea_t[s][0:27, :],
                             k.ea_parts[:, bass.ds(j * BS, BS), :].rearrange("r v e -> r (v e)").unsqueeze(0).to_broadcast([3, 9, BS * P])).then_inc(ea_in[s], 16)
                sp.dma_start(loc_row[s][:, :], k.local_rows[bass.ds(j * BS, BS), :].rearrange("(a v) e -> a (v e)", a=1)
                             .to_broadcast([P, BS * P])).then_inc(loc_in[s], 16)

            with sp.Fori(0, NBLK // 2) as it:
                for s in range(2):
                    bring(it * 2 + s, s)
            bring(NBLK, 0)
            sp.wait_ge(ea_in[0], 16 * (NBLK // 2 + 1))
            sp.wait_ge(loc_in[0], 16 * (NBLK // 2 + 1))

        @block.gpsimd
        def _(pool):
            for s in range(2):
                nc.gpsimd.memset(ea_t[s][:, :], 1.0).then_inc(set_up, 1)
            sources.run(pool)

        @block.scalar
        def _(act):
            act.sem_inc(hd_done, 2 * BS)
            act.sem_inc(onehot_ready, 2)
            act.sem_inc(taken_done, 4)
            act.sem_inc(prod_done, 4)
            act.sem_inc(reduced, 4)
            with act.Fori(0, NBLK // 2) as it:
                for s in range(2):
                    j = it * 2 + s
                    for b in range(BS):
                        v = j * BS + b
                        act.wait_ge(enc_done, v + 1)
                        act.wait_ge(prod_done, v + 1)
                        nc.scalar.activation(enc[:, b % 4, :], ps_enc[b % 4][:, 0:ROW], ACT.Relu).then_inc(taken_done, 1)

        @block.tensor
        def _(pe):
            def encode(v, s, b):
                if b % 2 == 0:
                    pe.wait_ge(taken_done, v + 2)
                nc.tensor.matmul(ps_enc[b % 4][:, 0:ROW], ea_t[s][:, b * P:(b + 1) * P], k.enc_w[:, :],
                                 start=True, stop=True).then_inc(enc_done, 1)

            def turn(it, last):
                tiles = [node_tiles(pe, k, it * 2), None]
                for s in range(2):
                    j = it * 2 + s
                    for b in range(BS):
                        v = j * BS + b
                        if b < BS - 1:
                            encode(v + 1, s, b + 1)
                        elif s == 0 or not last:
                            pe.wait_ge(ea_in[1 - s], (it + (1 + s)) * 16)
                            encode(v + 1, 1 - s, 0)
                        if s == 0 and b == 4:
                            tiles[1] = node_tiles(pe, k, j + 1)
                        if b == 0:
                            pe.wait_ge(onehot_ready, j + 3)
                        if b % 2 == 0:
                            pe.wait_ge(prod_done, v + 2)
                        for i in range(3):
                            mm = nc.tensor.matmul(ps_hd[b % 4][:, 0:ROW], onehot[s][:, b * P:(b + 1) * P],
                                                  hd_tab[:, bass.ds(tiles[s][b], 1), i * ROW:(i + 1) * ROW], start=i == 0, stop=i == 2)
                        mm.then_inc(hd_done, 1)

            pe.wait_ge(tab_in, 16 * (NT // G))
            pe.wait_ge(ea_in[0], 16)
            pe.wait_ge(taken_done, 4)
            encode(0, 0, 0)
            with pe.Fori(0, NBLK // 2 - 1) as it:
                turn(it, False)
            turn(NBLK // 2 - 1, True)

        @block.vector
        def _(dve):
            link = chain(dve, out_step)

            def one_hot(s):
                nc.vector.tensor_scalar(onehot[s][:, :], loc_row[s][:, :], k.iota_col[:, 0:1], None, ALU.is_equal).then_inc(onehot_ready, 1)

            def multiply(v, b):
                dve.wait_ge(hd_done, v + (2 * BS + 1))
                dve.wait_ge(taken_done, v + 5)
                dve.wait_ge(reduced, v + 1)
                nc.vector.tensor_tensor(prod[:, b % 4, :], enc[:, b % 4, :], ps_hd[b % 4][:, 0:ROW], ALU.mult).then_inc(prod_done, 1)

            def turn(it, last):
                for s in range(2):
                    j = it * 2 + s
                    for b in range(BS):
                        v = j * BS + b
                        if b == BS // 2:
                            dve.wait_ge(loc_in[1 - s], (it + (1 + s)) * 16)
                            dve.wait_ge(hd_done, (j + 2) * BS)
                            one_hot(1 - s)
                        if not last or s == 0 or b < BS - 1:
                            multiply(v + 1, b + 1)
                        dve.wait_ge(prod_done, v + 5)
                        nc.vector.tensor_reduce(k.alpha[:, bass.ds(v, 1), :], heads(prod[:, b % 4, :], HW), AX.X, ALU.add).then_inc(reduced, 1)

            link(nc.vector.tensor_scalar(outside[:, :], k.local_col[:, 0:V], 0.0, -BIG, ALU.is_lt, ALU.mult))
            link(nc.vector.tensor_scalar(outside2[:, :], k.local_col[:, 0:V], float(P), -BIG, ALU.is_ge, ALU.mult))
            link(nc.vector.tensor_tensor(outside[:, :], outside[:, :], outside2[:, :], ALU.add))
            dve.wait_ge(loc_in[0], 16)
            one_hot(0)
            multiply(0, 0)
            with dve.Fori(0, NBLK // 2 - 1) as it:
                turn(it, False)
            turn(NBLK // 2 - 1, True)
            dve.wait_ge(reduced, V + 4)
            link(nc.vector.tensor_tensor(k.alpha[:, :, :], k.alpha[:, :, :], outside[:, :].unsqueeze(2).to_broadcast([P, V, H]), ALU.add))
            for part in range(4):
                n = V // 4
                alpha, src = k.alpha[:, part * n:(part + 1) * n, :], k.src_all[:, part * n:(part + 1) * n, :]
                dve.wait_ge(sources.taken, V // GS * (part + 1) // 4 - EARLY)
                link(nc.vector.tensor_tensor(alpha, alpha, src, ALU.add))
                link(nc.vector.scalar_tensor_tensor(alpha, alpha, 0.2, alpha, ALU.mult, ALU.max))


def segment_softmax(nc, k):
    with ExitStack() as ctx:
        sb, ps, sem = allocators(nc, ctx)
        L = CT * P
        gathered_cols = [sb(f"turn_in{s}", [P, 2, P]) for s in range(2)]
        alpha_t = sb("alpha_t", [P, L])
        key_t = sb("key_t", [P, L])
        reset = sb("reset", [P, L + 1])
        fwd = sb("fwd", [P, L])
        best = sb("best", [P, L])
        edge_stat = sb("edge_stat", [P, 4])
        stat_all = sb("stat_all", [P, CH, 4])
        other = sb("other", [P, 2, 2, CH])
        across = sb("across", [P, 2])
        zeros = sb("zero_rows", [P, 2, LW])
        zeroed, cleared = sem("zero_rows_set"), sem("cleared")
        ps_in = [ps(f"ps_in{s}", [P, 512]) for s in range(2)]
        ps_out = [ps(f"ps_out{s}", [P, 512]) for s in range(2)]
        keys_in, stat_ready, stat_out, stat_in = sem("keys_in"), sem("stat_ready"), sem("stat_out"), sem("stat_in")
        cols_ready, cols_turned, cols_copied = sem("s_cols_ready"), sem("s_cols_turned"), sem("s_cols_copied")
        shifted, exp_ready, exp_turned, exp_copied = sem("shifted"), sem("exp_ready"), sem("exp_turned"), sem("exp_copied")
        dve_step = sem("s_dve_step")
        block = ctx.enter_context(nc.Block())
        by_chunk = k.alpha[:, :, :].rearrange("p (j g) h -> p g j h", g=CT)

        @block.sync
        def _(sp):
            for j in range(CH):
                sp.dma_start(key_t[H * j:H * (j + 1), :], k.key_rows[j * CT:(j + 1) * CT, :].rearrange("(a v) e -> a (v e)", a=1)
                             .to_broadcast([H, L])).then_inc(keys_in, 16)
            sp.wait_ge(stat_ready, 4)
            sp.dma_start(k.chunk_stats[:, :], edge_stat[:, :]).then_inc(stat_out, 16)
            sp.wait_ge(stat_out, 16)
            for j in range(CH):
                sp.dma_start(stat_all[H * j:H * (j + 1), :, :], k.chunk_stats.rearrange("(i h) c -> h i c", h=H)).then_inc(stat_in, 16)
            sp.wait_ge(zeroed, 1)
            for b in range(0, NB, 2):
                sp.dma_start(k.list_rows[b * P:(b + 2) * P, :].rearrange("(t p) c -> p t c", p=P), zeros[:, :, :]).then_inc(cleared, 16)
            sp.dma_start(k.node_out[NPAD + 1:NPAD + P + 1, :], zeros[:, 0, 0:C]).then_inc(cleared, 16)
            sp.wait_ge(cleared, 8 * NB + 16)

        @block.gpsimd
        def _(pool):
            nc.gpsimd.memset(zeros[:, :, :], 0.0).then_inc(zeroed, 1)

        @block.scalar
        def _(act):
            act.sem_inc(cols_turned, 2)
            act.sem_inc(cols_copied, 2)
            with act.Fori(0, CT // 4) as it:
                for s in range(2):
                    act.wait_ge(cols_turned, it * 2 + (s + 1))
                    nc.scalar.copy(gathered_cols[s][:, :, :].rearrange("p g (j h) -> p g j h", h=H),
                                   by_chunk[:, bass.ds(it * 4 + 2 * s, 2), :, :]).then_inc(cols_ready, 1)
            act.preload_act_table(ACT.Exp)
            act.wait_ge(shifted, 1)
            with act.Fori(0, CT // 4) as it:
                for s in range(2):
                    act.wait_ge(exp_turned, it * 2 + (s + 1))
                    nc.scalar.activation(gathered_cols[s][:, :, :].rearrange("p g e -> p (g e)"),
                                         alpha_t[:, bass.ds((it * 4 + 2 * s) * P, 2 * P)], ACT.Exp).then_inc(exp_ready, 1)

        @block.tensor
        def _(pe):
            with pe.Fori(0, CT // 4) as it:
                for s in range(2):
                    pe.wait_ge(cols_ready, it * 2 + (s + 1))
                    pe.wait_ge(cols_copied, it * 2 + (s + 1))
                    for g in range(2):
                        last = nc.tensor.transpose(ps_in[s][:, g * P:(g + 1) * P], gathered_cols[s][:, g, :], k.ident[:, :])
                    last.then_inc(cols_turned, 1)
            with pe.Fori(0, CT // 4) as it:
                for s in range(2):
                    pe.wait_ge(exp_ready, it * 2 + (s + 1))
                    pe.wait_ge(exp_copied, it * 2 + (s + 1))
                    for g in range(2):
                        last = nc.tensor.transpose(ps_out[s][:, g * P:(g + 1) * P], gathered_cols[s][:, g, :], k.ident[:, :])
                    last.then_inc(exp_turned, 1)

        @block.vector
        def _(dve):
            link = chain(dve, dve_step)
            dve.sem_inc(exp_turned, 2)
            dve.sem_inc(exp_copied, 2)
            with dve.Fori(0, CT // 4) as it:
                for s in range(2):
                    dve.wait_ge(cols_turned, it * 2 + (s + 3))
                    nc.vector.tensor_copy(alpha_t[:, bass.ds((it * 4 + 2 * s) * P, 2 * P)], ps_in[s][:, 0:2 * P]).then_inc(cols_copied, 1)
            dve.wait_ge(keys_in, 16 * CH)
            nc.vector.memset(reset[:, 0:1], 0.0)
            nc.vector.memset(reset[:, L:L + 1], 0.0)
            link(nc.vector.tensor_tensor(reset[:, 1:L], key_t[:, 1:L], key_t[:, 0:L - 1], ALU.not_equal))
            link(nc.vector.tensor_scalar(reset[:, 1:L], reset[:, 1:L], -BIG * 1e6, None, ALU.mult))
            dve.wait_ge(cols_copied, CT // 2 + 2)
            link(nc.vector.tensor_tensor_scan(fwd[:, :], reset[:, 0:L], alpha_t[:, :], -BIG * 1e6, ALU.add, ALU.max))
            link(nc.vector.tensor_tensor_scan(best[:, ::-1], reset[:, 1:L + 1][:, ::-1], fwd[:, ::-1], -BIG * 1e6, ALU.add, ALU.max))
            for c, col in enumerate((best[:, 0:1], best[:, L - 1:L], key_t[:, 0:1], key_t[:, L - 1:L])):
                nc.vector.tensor_copy(edge_stat[:, c:c + 1], col).then_inc(stat_ready, 1)
            dve.wait_ge(stat_ready, 4)
            for mine, far in enumerate((reset, fwd)):
                link(nc.vector.tensor_scalar(far[:, 0:L], key_t[:, :], edge_stat[:, 2 + mine:3 + mine], -BIG * 1e6,
                                             ALU.not_equal, ALU.mult))
            dve.wait_ge(stat_in, 16 * CH)
            for mine in range(2):
                for theirs in range(2):
                    link(nc.vector.tensor_scalar(other[:, mine, theirs, :], stat_all[:, :, 2 + theirs], edge_stat[:, 2 + mine:3 + mine],
                                                 -BIG * 1e6, ALU.not_equal, ALU.mult))
                    link(nc.vector.tensor_tensor(other[:, mine, theirs, :], other[:, mine, theirs, :], stat_all[:, :, theirs], ALU.add))
            link(nc.vector.tensor_reduce(across[:, :], other[:, :, :, :], AX.XY, ALU.max))
            for mine, far in enumerate((reset, fwd)):
                link(nc.vector.scalar_tensor_tensor(best[:, :], far[:, 0:L], across[:, mine:mine + 1], best[:, :], ALU.add, ALU.max))
            nc.vector.tensor_tensor(alpha_t[:, :], alpha_t[:, :], best[:, :], ALU.subtract).then_inc(shifted, 1)
            with dve.Fori(0, CT // 4) as it:
                for s in range(2):
                    dve.wait_ge(exp_turned, it * 2 + (s + 3))
                    nc.vector.tensor_copy(by_chunk[:, bass.ds(it * 4 + 2 * s, 2), :, :],
                                          ps_out[s][:, 0:2 * P].rearrange("p (g j h) -> p g j h", g=2, h=H)).then_inc(exp_copied, 1)


def aggregate(nc, k):
    with ExitStack() as ctx:
        sb, ps, sem = allocators(nc, ctx)
        src_idx = [sb(f"row_idx{s}", [P, BS], U32) for s in range(SLOTS)]
        rows = [sb(f"rows{s}", [P, BS, ROW]) for s in range(SLOTS)]
        weighted = sb("weighted", [P, 4, ROW])
        away = sb("away", [P, 4, P])
        onehot = sb("onehot_f", [P, 4, P])
        ps_sum = [ps(f"ps_sum{i}", [P, 512]) for i in range(4)]
        rows_in = [sem(f"rows_in{s}") for s in range(SLOTS)]
        idx_in = [sem(f"row_idx_in{s}") for s in range(SLOTS)]
        idx_seen, weighted_ready, onehot_ready = sem("d_idx_seen"), sem("weighted_ready"), sem("d_onehot_ready")
        summed, added, away_ready = sem("summed"), sem("added"), sem("away_ready")
        block = ctx.enter_context(nc.Block())

        @block.sync
        def _(sp):
            def bring(turn, s):
                sp.dma_start(src_idx[s][:, :], k.src_col[:, bass.ds((turn * SLOTS + s) * BS, BS)]).then_inc(idx_in[s], 16)

            for s in range(SLOTS):
                bring(0, s)
            with sp.Fori(0, NBLK // SLOTS) as it:
                for s in range(SLOTS):
                    sp.wait_ge(rows_in[s], (it + 1) * (16 * BS))
                    bring(it + 1, s)
            for s in range(SLOTS):
                sp.wait_ge(idx_in[s], 16 * (NBLK // SLOTS + 1))

        @block.gpsimd
        def _(pool):
            with pool.Fori(0, NBLK // SLOTS) as it:
                for s in range(SLOTS):
                    pool.wait_ge(idx_in[s], (it + 1) * 16)
                    pool.wait_ge(weighted_ready, (it * SLOTS + (s + 1)) * BS)
                    pool.sem_inc(idx_seen, 1)
                    for b in range(BS):
                        pool.indirect_dma_start(rows[s][:, b, :], None, k.h_rows[:, :],
                                                bass.IndirectOffsetOnAxis(ap=src_idx[s][:, b:b + 1], axis=0)).then_inc(rows_in[s], 16)

        @block.scalar
        def _(act):
            with act.Fori(0, NBLK // 2) as it:
                for s in range(2):
                    for b in range(BS):
                        v = (it * 2 + s) * BS + b
                        act.wait_ge(summed, v + 1)
                        nc.scalar.activation(away[:, b % 4, :], k.iota_row[:, :], ACT.Abs, scale=-1.0,
                                             bias=k.local_col[:, bass.ds(v, 1)]).then_inc(away_ready, 1)
                        act.wait_ge(away_ready, v + 1)
                        nc.scalar.activation(onehot[:, b % 4, :], away[:, b % 4, :], ACT.Relu, scale=-1.0, bias=1.0).then_inc(onehot_ready, 1)

        @block.tensor
        def _(pe):
            with pe.Fori(0, NBLK // 2) as it:
                for s in range(2):
                    for b in range(BS):
                        v = (it * 2 + s) * BS + b
                        pe.wait_ge(weighted_ready, v + (SLOTS * BS + 1))
                        pe.wait_ge(onehot_ready, v + 1)
                        pe.wait_ge(added, v + 1)
                        nc.tensor.matmul(ps_sum[b % 4][:, 0:ROW], onehot[:, b % 4, :], weighted[:, b % 4, :],
                                         start=True, stop=True).then_inc(summed, 1)

        @block.vector
        def _(dve):
            nc.vector.memset(k.acc[:, :, :], 0.0).then_inc(added, 4)
            dve.sem_inc(weighted_ready, SLOTS * BS)
            dve.sem_inc(summed, 4)

            def weigh(v, s, b):
                dve.wait_ge(summed, v + 1)
                nc.vector.tensor_tensor(heads(weighted[:, b % 4, :], HW), heads(rows[s][:, b, :], HW),
                                        k.alpha[:, bass.ds(v, 1), :].rearrange("p a h -> p h a").to_broadcast([P, H, HW]),
                                        ALU.mult).then_inc(weighted_ready, 1)

            def turn(it, last):
                tiles = [node_tiles(dve, k, it * SLOTS), None]
                for s in range(SLOTS):
                    for b in range(BS):
                        v = (it * SLOTS + s) * BS + b
                        ahead = s * BS + b + 2
                        at, a = ahead // BS, ahead % BS
                        if at < SLOTS or not last:
                            if a == 0:
                                dve.wait_ge(rows_in[at % SLOTS], (it + (1 + at // SLOTS)) * (16 * BS))
                            weigh(v + 2, at % SLOTS, a)
                        if b == BS // 2 and s < SLOTS - 1:
                            tiles[(s + 1) % 2] = node_tiles(dve, k, it * SLOTS + (s + 1))
                        tile = bass.ds(tiles[s % 2][b], 1)
                        dve.wait_ge(summed, v + 5)
                        dve.wait_ge(added, v + 4)
                        nc.vector.tensor_tensor(k.acc[:, tile, :], k.acc[:, tile, :], ps_sum[b % 4][:, 0:ROW], ALU.add).then_inc(added, 1)

            dve.wait_ge(rows_in[0], 16 * BS)
            weigh(0, 0, 0)
            weigh(1, 0, 1)
            with dve.Fori(0, NBLK // SLOTS - 1) as it:
                turn(it, False)
            turn(NBLK // SLOTS - 1, True)


def linear_attention(nc, k):
    with ExitStack() as ctx:
        sb, ps, sem = allocators(nc, ctx)
        q_max = sb("q_max", [P, NT * MH])
        q_sum = sb("q_sum", [P, NT * MH])
        beyond = sb("beyond", [P, 1])
        k_max = sb("k_max", [P, MHID])
        k_top = sb("k_top", [P, 4])
        k_top_b = sb("k_top_b", [P, P])
        k_top_row = sb("k_top_row", [P, P])
        mem_k = sb("mem_k", [P, MEM])
        mem_v = sb("mem_v", [P, MEM])
        mem_kt = sb("mem_kt", [MEM, P])
        mem_vt = sb("mem_vt", [MEM, P + 1])
        same_head = sb("same_head", [P, P])
        w_out = sb("w_out_sb", [P, C])
        b_out = sb("b_out_sb", [P, C])
        g_out = sb("g_out_sb", [P, C])
        bias = sb("bias_sb", [P, C])
        exp_k = sb("exp_k", [P, 4, P])
        context = sb("context", [P, P])
        context_t = sb("context_t", [P, P])
        mixer = sb("mixer", [P, C])
        k_total = sb("k_total", [P, 1])
        q_norm = sb("q_norm", [P, 4, P])
        q_t = sb("q_t", [P, 2, P])
        squares = sb("squares_dump", [P, 2, C])
        out_norm = sb("out_norm", [P, NT])
        xn = sb("xn_again", [P, G, C])
        rstd_1 = sb("rstd_1", [P, NT])
        base = sb("base_ring", [P, G, C])
        ps_a = ps("m_ps_a", [P, 512])
        ps_b = ps("m_ps_b", [P, 512])
        ps_c = ps("m_ps_c", [P, 512])
        ps_qt = [ps(f"ps_qt{i}", [P, 512]) for i in range(2)]
        ps_o = [ps(f"ps_o{i}", [P, 512]) for i in range(2)]
        small_in, masks_ready, q_shifted, q_exp = sem("small_in"), sem("masks_ready"), sem("q_shifted"), sem("q_exp")
        kmax_ready, kmax_turned, top_ready, top_spread, k_shifted = (
            sem("kmax_ready"), sem("kmax_turned"), sem("top_ready"), sem("top_spread"), sem("k_shifted"))
        mem_exp, mem_turned, mem_ready = sem("mem_exp"), sem("mem_turned"), sem("mem_ready")
        exp_ready, exp_used, context_done = sem("m_exp_ready"), sem("m_exp_used"), sem("context_done")
        ctx_ready, ctx_turned, ctx_t_ready, mixed, mixer_ready = (
            sem("ctx_ready"), sem("ctx_turned"), sem("ctx_t_ready"), sem("mixed"), sem("mixer_ready"))
        qn_ready, qn_turned, qt_ready, out_done, out_copied, squared = (
            sem("qn_ready"), sem("qn_turned"), sem("qt_ready"), sem("m_out_done"), sem("out_copied"), sem("m_squared"))
        roots, scale_ready, xn_ready, base_step, base_ready = (
            sem("roots"), sem("m_scale_ready"), sem("m_xn_ready"), sem("base_step"), sem("base_ready"))
        sources = SourceGathers(nc, k, sb, sem, "early", 0, EARLY)
        base_out = [sem(f"base_out{g}") for g in range(G)]
        dve_step, pool_step = sem("m_dve_step"), sem("m_pool_step")
        block = ctx.enter_context(nc.Block())
        q_heads = k.qkv[:, :, 0:MHID].rearrange("p t (h d) -> p t h d", d=MD)
        keys = k.qkv[:, :, MHID:2 * MHID]
        out_raw = k.qkv[:, :, 0:C]

        @block.sync
        def _(sp):
            sp.dma_start(mem_k[:, :], k.mem_kv[0].rearrange("h d m -> (h d) m")).then_inc(small_in, 16)
            sp.dma_start(mem_v[:, :], k.mem_kv[1].rearrange("h d m -> (h d) m")).then_inc(small_in, 16)
            sp.dma_start(w_out[:, :], k.w_out[:, :]).then_inc(small_in, 16)
            sp.dma_start(b_out[:, :], k.b_out.rearrange("(a c) -> a c", a=1).to_broadcast([P, C])).then_inc(small_in, 16)
            sp.dma_start(g_out[:, :], k.g_out.rearrange("(a c) -> a c", a=1).to_broadcast([P, C])).then_inc(small_in, 16)
            sp.dma_start(bias[:, :], k.bias.rearrange("(a c) -> a c", a=1).to_broadcast([P, C])).then_inc(small_in, 16)
            with sp.Fori(0, NT // G) as it:
                for g in range(G):
                    sp.wait_ge(base_ready, it * G + (g + 1 + G))
                    sp.dma_start(k.base_rows[bass.ds((it * G + g) * P, P), :], base[:, g, :]).then_inc(base_out[g], 16)
            for g in range(G):
                sp.wait_ge(base_out[g], 16 * (NT // G + 1))

        @block.gpsimd
        def _(pool):
            link = chain(pool, pool_step)
            nc.gpsimd.memset(mem_vt[:, :], 1.0).then_inc(masks_ready, 1)
            nc.gpsimd.memset(k.qkv[:, :, QW:QW + 1], 1.0).then_inc(masks_ready, 1)
            link(nc.gpsimd.memset(same_head[:, :], 1.0))
            link(nc.gpsimd.affine_select(out=heads(same_head[:, :], MD), in_=heads(same_head[:, :], MD), compare_op=ALU.is_ge,
                                         fill=0.0, base=0, pattern=[[-MD, MH], [0, MD]], channel_multiplier=1))
            nc.gpsimd.affine_select(out=heads(same_head[:, :], MD), in_=heads(same_head[:, :], MD), compare_op=ALU.is_ge,
                                    fill=0.0, base=MD - 1, pattern=[[MD, MH], [0, MD]], channel_multiplier=-1).then_inc(masks_ready, 1)
            sources.run(pool)

        @block.vector
        def _(dve):
            link = chain(dve, dve_step)
            link(nc.vector.tensor_reduce(q_max[:, :], q_heads, AX.X, ALU.max))
            nc.vector.tensor_tensor(q_heads, q_heads, q_max[:, :].rearrange("p (t h) -> p t h", h=MH).unsqueeze(3)
                                    .to_broadcast([P, NT, MH, MD]), ALU.subtract).then_inc(q_shifted, 1)
            link(nc.vector.tensor_scalar(beyond[:, :], k.iota_col[:, :], float(NLAST), -BIG, ALU.is_ge, ALU.mult))
            link(nc.vector.tensor_scalar(keys[:, NT - 1, :], keys[:, NT - 1, :], beyond[:, 0:1], None, ALU.add))
            nc.vector.tensor_reduce(k_max[:, :], keys.rearrange("p t c -> p c t"), AX.X, ALU.max).then_inc(kmax_ready, 1)
            dve.wait_ge(small_in, 96)
            link(nc.vector.tensor_reduce(k_top[:, 0:1], mem_k[:, :], AX.X, ALU.max))
            dve.wait_ge(kmax_turned, 1)
            link(nc.vector.tensor_reduce(k_top[:, 1:2], ps_a[:, 0:P], AX.X, ALU.max))
            link(nc.vector.tensor_tensor(k_top[:, 2:3], k_top[:, 0:1], k_top[:, 1:2], ALU.max))
            link(nc.vector.memset(k_top_b[:, :], 0.0))
            link(nc.vector.tensor_scalar(k_top_b[:, :], k_top_b[:, :], k_top[:, 2:3], None, ALU.add))
            nc.vector.tensor_scalar(k_top[:, 3:4], k_top[:, 2:3], -1.0, None, ALU.mult).then_inc(top_ready, 1)
            dve.wait_ge(top_spread, 1)
            link(nc.vector.tensor_copy(k_top_row[:, :], ps_b[:, 0:P]))
            nc.vector.tensor_tensor(keys, keys, k_top_row[:, :].unsqueeze(1).to_broadcast([P, NT, P]), ALU.subtract).then_inc(k_shifted, 1)
            dve.wait_ge(q_exp, 1)
            link(nc.vector.tensor_reduce(q_sum[:, :], q_heads, AX.X, ALU.add))
            link(nc.vector.reciprocal(q_sum[:, :], q_sum[:, :]))
            dve.wait_ge(mem_turned, 1)
            dve.wait_ge(masks_ready, 3)
            nc.vector.tensor_copy(mem_kt[:, :], ps_a[0:MEM, P:2 * P])
            nc.vector.tensor_copy(mem_vt[:, 0:P], ps_a[0:MEM, 2 * P:3 * P]).then_inc(mem_ready, 1)
            dve.wait_ge(context_done, 1)
            link(nc.vector.reciprocal(k_total[:, :], ps_c[:, P:P + 1]))
            link(nc.vector.tensor_scalar(k_total[:, :], k_total[:, :], float(MD) ** -0.5, None, ALU.mult))
            nc.vector.scalar_tensor_tensor(context[:, :], ps_c[:, 0:P], k_total[:, 0:1], same_head[:, :], ALU.mult, ALU.mult).then_inc(ctx_ready, 1)
            dve.wait_ge(ctx_turned, 1)
            nc.vector.tensor_copy(context_t[:, :], ps_b[:, P:2 * P]).then_inc(ctx_t_ready, 1)
            dve.wait_ge(mixed, 1)
            nc.vector.tensor_copy(mixer[:, :], ps_a[:, 0:C]).then_inc(mixer_ready, 1)
            dve.sem_inc(qn_turned, 4)

            def normed_q(t, g):
                dve.wait_ge(qn_turned, t + 1)
                nc.vector.tensor_tensor(q_norm[:, g % 4, :].rearrange("p (a h d) -> p a h d", a=1, d=MD), q_heads[:, bass.ds(t, 1)],
                                        q_sum[:, bass.ds(t * MH, MH)].rearrange("p (a h) -> p a h", a=1).unsqueeze(3)
                                        .to_broadcast([P, 1, MH, MD]), ALU.mult).then_inc(qn_ready, 1)

            def taken_out(t, s):
                dve.wait_ge(out_done, t + 1)
                dve.wait_ge(qn_ready, t + 1)
                nc.vector.tensor_tensor(out_raw[:, bass.ds(t, 1), :].rearrange("p a c -> p (a c)"), ps_o[s][:, 0:C], b_out[:, :],
                                        ALU.add).then_inc(out_copied, 1)

            normed_q(0, 0)
            normed_q(1, 1)
            with dve.Fori(0, NT // R - 1) as it:
                for g in range(R):
                    normed_q(it * R + (g + 2), g + 2)
                    taken_out(it * R + g, g % 2)
            for t in range(NT - 1 - R, NT):
                if t + 2 < NT:
                    normed_q(t + 2, t + 2)
                taken_out(t, t % 2)
            nc.vector.tensor_scalar(rstd_1[:, :], k.rstd[:, :], 1.0, None, ALU.add).then_inc(scale_ready, 1)
            dve.wait_ge(roots, 1)
            link(nc.vector.tensor_scalar(out_norm[:, :], out_norm[:, :], 1e-12, 1.0 / 16.0, ALU.max, ALU.mult))
            link(nc.vector.reciprocal(out_norm[:, :], out_norm[:, :]))
            dve.sem_inc(base_ready, G)
            for g in range(G):
                dve.sem_inc(base_out[g], 16)
            with dve.Fori(0, NT // G) as it:
                for g in range(G):
                    t = it * G + g
                    dve.wait_ge(base_out[g], it * 16 + 16)
                    nc.vector.scalar_tensor_tensor(base[:, g, :], out_raw[:, bass.ds(t, 1), :], out_norm[:, bass.ds(t, 1)],
                                                   g_out[:, :], ALU.mult, ALU.mult).then_inc(base_step, 1)
                    dve.wait_ge(xn_ready, t + 1)
                    dve.wait_ge(base_step, t * 2 + 1)
                    nc.vector.tensor_tensor(base[:, g, :], base[:, g, :], xn[:, g, :], ALU.add).then_inc(base_step, 1)
                    dve.wait_ge(base_step, t * 2 + 2)
                    nc.vector.tensor_tensor(base[:, g, :], base[:, g, :], bias[:, :], ALU.add).then_inc(base_ready, 1)

        @block.scalar
        def _(act):
            act.sem_inc(exp_used, 4)
            act.sem_inc(out_copied, 2)
            act.sem_inc(qt_ready, 2)
            act.sem_inc(squared, 2)
            act.wait_ge(q_shifted, 1)
            nc.scalar.activation(k.qkv[:, :, 0:MHID], k.qkv[:, :, 0:MHID], ACT.Exp).then_inc(q_exp, 1)
            act.wait_ge(top_ready, 1)
            nc.scalar.activation(mem_k[:, :], mem_k[:, :], ACT.Exp, bias=k_top[:, 3:4]).then_inc(mem_exp, 1)
            act.wait_ge(k_shifted, 1)
            nc.scalar.activation(exp_k[:, 0, :], keys[:, 0, :], ACT.Exp).then_inc(exp_ready, 1)
            with act.Fori(0, (NT - 1) // 4) as it:
                for g in range(4):
                    act.wait_ge(exp_used, it * 4 + (g + 2))
                    nc.scalar.activation(exp_k[:, (g + 1) % 4, :], keys[:, bass.ds(it * 4 + (g + 1), 1), :], ACT.Exp).then_inc(exp_ready, 1)

            def turned_q(t, s):
                act.wait_ge(qn_turned, t + 5)
                nc.scalar.copy(q_t[:, s, :], ps_qt[s][:, 0:P]).then_inc(qt_ready, 1)

            def squares_of(t, s):
                act.wait_ge(out_copied, t + 3)
                act.wait_ge(squared, t + 1)
                nc.scalar.activation(squares[:, s, :], out_raw[:, bass.ds(t, 1), :], ACT.Square, accum_out=out_norm[:, bass.ds(t, 1)]).then_inc(squared, 1)

            turned_q(0, 0)
            with act.Fori(0, NT // R) as it:
                for g in range(R):
                    turned_q(it * R + (g + 1), (g + 1) % 2)
                    squares_of(it * R + g, g % 2)
            squares_of(NT - 1, 0)
            act.wait_ge(squared, NT + 2)
            nc.scalar.activation(out_norm[:, :], out_norm[:, :], ACT.Sqrt).then_inc(roots, 1)
            act.wait_ge(scale_ready, 1)
            with act.Fori(0, NT // G) as it:
                for g in range(G):
                    t = it * G + g
                    act.wait_ge(base_ready, t + 1)
                    nc.scalar.activation(xn[:, g, :], k.x_res[:, bass.ds(t, 1), :], ACT.Identity, scale=rstd_1[:, bass.ds(t, 1)],
                                         bias=k.shift[:, bass.ds(t, 1)]).then_inc(xn_ready, 1)

        @block.tensor
        def _(pe):
            pe.wait_ge(kmax_ready, 1)
            nc.tensor.transpose(ps_a[:, 0:P], k_max[:, :], k.ident[:, :]).then_inc(kmax_turned, 1)
            pe.wait_ge(top_ready, 1)
            nc.tensor.matmul(ps_b[:, 0:P], k_top_b[:, :], k.ident[:, :], start=True, stop=True).then_inc(top_spread, 1)
            pe.wait_ge(mem_exp, 1)
            nc.tensor.transpose(ps_a[0:MEM, P:2 * P], mem_k[:, :], k.ident[:, :])
            nc.tensor.transpose(ps_a[0:MEM, 2 * P:3 * P], mem_v[:, :], k.ident[:, :]).then_inc(mem_turned, 1)
            pe.wait_ge(masks_ready, 3)
            pe.wait_ge(exp_ready, 1)
            nc.tensor.matmul(ps_c[:, 0:P + 1], exp_k[:, 0, :], k.qkv[:, 0, 2 * MHID:QW + 1], start=True, stop=False).then_inc(exp_used, 1)
            with pe.Fori(0, (NT - 1) // 4) as it:
                for g in range(4):
                    pe.wait_ge(exp_ready, it * 4 + (g + 2))
                    nc.tensor.matmul(ps_c[:, 0:P + 1], exp_k[:, (g + 1) % 4, :], k.qkv[:, bass.ds(it * 4 + (g + 1), 1), 2 * MHID:QW + 1],
                                     start=False, stop=False).then_inc(exp_used, 1)
            pe.wait_ge(mem_ready, 1)
            nc.tensor.matmul(ps_c[:, 0:P + 1], mem_kt[:, :], mem_vt[:, :], start=False, stop=True).then_inc(context_done, 1)
            pe.wait_ge(ctx_ready, 1)
            nc.tensor.transpose(ps_b[:, P:2 * P], context[:, :], k.ident[:, :]).then_inc(ctx_turned, 1)
            pe.wait_ge(ctx_t_ready, 1)
            nc.tensor.matmul(ps_a[:, 0:C], context_t[:, :], w_out[:, :], start=True, stop=True).then_inc(mixed, 1)
            pe.wait_ge(mixer_ready, 1)

            def turn_q(t, g):
                pe.wait_ge(qn_ready, t + 1)
                pe.wait_ge(qt_ready, t + 1)
                nc.tensor.transpose(ps_qt[g % 2][:, 0:P], q_norm[:, g % 4, :], k.ident[:, :]).then_inc(qn_turned, 1)

            def output(t, s):
                pe.wait_ge(qt_ready, t + 3)
                pe.wait_ge(out_copied, t + 1)
                nc.tensor.matmul(ps_o[s][:, 0:C], q_t[:, s, :], mixer[:, :], start=True, stop=True).then_inc(out_done, 1)

            turn_q(0, 0)
            with pe.Fori(0, NT // R) as it:
                for g in range(R):
                    turn_q(it * R + (g + 1), g + 1)
                    output(it * R + g, g % 2)
            output(NT - 1, 0)


def gate(nc, k):
    with ExitStack() as ctx:
        sb, ps, sem = allocators(nc, ctx)
        x1 = sb("x1", [P, NT, C])
        den = sb("den", [P, NT * H])
        stats = sb("stats2", [P, NT, 6])
        mv = sb("mv2", [P, NT, 2])
        std = sb("std2", [P, NT])
        rstd, shift = k.rstd_out, k.shift_out
        wg_in = sb("wg_in", [NE, C])
        wg_t = sb("wg_t", [P, 2, NE])
        bg = sb("bg_rows", [P, NE])
        ones = sb("ones_sq", [P, P])
        before = sb("before", [P, P])
        y = sb("y", [P, R, C])
        y_t = sb("y_t", [P, 2, 2, P])
        score = sb("score", [P, NT, NE])
        score2 = sb("score2", [P, NT, NE])
        expert_i = sb("expert_i", [P, NT, NE], I32)
        expert_no = sb("expert_no", [P, NT, NE])
        cand = sb("cand", [P, NT, NE])
        first = sb("first", [P, NT, NE])
        second = sb("second", [P, NT, NE])
        both = sb("both", [P, NT, NE])
        top = sb("top", [P, 2, NT])
        which = sb("which", [P, NT])
        gap = sb("gap", [P, NT])
        totals = sb("totals", [P, NT, NE])
        upto = sb("upto", [P, NT, NE])
        place = sb("place", [P, NT, NE])
        count_i = sb("count_i", [P, NE], I32)
        padded = sb("padded_count", [P, NE])
        ends = sb("ends", [P, NE])
        starts = sb("starts", [P, NE])
        block_i = sb("block_i", [P, NB, NE], I32)
        block_no = sb("block_no", [P, NB, NE])
        expert_f = sb("expert_f", [P, NB])
        place_f = sb("place_f", [P, 2, NT])
        weights = sb("weights", [P, 2, NT])
        tile_start_i = sb("tile_start_i", [P, NB], I32)
        tile_start = sb("tile_start", [P, NT])
        ps_w = ps("g_ps_w", [P, 512])
        ps_t = [ps(f"g_ps_t{i}", [P, 512]) for i in range(2)]
        ps_s = ps("g_ps_s", [P, NT * NE])
        ps_before = ps("ps_before", [P, 512])
        ps_total = ps("ps_total", [P, 512])
        base_in, w_in, consts_ready, dve_step, pool_step = sem("base_in"), sem("g_w_in"), sem("g_consts"), sem("g_dve_step"), sem("g_pool_step")
        x1_ready, x1_out, stat_steps, moments_ready, std_ready = (
            sem("x1_ready"), sem("x1_out"), sem("g_stat_steps"), sem("g_moments"), sem("g_std"))
        wg_turned, wg_ready, y_ready, y_turned, yt_ready, scored = (
            sem("wg_turned"), sem("wg_ready"), sem("y_ready"), sem("y_turned"), sem("yt_ready"), sem("scored"))
        gap_ready, gap_exp, picked, counted = sem("gap_ready"), sem("gap_exp"), sem("picked"), sem("counted")
        block = ctx.enter_context(nc.Block())
        sums = k.acc[:, :, :].rearrange("p t (h w) -> p (t h) w", w=HW)

        @block.sync
        def _(sp):
            for t in range(0, NT, G):
                sp.dma_start(x1[:, t:t + G, :], k.base_rows[t * P:(t + G) * P, :].rearrange("(t p) c -> p t c", p=P)).then_inc(base_in, 16)
            sp.dma_start(wg_in[:, :], k.Wg[:, :]).then_inc(w_in, 16)
            sp.dma_start(bg[:, :], k.bg.rearrange("(a e) -> a e", a=1).to_broadcast([P, NE])).then_inc(w_in, 16)
            sp.wait_ge(x1_ready, 1)
            for t in range(0, NT, G):
                sp.dma_start(k.node_out[t * P + 1:(t + G) * P + 1, :].rearrange("(t p) c -> p t c", p=P), x1[:, t:t + G, :]).then_inc(x1_out, 16)
            sp.wait_ge(x1_out, 16 * (NT // G))

        @block.gpsimd
        def _(pool):
            link = chain(pool, pool_step)
            nc.gpsimd.memset(ones[:, :], 1.0).then_inc(consts_ready, 1)
            link(nc.gpsimd.memset(before[:, :], 1.0))
            nc.gpsimd.affine_select(out=before[:, :], in_=before[:, :], compare_op=ALU.is_gt, fill=0.0, base=0,
                                    pattern=[[1, P]], channel_multiplier=-1).then_inc(consts_ready, 1)
            link(nc.gpsimd.iota(expert_i[:, :, :], [[0, NT], [1, NE]], 0, 0))
            nc.gpsimd.tensor_copy(expert_no[:, :, :], expert_i[:, :, :]).then_inc(consts_ready, 1)
            link(nc.gpsimd.iota(block_i[:, :, :], [[1, NB], [0, NE]], 0, 0))
            nc.gpsimd.tensor_copy(block_no[:, :, :], block_i[:, :, :]).then_inc(consts_ready, 1)
            link(nc.gpsimd.iota(tile_start_i[:, :], [[P, NB]], 0, 0))
            nc.gpsimd.tensor_copy(tile_start[:, :], tile_start_i[:, 0:NT]).then_inc(consts_ready, 1)
            pool.wait_ge(consts_ready, 5)
            link(nc.gpsimd.iota(tile_start_i[:, :], [[P, NB]], 0, 1))
            nc.gpsimd.tensor_copy(k.list_row[:, :], tile_start_i[:, :]).then_inc(consts_ready, 1)
            pool.wait_ge(consts_ready, 6)
            link(nc.gpsimd.iota(tile_start_i[:, 0:1], [[1, 1]], NPAD + 1, 1))
            nc.gpsimd.tensor_copy(k.no_node[:, :], tile_start_i[:, 0:1]).then_inc(consts_ready, 1)

        @block.vector
        def _(dve):
            link = chain(dve, dve_step)
            link(nc.vector.tensor_scalar(den[:, :], sums[:, :, D], 1e-10, None, ALU.max))
            link(nc.vector.reciprocal(den[:, :], den[:, :]))
            link(nc.vector.tensor_tensor(sums[:, :, 0:D], sums[:, :, 0:D], den[:, :].unsqueeze(2).to_broadcast([P, NT * H, D]), ALU.mult))
            dve.wait_ge(base_in, 16 * (NT // G))
            x1_heads = x1[:, :, :].rearrange("p t (h d) -> p (t h) d", d=D)
            link(nc.vector.tensor_tensor(x1_heads, x1_heads, sums[:, :, 0:D], ALU.add))
            dve.sem_inc(x1_ready, 1)
            with dve.Fori(0, NT // G) as it:
                for g in range(G):
                    t = it * G + g
                    nc.vector.bn_stats(stats[:, bass.ds(t, 1), :], x1[:, bass.ds(t, 1), :]).then_inc(stat_steps, 1)
            dve.wait_ge(stat_steps, NT)
            moments(nc, link, stats, mv, moments_ready)
            dve.wait_ge(moments_ready, 1)
            dve.wait_ge(std_ready, 1)
            link(nc.vector.reciprocal(rstd[:, :], std[:, :]))
            link(nc.vector.scalar_tensor_tensor(shift[:, :], mv[:, :, 0], -1.0, rstd[:, :], ALU.mult, ALU.mult))
            dve.wait_ge(wg_turned, 1)
            nc.vector.tensor_copy(wg_t[:, :, :], ps_w[:, 0:2 * NE].rearrange("p (a e) -> p a e", a=2)).then_inc(wg_ready, 1)
            dve.sem_inc(y_turned, R)

            def normed(t, g):
                dve.wait_ge(y_turned, t + 1)
                nc.vector.tensor_scalar(y[:, g, :], x1[:, bass.ds(t, 1), :].rearrange("p a c -> p (a c)"),
                                        rstd[:, bass.ds(t, 1)], shift[:, bass.ds(t, 1)], ALU.mult, ALU.add).then_inc(y_ready, 1)

            with dve.Fori(0, NT // R) as it:
                for g in range(R):
                    normed(it * R + g, g)
            normed(NT - 1, 0)
            dve.wait_ge(scored, NT + 2)
            link(nc.vector.tensor_tensor(score[:, :, :], ps_s[:, :].rearrange("p (t e) -> p t e", e=NE),
                                         bg[:, :].unsqueeze(1).to_broadcast([P, NT, NE]), ALU.add))
            dve.wait_ge(consts_ready, 7)

            def across(ap):
                return ap.unsqueeze(2).to_broadcast([P, NT, NE])

            for n, (s, hot) in enumerate(((score, first), (score2, second))):
                link(nc.vector.tensor_reduce(top[:, n, :], s[:, :, :], AX.X, ALU.max))
                link(nc.vector.tensor_tensor(cand[:, :, :], s[:, :, :], across(top[:, n, :]), ALU.is_equal))
                link(nc.vector.tensor_scalar(cand[:, :, :], cand[:, :, :], -100.0, None, ALU.mult))
                link(nc.vector.tensor_tensor(cand[:, :, :], cand[:, :, :], expert_no[:, :, :], ALU.add))
                link(nc.vector.tensor_reduce(which[:, :], cand[:, :, :], AX.X, ALU.min))
                link(nc.vector.tensor_scalar(which[:, :], which[:, :], 100.0, None, ALU.add))
                link(nc.vector.tensor_tensor(hot[:, :, :], expert_no[:, :, :], across(which[:, :]), ALU.is_equal))
                if n == 0:
                    link(nc.vector.tensor_scalar(cand[:, :, :], hot[:, :, :], -BIG, None, ALU.mult))
                    link(nc.vector.tensor_tensor(score2[:, :, :], score[:, :, :], cand[:, :, :], ALU.add))
            nc.vector.tensor_tensor(gap[:, :], top[:, 1, :], top[:, 0, :], ALU.subtract).then_inc(gap_ready, 1)
            nc.vector.tensor_tensor(both[:, :, :], first[:, :, :], second[:, :, :], ALU.add).then_inc(picked, 1)
            dve.wait_ge(gap_exp, 1)
            link(nc.vector.tensor_scalar(weights[:, 0, :], gap[:, :], 1.0, None, ALU.add))
            link(nc.vector.reciprocal(weights[:, 0, :], weights[:, 0, :]))
            link(nc.vector.tensor_tensor(weights[:, 1, :], weights[:, 0, :], gap[:, :], ALU.mult))
            dve.wait_ge(counted, 1)
            link(nc.vector.tensor_copy(totals[:, :, :], ps_total[:, 0:NT * NE].rearrange("p (t e) -> p t e", e=NE)))
            for e in range(NE):
                link(nc.vector.tensor_tensor_scan(upto[:, :, e], ones[:, 0:NT], totals[:, :, e], 0.0, ALU.mult, ALU.add))
            link(nc.vector.tensor_scalar(count_i[:, :], upto[:, NT - 1, :], float(P - 1), None, ALU.add))
            link(nc.vector.tensor_scalar(count_i[:, :], count_i[:, :], 7, None, ALU.arith_shift_right))
            link(nc.vector.tensor_copy(padded[:, :], count_i[:, :]))
            link(nc.vector.tensor_tensor_scan(ends[:, :], ones[:, 0:NE], padded[:, :], 0.0, ALU.mult, ALU.add))
            link(nc.vector.tensor_tensor(starts[:, :], ends[:, :], padded[:, :], ALU.subtract))
            link(nc.vector.tensor_scalar(starts[:, :], starts[:, :], float(P), None, ALU.mult))
            link(nc.vector.tensor_tensor(upto[:, :, :], upto[:, :, :], totals[:, :, :], ALU.subtract))
            link(nc.vector.tensor_tensor(upto[:, :, :], upto[:, :, :], starts[:, :].unsqueeze(1).to_broadcast([P, NT, NE]), ALU.add))
            link(nc.vector.tensor_tensor(upto[:, :, :], upto[:, :, :], ps_before[:, 0:NT * NE].rearrange("p (t e) -> p t e", e=NE), ALU.add))
            for n, hot in enumerate((first, second)):
                link(nc.vector.tensor_tensor(place[:, :, :], upto[:, :, :], hot[:, :, :], ALU.mult))
                link(nc.vector.tensor_reduce(place_f[:, n, :], place[:, :, :], AX.X, ALU.add))
            link(nc.vector.tensor_copy(k.places[:, :, :], place_f[:, :, :]))
            link(nc.vector.tensor_scalar(k.tags[:, :, 0], tile_start[:, :], k.iota_col[:, 0:1], 1.0, ALU.add, ALU.add))
            link(nc.vector.tensor_copy(k.tags[:, :, 1], place_f[:, 0, :]))
            link(nc.vector.tensor_copy(k.tags[:, :, 2], weights[:, 1, :]))
            link(nc.vector.tensor_tensor(k.tags[:, :, 3], weights[:, 0, :], weights[:, 1, :], ALU.subtract))
            link(nc.vector.tensor_tensor(block_no[:, :, :], block_no[:, :, :], ends[:, :].unsqueeze(1).to_broadcast([P, NB, NE]), ALU.is_ge))
            link(nc.vector.tensor_reduce(expert_f[:, :], block_no[:, :, :], AX.X, ALU.add))
            link(nc.vector.tensor_scalar(expert_f[:, :], expert_f[:, :], float(NE - 1), None, ALU.min))
            link(nc.vector.tensor_copy(k.expert_row[:, :], expert_f[0:1, :]))

        @block.scalar
        def _(act):
            act.sem_inc(yt_ready, 2)
            act.sem_inc(scored, 2)
            act.wait_ge(moments_ready, 1)
            nc.scalar.activation(std[:, :], mv[:, :, 1], ACT.Sqrt, bias=k.eps[:, 0:1]).then_inc(std_ready, 1)

            def turned_copy(t, s):
                act.wait_ge(y_turned, t + (R + 1))
                act.wait_ge(scored, t + 1)
                nc.scalar.copy(y_t[:, s].rearrange("p a n -> p (a n)"), ps_t[s][:, 0:C]).then_inc(yt_ready, 1)

            with act.Fori(0, NT // R) as it:
                for g in range(R):
                    turned_copy(it * R + g, g % 2)
            turned_copy(NT - 1, 0)
            act.wait_ge(gap_ready, 1)
            nc.scalar.activation(gap[:, :], gap[:, :], ACT.Exp).then_inc(gap_exp, 1)

        @block.tensor
        def _(pe):
            pe.wait_ge(w_in, 32)
            for a in range(2):
                last = nc.tensor.transpose(ps_w[:, NE * a:NE * (a + 1)], wg_in[:, a * P:(a + 1) * P], k.ident[0:NE, 0:NE])
            last.then_inc(wg_turned, 1)
            pe.wait_ge(wg_ready, 1)
            pe.wait_ge(consts_ready, 2)

            def turn_rows(t, g):
                pe.wait_ge(y_ready, t + 1)
                pe.wait_ge(yt_ready, t + 1)
                for a in range(2):
                    last = nc.tensor.transpose(ps_t[g % 2][:, a * P:(a + 1) * P], y[:, g % R, a * P:(a + 1) * P], k.ident[:, :])
                last.then_inc(y_turned, 1)

            def score_tile(t, s):
                pe.wait_ge(yt_ready, t + 3)
                out = ps_s[:, bass.ds(t * NE, NE)]
                for a in range(2):
                    last = nc.tensor.matmul(out, y_t[:, s, a, :], wg_t[:, a, :], start=a == 0, stop=a == 1)
                last.then_inc(scored, 1)

            turn_rows(0, 0)
            with pe.Fori(0, NT // R) as it:
                for g in range(R):
                    turn_rows(it * R + (g + 1), g + 1)
                    score_tile(it * R + g, g % 2)
            score_tile(NT - 1, 0)
            pe.wait_ge(picked, 1)
            flat = both[:, :, :].rearrange("p t e -> p (t e)")
            nc.tensor.matmul(ps_before[:, 0:NT * NE], before[:, :], flat, start=True, stop=True)
            nc.tensor.matmul(ps_total[:, 0:NT * NE], ones[:, :], flat, start=True, stop=True).then_inc(counted, 1)


def dispatch_and_weights(nc, k):
    with ExitStack() as ctx:
        sb, ps, sem = allocators(nc, ctx)
        y = [sb(f"y_out{h}", [P, G, LW]) for h in range(2)]
        place_idx = [sb(f"place_idx{h}", [P, 2, G], U32) for h in range(2)]
        x1_in = [sem(f"d_x1_in{h}") for h in range(2)]
        sent = [sem(f"sent{h}") for h in range(2)]
        y_ready, idx_ready, pool_seen = sem("d_y_ready"), sem("d_idx_ready"), sem("d_pool_seen")
        w1_in = [sb(f"w1_in{s}", [P, 8, C]) for s in range(2)]
        w2_in = [sb(f"w2_in{s}", [P, 2, HID]) for s in range(2)]
        b1_in = sb("b1_in_sb", [B1_ROWS, P])
        b2_in = sb("b2_in_sb", [B2_ROWS, P])
        b2_rest = sb("b2_rest", [B2_ROWS, P])
        b2_parts = sb("b2_parts", [B2_ROWS, 3, P], BF16)
        ps_a = [ps(f"w_ps_a{i}", [P, 512]) for i in range(4)]
        ps_d = [ps(f"w_ps_d{i}", [P, 512]) for i in range(4)]
        w_in = [sem(f"ew_in{s}") for s in range(2)]
        turned_a, turned_d, copied_a, copied_d = sem("turned_a"), sem("turned_d"), sem("copied_a"), sem("copied_d")
        b_in, b_split, b_out, dve_step = sem("b_in"), sem("b_split"), sem("b_out"), sem("w_dve_step")
        b1_turned, b1_ready = sem("b1_turned"), sem("b1_ready")
        block = ctx.enter_context(nc.Block())

        @block.sync
        def _(sp):
            sp.dma_start(b1_in[:, :], k.b1.rearrange("e (i p) -> (e i) p", p=P)).then_inc(b_in, 16)
            sp.dma_start(b2_in[:, :], k.b2.rearrange("e (i p) -> (e i) p", p=P)).then_inc(b_in, 16)

            def bring_rows(n, h):
                rows = k.node_out[bass.ds((n * 2 + h) * (G * P) + 1, G * P), :].rearrange("(t p) c -> p t c", p=P)
                sp.dma_start(y[h][:, :, 0:C], rows).then_inc(x1_in[h], 16)

            def bring_weights(n, s):
                e = n * 2 + s
                sp.wait_ge(w_in[s], n * 32 + 1)
                sp.wait_ge(turned_a, e * 4 + 4)
                sp.wait_ge(turned_d, e * 4 + 4)
                sp.dma_start(w1_in[s][:, :, :], k.W1[bass.ds(e, 1), :, :].rearrange("e (i p) c -> p (e i) c", p=P)).then_inc(w_in[s], 16)
                sp.dma_start(w2_in[s][:, :, :], k.W2[bass.ds(e, 1), :, :].rearrange("e (i p) c -> p (e i) c", p=P)).then_inc(w_in[s], 16)

            bring_rows(0, 0)
            bring_rows(0, 1)
            for s in range(2):
                bring_weights(0, s)
            with sp.Fori(1, NT // G // 2) as it:
                for s in range(2):
                    sp.wait_ge(sent[s], it * (32 * G))
                    bring_rows(it, s)
                    bring_weights(it, s)
            sp.wait_ge(sent[0], NT // G // 2 * (32 * G))
            bring_rows(NT // G // 2, 0)
            for s in range(2):
                bring_weights(NE // 2 - 1, s)
            sp.wait_ge(b_split, 1)
            sp.dma_start(k.bias_rows.rearrange("j (r p) -> r j p", p=P), b2_parts[:, :, :]).then_inc(b_out, 16)
            sp.wait_ge(b_out, 16)
            sp.dma_start(k.biases[:, :], k.bias_rows[:, :]).then_inc(b_out, 16)
            sp.wait_ge(b_out, 32)

        @block.gpsimd
        def _(pool):
            def dispatch(n, h):
                nc.gpsimd.tensor_copy(place_idx[h][:, :, :], k.places[:, :, bass.ds((n * 2 + h) * G, G)]).then_inc(idx_ready, 1)
                pool.wait_ge(idx_ready, n * 2 + (h + 1))
                pool.wait_ge(y_ready, (n * 2 + (h + 1)) * G)
                pool.sem_inc(pool_seen, 1)
                for g in range(G):
                    for a in range(2):
                        pool.indirect_dma_start(k.list_rows[:, :], bass.IndirectOffsetOnAxis(ap=place_idx[h][:, a, g:g + 1], axis=0),
                                                y[h][:, g, :], None).then_inc(sent[h], 16)

            dispatch(0, 0)
            dispatch(0, 1)
            with pool.Fori(1, NT // G // 2) as it:
                for h in range(2):
                    pool.wait_ge(sent[h], it * (32 * G))
                    pool.sem_inc(pool_seen, 1)
                    dispatch(it, h)
            pool.wait_ge(sent[0], NT // G // 2 * (32 * G))
            dispatch(NT // G // 2, 0)
            pool.wait_ge(sent[0], (NT // G // 2 + 1) * (32 * G))
            pool.wait_ge(sent[1], NT // G // 2 * (32 * G))

        @block.tensor
        def _(pe):
            pe.wait_ge(b_in, 32)
            nc.tensor.transpose(ps_a[0][:, 0:B1_ROWS], b1_in[:, :], k.ident[0:B1_ROWS, 0:B1_ROWS]).then_inc(b1_turned, 1)
            pe.wait_ge(b1_ready, 1)
            with pe.Fori(0, NE // 2) as it:
                for s in range(2):
                    e = it * 2 + s
                    pe.wait_ge(w_in[s], it * 32 + 33)
                    for n in range(4):
                        pe.wait_ge(copied_a, e * 4 + (n + 1))
                        for i in range(4):
                            a, chunk = n // 2, (n % 2) * 4 + i
                            last = nc.tensor.transpose(ps_a[n][:, i * P:(i + 1) * P], w1_in[s][:, chunk, a * P:(a + 1) * P], k.ident[:, :])
                        last.then_inc(turned_a, 1)
                        pe.wait_ge(copied_d, e * 4 + (n + 1))
                        for i in range(4):
                            chunk, a = n * 2 + i // 2, i % 2
                            last = nc.tensor.transpose(ps_d[n][:, i * P:(i + 1) * P], w2_in[s][:, a, chunk * P:(chunk + 1) * P], k.ident[:, :])
                        last.then_inc(turned_d, 1)

        @block.scalar
        def _(act):
            act.sem_inc(w_in[0], 1)
            act.sem_inc(w_in[1], 1)
            act.sem_inc(turned_a, 8)
            act.sem_inc(copied_a, 4)
            act.sem_inc(turned_d, 8)
            act.sem_inc(copied_d, 4)
            with act.Fori(0, NE) as e:
                for n in range(4):
                    act.wait_ge(turned_a, e * 4 + (n + 9))
                    nc.scalar.copy(k.w1_t[:, bass.ds(e * 4 + n, 1), :], ps_a[n][:, :]).then_inc(copied_a, 1)
                    act.wait_ge(turned_d, e * 4 + (n + 9))
                    nc.scalar.copy(k.w2_t[:, bass.ds(e * 4 + n, 1), :], ps_d[n][:, :]).then_inc(copied_d, 1)

        @block.vector
        def _(dve):
            link = chain(dve, dve_step)
            dve.wait_ge(b_in, 32)
            link(nc.vector.tensor_copy(b2_parts[:, 0, :], b2_in[:, :]))
            link(nc.vector.tensor_tensor(b2_rest[:, :], b2_in[:, :], b2_parts[:, 0, :], ALU.subtract))
            link(nc.vector.tensor_copy(b2_parts[:, 1, :], b2_rest[:, :]))
            nc.vector.tensor_tensor(b2_parts[:, 2, :], b2_rest[:, :], b2_parts[:, 1, :], ALU.subtract).then_inc(b_split, 1)
            dve.wait_ge(b1_turned, 1)
            nc.vector.tensor_copy(k.b1_cols[:, :], ps_a[0][:, 0:B1_ROWS]).then_inc(b1_ready, 1)
            def normed(n, h):
                dve.wait_ge(x1_in[h], n * 16 + 16)
                for g in range(G):
                    t = (n * 2 + h) * G + g
                    nc.vector.tensor_scalar(y[h][:, g, 0:C], y[h][:, g, 0:C], k.rstd_out[:, bass.ds(t, 1)], k.shift_out[:, bass.ds(t, 1)],
                                            ALU.mult, ALU.add)
                nc.vector.tensor_copy(y[h][:, :, C:LW], k.tags[:, bass.ds((n * 2 + h) * G, G), :]).then_inc(y_ready, G)

            with dve.Fori(0, NT // G // 2) as it:
                for h in range(2):
                    normed(it, h)
            normed(NT // G // 2, 0)


def experts(nc, k):
    with ExitStack() as ctx:
        sb, ps, sem = allocators(nc, ctx)
        rows = [sb(f"e_rows{s}", [P, LW]) for s in range(2)]
        rows_t = [sb(f"e_rows_t{s}", [P, C]) for s in range(2)]
        hidden = sb("hidden", [P, HID])
        hidden_t = sb("hidden_t", [P, 8, P])
        out = [sb(f"e_out{s}", [P, C]) for s in range(2)]
        row_weight = [sb(f"row_weight{s}", [P, 1]) for s in range(2)]
        node_f = sb("node_f", [P, 2])
        node_row = [sb(f"node_row{s}", [P, 1], U32) for s in range(2)]
        ones = sb("e_ones", [3, P], BF16)
        ps_x = ps("e_ps_x", [P, 512])
        ps_h = [ps(f"e_ps_h{i}", [P, 512]) for i in range(2)]
        ps_ht = [ps(f"e_ps_ht{i}", [P, 512]) for i in range(2)]
        ps_y = ps("e_ps_y", [P, 512])
        rows_in = [sem(f"e_rows_in{s}") for s in range(2)]
        out_sent = [sem(f"e_out_sent{s}") for s in range(2)]
        turned, xt_ready, h_done = sem("e_turned"), sem("e_xt_ready"), sem("e_h_done")
        taken_a, taken_d, ht_done, ht_a, ht_d, y_done, y_copied, set_up = (
            sem("taken_a"), sem("taken_d"), sem("ht_done"), sem("ht_a"), sem("ht_d"), sem("y_done"), sem("y_copied"), sem("e_set_up"))
        pool_seen, tag_step, tags_read, copied = sem("e_pool_seen"), sem("tag_step"), sem("tags_read"), sem("copied_out")
        block = ctx.enter_context(nc.Block())
        pairs = (NB - 2) // 2

        def expert_of(eng, i):
            return eng.value_load(k.expert_row[0:1, bass.ds(i, 1)], min_val=0, max_val=NE - 1)

        @block.sync
        def _(sp):
            for i in range(2):
                sp.dma_start(rows[i][:, :], k.list_rows[i * P:(i + 1) * P, :]).then_inc(rows_in[i], 16)
            with sp.Fori(0, pairs) as it:
                for s in range(2):
                    i = it * 2 + (2 + s)
                    sp.wait_ge(tags_read, i - 1)
                    sp.dma_start(rows[s][:, :], k.list_rows[bass.ds(i * P, P), :]).then_inc(rows_in[s], 16)
            sp.wait_ge(copied, 1)
            sp.dma_start(k.out[:, :], k.node_out[1:N + 1, :]).then_inc(copied, 16)
            sp.wait_ge(copied, 17)

        @block.gpsimd
        def _(pool):
            def add_rows(i, s):
                pool.wait_ge(y_copied, i + 2)
                pool.sem_inc(pool_seen, 1)
                pool.indirect_dma_start(k.node_out[:, :], bass.IndirectOffsetOnAxis(ap=node_row[s][:, 0:1], axis=0),
                                        out[s][:, :], None, compute_op=ALU.add).then_inc(out_sent[s], 16)

            add_rows(0, 0)
            pool.wait_ge(out_sent[0], 16)
            add_rows(1, 1)
            with pool.Fori(1, pairs) as it:
                pool.wait_ge(out_sent[1], it * 16)
                add_rows(it * 2, 0)
                pool.wait_ge(out_sent[0], it * 16 + 16)
                add_rows(it * 2 + 1, 1)
            pool.wait_ge(out_sent[1], pairs * 16)
            add_rows(NB - 2, 0)
            pool.wait_ge(out_sent[0], 16 * (pairs + 1))
            pool.sem_inc(copied, 1)

        def turn(pe, s, i, n):
            pe.wait_ge(rows_in[s], n * 16)
            pe.wait_ge(xt_ready, i + 1)
            for a in range(2):
                last = nc.tensor.transpose(ps_x[:, a * P:(a + 1) * P], rows[s][:, a * P:(a + 1) * P], k.ident[:, :])
            last.then_inc(turned, 1)

        def up(pe, s, i, e):
            pe.wait_ge(xt_ready, i + 2)
            pe.wait_ge(taken_a, i + 1)
            pe.wait_ge(taken_d, i + 1)
            for n in range(2):
                for a in range(2):
                    last = nc.tensor.matmul(ps_h[n][:, :], rows_t[s][:, a * P:(a + 1) * P],
                                            k.w1_t[:, bass.ds(e * 4 + (2 * a + n), 1), :], start=a == 0, stop=a == 1)
                last.then_inc(h_done, 1)

        def turn_hidden(pe, i):
            for n in range(2):
                pe.wait_ge((taken_a, taken_d)[n], i + 2)
                pe.wait_ge((ht_a, ht_d)[n], i + 1)
                for m in range(4):
                    last = nc.tensor.transpose(ps_ht[n][:, m * P:(m + 1) * P], hidden[:, (4 * n + m) * P:(4 * n + m + 1) * P], k.ident[:, :])
                last.then_inc(ht_done, 1)

        def down(pe, i, e):
            pe.wait_ge(y_copied, i + 1)
            nc.tensor.matmul(ps_y[:, 0:C], ones[:, :], k.biases[:, bass.ds(e * C, C)], start=True, stop=False)
            for m in range(8):
                if m % 4 == 0:
                    pe.wait_ge((ht_a, ht_d)[m // 4], i + 2)
                last = nc.tensor.matmul(ps_y[:, 0:C], hidden_t[:, m, :],
                                        k.w2_t[:, bass.ds(e * 4 + m // 2, 1), (m % 2) * C:(m % 2 + 1) * C], start=False, stop=m == 7)
            last.then_inc(y_done, 1)

        @block.tensor
        def _(pe):
            pe.wait_ge(set_up, 1)
            turn(pe, 0, 0, 1)
            turn(pe, 1, 1, 1)
            e = expert_of(pe, 0)
            up(pe, 0, 0, e)
            turn_hidden(pe, 0)
            with pe.Fori(0, pairs) as it:
                for s in range(2):
                    i = it * 2 + (1 + s)
                    e = expert_of(pe, i)
                    before = expert_of(pe, i - 1)
                    turn(pe, s, i + 1, it + 2)
                    up(pe, (1 + s) % 2, i, e)
                    down(pe, i - 1, before)
                    turn_hidden(pe, i)
            e = expert_of(pe, NB - 2)
            down(pe, NB - 2, e)

        def rows_copy(act, s, i):
            act.wait_ge(turned, i + 1)
            act.wait_ge(h_done, 2 * i + 1)
            nc.scalar.copy(rows_t[s][:, :], ps_x[:, 0:C]).then_inc(xt_ready, 1)

        def out_copy(act, s, i, n):
            act.wait_ge(y_done, i + 1)
            act.wait_ge(tags_read, i + 1)
            if n is not None:
                act.wait_ge(out_sent[s], n * 16)
            nc.scalar.activation(out[s][:, :], ps_y[:, 0:C], ACT.Copy, scale=row_weight[s][:, 0:1]).then_inc(y_copied, 1)

        def take_first(act, i):
            act.wait_ge(h_done, 2 * i + 4)
            nc.scalar.copy(hidden[:, 0:512], ps_h[0][:, :]).then_inc(taken_a, 1)

        def relu_first(act, i, e):
            act.wait_ge(ht_done, 2 * i + 1)
            for m in range(4):
                last = nc.scalar.activation(hidden_t[:, m, :], ps_ht[0][:, m * P:(m + 1) * P], ACT.Relu,
                                            bias=k.b1_cols[:, bass.ds(e * 8 + m, 1)])
            last.then_inc(ht_a, 1)

        @block.scalar
        def _(act):
            act.sem_inc(xt_ready, 1)
            act.sem_inc(taken_a, 1)
            act.sem_inc(taken_d, 1)
            act.sem_inc(ht_a, 1)
            act.sem_inc(ht_d, 1)
            act.sem_inc(y_copied, 1)
            act.sem_inc(h_done, 3)
            rows_copy(act, 0, 0)
            rows_copy(act, 1, 1)
            take_first(act, 0)
            relu_first(act, 0, expert_of(act, 0))

            def turn_of_two(it, n):
                for s in range(2):
                    i = it * 2 + (1 + s)
                    e = expert_of(act, i)
                    rows_copy(act, s, i + 1)
                    take_first(act, i)
                    out_copy(act, s, i - 1, n)
                    relu_first(act, i, e)

            turn_of_two(0, None)
            with act.Fori(1, pairs) as it:
                turn_of_two(it, it)
            out_copy(act, 0, NB - 2, pairs)

        @block.vector
        def _(dve):
            nc.vector.memset(ones[:, :], 1.0).then_inc(set_up, 1)

            def read_tags(i, s, n):
                tag = rows[s][:, C:LW]
                step = 3 * i
                if n is not None:
                    dve.wait_ge(out_sent[s], n * 16)
                nc.vector.tensor_scalar(row_weight[s][:, :], tag[:, 1:2], k.list_row[:, bass.ds(i, 1)], tag[:, 3:4],
                                        ALU.is_equal, ALU.mult).then_inc(tag_step, 1)
                nc.vector.tensor_scalar(node_f[:, 0:1], tag[:, 0:1], 0.0, k.no_node[:, 0:1], ALU.is_equal, ALU.mult).then_inc(tag_step, 1)
                dve.wait_ge(tag_step, step + 1)
                nc.vector.tensor_tensor(row_weight[s][:, :], row_weight[s][:, :], tag[:, 2:3], ALU.add)
                dve.wait_ge(tag_step, step + 2)
                nc.vector.tensor_tensor(node_f[:, 1:2], node_f[:, 0:1], tag[:, 0:1], ALU.add).then_inc(tag_step, 1)
                dve.wait_ge(tag_step, step + 3)
                nc.vector.tensor_copy(node_row[s][:, :], node_f[:, 1:2]).then_inc(tags_read, 1)

            def take_second(i):
                dve.wait_ge(h_done, 2 * i + 5)
                nc.vector.tensor_copy(hidden[:, 512:HID], ps_h[1][:, :]).then_inc(taken_d, 1)

            def relu_second(i, e):
                dve.wait_ge(ht_done, 2 * i + 2)
                for m in range(4, 8):
                    last = nc.vector.tensor_scalar(hidden_t[:, m, :], ps_ht[1][:, (m - 4) * P:(m - 3) * P],
                                                   k.b1_cols[:, bass.ds(e * 8 + m, 1)], 0.0, ALU.add, ALU.max)
                last.then_inc(ht_d, 1)

            def turn_of_two(it, uses):
                for s in range(2):
                    i = it * 2 + (1 + s)
                    e = expert_of(dve, i)
                    take_second(i)
                    read_tags(i, 1 - s, uses[s])
                    relu_second(i, e)

            take_second(0)
            read_tags(0, 0, None)
            relu_second(0, expert_of(dve, 0))
            turn_of_two(0, (None, 1))
            with dve.Fori(1, pairs) as it:
                turn_of_two(it, (it, it + 1))


def program(nc, k):
    with ExitStack() as ctx:
        sb, ps, sem = allocators(nc, ctx)
        dram = lambda name, shape, dt=F32: nc.dram_tensor(name, shape, dt, kind="Internal").ap()
        k.dst_rows = dram("dst_rows", [EROWS, P], I32)
        k.src_rows = dram("src_rows", [EROWS, P], I32)
        k.ea_rows = dram("ea_rows", [EROWS, 3 * P])
        k.nt_list = dram("nt_list", [VPAD], I32)
        k.local_rows = dram("local_rows", [VPAD, P], BF16)
        k.key_rows = dram("key_rows", [VPAD, P])
        k.ea_parts = dram("ea_part_rows", [9, VPAD, P], BF16)
        k.ew_rows = dram("ew_rows", [3, 3, ROW], BF16)
        k.eb_rows = dram("eb_rows", [3, ROW], BF16)
        k.h_rows = dram("h_rows", [NPAD, ROW])
        k.hd_parts = dram("hd_part_rows", [NPAD, 3 * ROW], BF16)
        k.chunk_stats = dram("chunk_stats", [P, 4])
        k.src_logits = dram("src_logits", [NPAD, H])
        k.base_rows = dram("base_rows", [NPAD, C])
        k.node_out = dram("node_out", [NPAD + P + 1, C])
        k.bias_rows = dram("bias_rows", [3, B2_ROWS * P], BF16)
        k.list_rows = dram("list_rows", [NB * P, LW])

        k.ident = sb("ident", [P, P])
        k.eps = sb("eps", [P, 1])
        k.iota_row = sb("iota_row", [P, P])
        k.iota_col = sb("iota_col", [P, 1])
        k.enc_w = sb("enc_w", [30, ROW], BF16)
        k.nt_words = sb("nt_words", [1, VPAD // 4], I32)
        k.places = sb("places", [P, 2, NT], U32)
        k.tags = sb("tags", [P, NT, 4])
        k.list_row = sb("list_row", [P, NB])
        k.no_node = sb("no_node", [P, 1])
        k.expert_row = sb("expert_row", [1, NB], I32)
        k.rstd_out = sb("rstd_out", [P, NT])
        k.shift_out = sb("shift_out", [P, NT])
        constants(nc, k)
        with ExitStack() as edges:
            k.local_col = edges.enter_context(nc.sbuf_tensor("local_col", [P, VPAD], F32))
            k.src_col = edges.enter_context(nc.sbuf_tensor("src_col", [P, VPAD], U32))
            k.src_all = edges.enter_context(nc.sbuf_tensor("src_all", [P, V, H], F32))
            with ExitStack() as nodes:
                k.x_res = nodes.enter_context(nc.sbuf_tensor("x_res", [P, NT, C], F32))
                edge_tables(nc, k)
                k.rstd = nodes.enter_context(nc.sbuf_tensor("rstd", [P, NT], F32))
                k.shift = nodes.enter_context(nc.sbuf_tensor("shift", [P, NT], F32))
                k.norm = nodes.enter_context(nc.sbuf_tensor("norm", [P, NT], F32))
                k.qkv = nodes.enter_context(nc.sbuf_tensor("qkv", [P, NT, QW + 1], F32))
                node_rows(nc, k)
                linear_attention(nc, k)
            k.alpha = edges.enter_context(nc.sbuf_tensor("alpha", [P, V, H], F32))
            edge_logits(nc, k)
            segment_softmax(nc, k)
            k.acc = edges.enter_context(nc.sbuf_tensor("acc", [P, NT, ROW], F32))
            aggregate(nc, k)
            gate(nc, k)
        k.w1_t = sb("w1_t", [P, NE * 4, 512])
        k.w2_t = sb("w2_t", [P, NE * 4, 512])
        k.b1_cols = sb("b1_cols", [P, B1_ROWS])
        k.biases = sb("biases", [3, B2_ROWS * P], BF16)
        dispatch_and_weights(nc, k)
        experts(nc, k)


_NAMES = {"x": "x", "src": "src", "dst": "dst", "edge_attr_3": "edge_attr", "L0_gnn_W": "W", "L0_gnn_a_src": "a_src",
          "L0_gnn_a_dst": "a_dst", "L0_gnn_edge_W": "edge_W", "L0_gnn_edge_b": "edge_b", "L0_gnn_bias": "bias",
          "L0_mix_w_qkv": "w_qkv", "L0_mix_mem_kv": "mem_kv", "L0_mix_w_out": "w_out", "L0_mix_b_out": "b_out",
          "L0_mix_g_out": "g_out", "L0_mix_g_pre": "g_pre", "L0_ffn_Wg": "Wg", "L0_ffn_bg": "bg", "L0_ffn_W1": "W1",
          "L0_ffn_b1": "b1", "L0_ffn_W2": "W2", "L0_ffn_b2": "b2"}


def kernel(**inputs):
    import numpy as np
    import concourse.bacc as bacc
    from concourse.bass_utils import run_bass_kernel_spmd as run

    nc = bacc.Bacc("TRN2", target_bir_lowering=False, num_devices=1)
    arrays, k = {}, Ctx()
    for name, short in _NAMES.items():
        a = np.ascontiguousarray(inputs[name])
        arrays["in_" + short] = a
        k.__dict__[short] = nc.dram_tensor("in_" + short, a.shape, mybir.dt.from_np(a.dtype), kind="ExternalInput").ap()
    k.out = nc.dram_tensor("out", (N, C), F32, kind="ExternalOutput").ap()
    program(nc, k)
    r = run(nc, [arrays], core_ids=[0])
    return r.results[0]["out"]
```
